# Optimizing a Trainium2 kernel written in Bass

```python
import numpy as np
import jax
import jax.numpy as jnp

def _softmax(x, axis=-1):
    return jax.nn.softmax(x, axis=axis)

def _gelu(x):
    return jax.nn.gelu(x, approximate=True)

def _silu(x):
    return jax.nn.silu(x)

def _sigmoid(x):
    return jax.nn.sigmoid(x)

def _layernorm(x, axis=-1, eps=1e-05):
    m = jnp.mean(x, axis=axis, keepdims=True)
    v = jnp.var(x, axis=axis, keepdims=True)
    return (x - m) / jnp.sqrt(v + eps)

def _scatter_add(tgt, idx, src, axis=0):
    return tgt.at[idx].add(src)

def _segment_sum(src, seg, n):
    return jax.ops.segment_sum(src, seg, n)
kernel_name = 'mk_flamingo_gated_d1_seqx_r2_db0393'

def setup_inputs(seed: int=0):
    np.random.seed(seed)
    _w = jnp.asarray

    def _rec_inputs():
        import jax
        import jax.numpy as jnp
        _rk = jax.random.key(seed)
        x = -0.0002928 + 1 * jax.random.normal(jax.random.fold_in(_rk, 1), (16, 256, 512), jnp.float32)
        _lenS = 256 - jax.random.randint(jax.random.fold_in(_rk, 7), (16,), 0, max(1, 256 // 4) + 1, jnp.int32)
        _lenS2 = 256 - jax.random.randint(jax.random.fold_in(_rk, 8), (16,), 0, max(1, 256 // 4) + 1, jnp.int32)
        _ctx_1024P = jax.random.normal(jax.random.fold_in(_rk, 11), (16, 16, 512), jnp.float32)
        _ctx_1024c = jax.random.dirichlet(jax.random.fold_in(_rk, 511), 0.3 * jnp.ones((16,), jnp.float32), (16, 256))
        _ctx_1024t = jnp.einsum('bsk,bkd->bsd', _ctx_1024c, _ctx_1024P)
        _ctx_1024t = _ctx_1024t * jax.lax.rsqrt(jnp.mean(jnp.square(_ctx_1024t)) + 1e-12) * 0.953939
        ctx_1024 = -1.39393e-06 + 0.999914 * (_ctx_1024t + 0.3 * jax.random.normal(jax.random.fold_in(_rk, 611), (16, 256, 512), jnp.float32))
        _g = jax.random.normal(jax.random.fold_in(_rk, 9001), (2, 1), jnp.float32)
        _g = jnp.sign(_g) * jnp.maximum(jnp.abs(_g), 1.0) + (_g == 0) * 1.0
        g_xattn = _g[0]
        g_ffn = _g[1]
        return (x, ctx_1024, g_xattn, g_ffn)
    x, ctx_1024, g_xattn, g_ffn = _rec_inputs()

    def _L0_xattn_setup():
        import jax, jax.numpy as jnp
        import numpy as np
        B, S, D, NH = (2, 1024, 512, 8)
        DH = D // NH
        EPS = 1e-06
        LN_EPS = 1e-05

        def _mlstm_cell(q, k, v, igate_w, igate_b, fgate_w, fgate_b, ln_scale):
            Slen = q.shape[0]
            ifg = jnp.concatenate([q, k, v], axis=-1)
            ig = (ifg @ igate_w.T + igate_b).T
            fg = (ifg @ fgate_w.T + fgate_b).T
            qh = q.reshape(Slen, NH, DH).transpose(1, 0, 2)
            kh = k.reshape(Slen, NH, DH).transpose(1, 0, 2)
            vh = v.reshape(Slen, NH, DH).transpose(1, 0, 2)
            log_f = jax.nn.log_sigmoid(fg)
            cs = jnp.cumsum(log_f, axis=1)
            fg_mat = cs[:, :, None] - cs[:, None, :]
            mask = jnp.tril(jnp.ones((Slen, Slen), dtype=bool))
            log_fg_mat = jnp.where(mask, fg_mat, -jnp.inf)
            log_D = log_fg_mat + ig[:, None, :]
            max_log_D = jnp.max(log_D, axis=-1, keepdims=True)
            D_mat = jnp.exp(log_D - max_log_D)
            qk = jnp.einsum('hsd,htd->hst', qh, kh) / np.sqrt(DH)
            C = qk * D_mat
            normalizer = jnp.maximum(jnp.abs(C.sum(axis=-1, keepdims=True)), jnp.exp(-max_log_D))
            h = jnp.einsum('hst,htd->hsd', C / (normalizer + EPS), vh)
            h = h.transpose(1, 0, 2).reshape(Slen, D)
            mu = h.mean(axis=-1, keepdims=True)
            var = h.var(axis=-1, keepdims=True)
            return (h - mu) / jnp.sqrt(var + LN_EPS) * ln_scale
        key = jax.random.key(seed)
        ks = jax.random.split(key, 8)
        rnd = lambda k, sh, s=1.0: jax.random.normal(k, sh, dtype=jnp.float32) * s
        return {'q': rnd(ks[0], (B, S, D)), 'k': rnd(ks[1], (B, S, D)), 'v': rnd(ks[2], (B, S, D)), 'igate_w': rnd(ks[3], (NH, 3 * D), 0.02), 'igate_b': jnp.linspace(3.0, 6.0, NH, dtype=jnp.float32), 'fgate_w': rnd(ks[4], (NH, 3 * D), 0.02), 'fgate_b': rnd(ks[5], (NH,), 0.3162278), 'ln_scale': jnp.ones((D,), dtype=jnp.float32)}
    _L0_xattn_all = _L0_xattn_setup()
    _L0_xattn_in = {k: v for k, v in _L0_xattn_all.items() if k in ('igate_w', 'igate_b', 'fgate_w', 'fgate_b', 'ln_scale')}
    del _L0_xattn_all

    def _L0_ffn_setup():
        import jax, jax.numpy as jnp
        import numpy as np
        H = 512
        I = 256
        E = 16
        K = 2
        N_SHARED = 2
        IS = I * N_SHARED
        B, S = (2, 1024)
        key = jax.random.key(seed)
        ks = jax.random.split(key, 9)
        sc = 0.02
        return {'hidden_states': jax.random.normal(ks[0], (B, S, H), jnp.float32), 'router_w': jax.random.normal(ks[1], (E, H), jnp.float32) * sc, 'expert_gate': jax.random.normal(ks[2], (E, H, I), jnp.float32) * sc, 'expert_up': jax.random.normal(ks[3], (E, H, I), jnp.float32) * sc, 'expert_down': jax.random.normal(ks[4], (E, I, H), jnp.float32) * sc, 'shared_gate': jax.random.normal(ks[5], (H, IS), jnp.float32) * sc, 'shared_up': jax.random.normal(ks[6], (H, IS), jnp.float32) * sc, 'shared_down': jax.random.normal(ks[7], (IS, H), jnp.float32) * sc}
    _L0_ffn_all = _L0_ffn_setup()
    _L0_ffn_in = {k: v for k, v in _L0_ffn_all.items() if k in ('router_w', 'expert_gate', 'expert_up', 'expert_down', 'shared_gate', 'shared_up', 'shared_down')}
    del _L0_ffn_all
    return {'x': x, 'ctx_1024': ctx_1024, 'g_xattn': g_xattn, 'g_ffn': g_ffn, 'L0_xattn_igate_w': _L0_xattn_in['igate_w'], 'L0_xattn_igate_b': _L0_xattn_in['igate_b'], 'L0_xattn_fgate_w': _L0_xattn_in['fgate_w'], 'L0_xattn_fgate_b': _L0_xattn_in['fgate_b'], 'L0_xattn_ln_scale': _L0_xattn_in['ln_scale'], 'L0_ffn_router_w': _L0_ffn_in['router_w'], 'L0_ffn_expert_gate': _L0_ffn_in['expert_gate'], 'L0_ffn_expert_up': _L0_ffn_in['expert_up'], 'L0_ffn_expert_down': _L0_ffn_in['expert_down'], 'L0_ffn_shared_gate': _L0_ffn_in['shared_gate'], 'L0_ffn_shared_up': _L0_ffn_in['shared_up'], 'L0_ffn_shared_down': _L0_ffn_in['shared_down']}

def reference(x, ctx_1024, g_xattn, g_ffn, L0_xattn_igate_w, L0_xattn_igate_b, L0_xattn_fgate_w, L0_xattn_fgate_b, L0_xattn_ln_scale, L0_ffn_router_w, L0_ffn_expert_gate, L0_ffn_expert_up, L0_ffn_expert_down, L0_ffn_shared_gate, L0_ffn_shared_up, L0_ffn_shared_down):
    import jax
    import jax.numpy as jnp

    def _L0_xattn_ref(q, k, v, igate_w, igate_b, fgate_w, fgate_b, ln_scale):
        import jax, jax.numpy as jnp
        import numpy as np
        B, S, D, NH = (2, 1024, 512, 8)
        DH = D // NH
        EPS = 1e-06
        LN_EPS = 1e-05

        def _mlstm_cell(q, k, v, igate_w, igate_b, fgate_w, fgate_b, ln_scale):
            Slen = q.shape[0]
            ifg = jnp.concatenate([q, k, v], axis=-1)
            ig = (ifg @ igate_w.T + igate_b).T
            fg = (ifg @ fgate_w.T + fgate_b).T
            qh = q.reshape(Slen, NH, DH).transpose(1, 0, 2)
            kh = k.reshape(Slen, NH, DH).transpose(1, 0, 2)
            vh = v.reshape(Slen, NH, DH).transpose(1, 0, 2)
            log_f = jax.nn.log_sigmoid(fg)
            cs = jnp.cumsum(log_f, axis=1)
            fg_mat = cs[:, :, None] - cs[:, None, :]
            mask = jnp.tril(jnp.ones((Slen, Slen), dtype=bool))
            log_fg_mat = jnp.where(mask, fg_mat, -jnp.inf)
            log_D = log_fg_mat + ig[:, None, :]
            max_log_D = jnp.max(log_D, axis=-1, keepdims=True)
            D_mat = jnp.exp(log_D - max_log_D)
            qk = jnp.einsum('hsd,htd->hst', qh, kh) / np.sqrt(DH)
            C = qk * D_mat
            normalizer = jnp.maximum(jnp.abs(C.sum(axis=-1, keepdims=True)), jnp.exp(-max_log_D))
            h = jnp.einsum('hst,htd->hsd', C / (normalizer + EPS), vh)
            h = h.transpose(1, 0, 2).reshape(Slen, D)
            mu = h.mean(axis=-1, keepdims=True)
            var = h.var(axis=-1, keepdims=True)
            return (h - mu) / jnp.sqrt(var + LN_EPS) * ln_scale
        return jax.vmap(lambda qq, kk, vv: _mlstm_cell(qq, kk, vv, igate_w, igate_b, fgate_w, fgate_b, ln_scale))(q, k, v)

    def _L0_ffn_ref(hidden_states, router_w, expert_gate, expert_up, expert_down, shared_gate, shared_up, shared_down):
        import jax, jax.numpy as jnp
        import numpy as np
        H = 512
        I = 256
        E = 16
        K = 2
        N_SHARED = 2
        IS = I * N_SHARED
        B, S = (2, 1024)
        orig_shape = hidden_states.shape
        x = hidden_states.reshape(-1, H)
        T = x.shape[0]
        scores = jax.nn.softmax(x @ router_w.T, axis=-1)
        topk_w, topk_idx = jax.lax.top_k(scores, K)
        topk_w = topk_w / jnp.sum(topk_w, axis=-1, keepdims=True)
        gates = jnp.zeros((T, E), x.dtype).at[jnp.arange(T)[:, None], topk_idx].add(topk_w)
        g = jnp.einsum('th,ehi->tei', x, expert_gate)
        u = jnp.einsum('th,ehi->tei', x, expert_up)
        a = jax.nn.silu(g) * u
        y = jnp.einsum('tei,eih,te->th', a, expert_down, gates)
        s = jax.nn.silu(x @ shared_gate) * (x @ shared_up) @ shared_down
        return (y + s).reshape(orig_shape)
    x = x + jnp.tanh(g_xattn[0]) * _L0_xattn_ref(_layernorm(x, axis=-1), ctx_1024, ctx_1024, L0_xattn_igate_w, L0_xattn_igate_b, L0_xattn_fgate_w, L0_xattn_fgate_b, L0_xattn_ln_scale)
    x = x + jnp.tanh(g_ffn[0]) * _L0_ffn_ref(_layernorm(x, axis=-1), L0_ffn_router_w, L0_ffn_expert_gate, L0_ffn_expert_up, L0_ffn_expert_down, L0_ffn_shared_gate, L0_ffn_shared_up, L0_ffn_shared_down)
    return x

_drawn_inputs = setup_inputs


def setup_inputs(seed=0):
    import zlib

    import numpy as np

    out = dict(_drawn_inputs(seed))
    spreads = {'L0_xattn_ln_scale': (1.0, 0.2)}
    factors = {'L0_ffn_router_w': 3.532,
     'L0_ffn_expert_gate': 3.369,
     'L0_ffn_expert_up': 3.306,
     'L0_ffn_expert_down': 3.306}
    for name, (base, spread) in spreads.items():
        noise = np.random.default_rng([zlib.crc32(name.encode()), seed]).standard_normal(out[name].shape)
        drawn = base * np.exp(spread * noise) if base else spread * noise
        out[name] = jnp.asarray(drawn.astype(out[name].dtype))
    for name, factor in factors.items():
        out[name] = (out[name] * factor).astype(out[name].dtype)
    return out
```

```python
from contextlib import ExitStack

import concourse.bass as bass
from concourse import mybir

F32 = mybir.dt.float32
BF16 = mybir.dt.bfloat16
I32 = mybir.dt.int32
U32 = mybir.dt.uint32
ALU = mybir.AluOpType
ACT = mybir.ActivationFunctionType
AX_X = mybir.AxisListType.X

P = 128
B, S, D = 16, 256, 512
NH, DH = 8, 64
E, I = 16, 256
IS = 512
TOPK = 2
T = B * S
ST = S // P
NT = T // P
DC = D // P
IC = I // P
SC = IS // P
LN_EPS = 1e-5
NORM_EPS = 1e-6
QK_SCALE = DH ** -0.5
MASK = 1e30
CAP = T + P
DUMP = E * CAP
TILES = (T * TOPK + E * (P - 1)) // P
TILES += TILES % 2
RING = 4
XRING = 4
TRI = S + P
VW = DH + 1


class Event:

    def __init__(self, sem, per=1, start=0):
        self.sem, self.per, self.start = sem, per, start

    def upto(self, n, k=None):
        value = n * self.per + (self.per if k is None else k)
        if isinstance(value, int) and value <= 0:
            return 0
        return value + self.start


class Item:

    def __init__(self, i, offset):
        self.i, self.offset = i, offset
        self.n = i * 2 + offset
        self.half = i + offset // 2
        self.par = offset % 2

    def __add__(self, k):
        return Item(self.i, self.offset + k)


def flamingo_kernel(nc, x, ctx_in, g_xattn, g_ffn, igate_w, igate_b, fgate_w, fgate_b, ln_scale,
                    router_w, expert_gate, expert_up, expert_down, shared_gate, shared_up,
                    shared_down, out):
    x_tok = x.rearrange("b (j p) d -> b p j d", p=P)
    c_tok = ctx_in.rearrange("b (j p) d -> b p j d", p=P)
    out_tok = out.rearrange("b s d -> (b s) d")
    routed_x = nc.dram_tensor("routed_x", (DUMP + P, D), F32).ap()
    routed_y = nc.dram_tensor("routed_y", (TILES * P, D), F32).ap()

    with ExitStack() as stack:
        def sb(name, shape, dt=F32):
            return stack.enter_context(nc.sbuf_tensor(name, shape, dt))

        def event(name, per=1, start=0):
            return Event(stack.enter_context(nc.semaphore(name)), per, start)

        bank = [stack.enter_context(nc.psum_tensor(f"bank{n}", [P, 512], F32)) for n in range(8)]
        TP, SM, MB, QK, HO, FF = bank[0], bank[1], bank[2:4], bank[4:6], bank[6], bank[7]

        ident = sb("ident", [P, P])
        identb = sb("identb", [P, P], BF16)
        upto_f = sb("upto_f", [P, P])
        ones_f = sb("ones_f", [P, P])
        before_b = sb("before_b", [P, P], BF16)
        ones_b = sb("ones_b", [P, P], BF16)
        mask_b = sb("mask_b", [P, P], BF16)
        head_sel = sb("head_sel", [P, NH, P], BF16)
        expert_no = sb("expert_no", [P, E])
        expert_row = sb("expert_row", [P, E])
        part_no = sb("part_no", [P, 1])
        minus_half = sb("minus_half", [P, ST])
        gate_wT = sb("gate_wT", [P, 2 * DC, 2 * NH])
        router_wT = sb("router_wT", [P, DC, E])
        gate_bias = sb("gate_bias", [P, 2 * NH])
        ln_row = sb("ln_row", [P, D])
        g_col = sb("g_col", [P, 2])
        tanh_g = sb("tanh_g", [P, 2])
        EW = DC * 2 * I + IC * D
        w_ring = sb("w_ring", [P, RING, EW])
        w_gu = w_ring[:, :, 0:DC * 2 * I].rearrange("p r (c i) -> p r c i", c=DC)
        w_dn = w_ring[:, :, DC * 2 * I:EW].rearrange("p r (c d) -> p r c d", c=IC)
        sh_w = w_ring[:, 2:4, :].rearrange("p r n -> p (r n)").rearrange("p (w c i) -> p w c i", w=3, c=DC)
        sh_gate, sh_up, sh_down = (sh_w[:, k] for k in range(3))
        last_w = w_ring[:, 0:2, :].rearrange("p r n -> p (r n)")

        xs = sb("xs", [P, 2, ST, D])
        cs_in = sb("cs_in", [P, 2, ST, D])
        v_aug = sb("v_aug", [P, 2, ST, NH, VW])
        xn = sb("xn", [P, ST, D])
        xnT = sb("xnT", [P, 2, DC, S])
        ctxT = sb("ctxT", [P, 2, DC, S])
        ln_stat = sb("ln_stat", [P, ST, 6])
        ln_mv = sb("ln_mv", [P, ST, 2])
        ln_var = sb("ln_var", [P, ST])
        ln_rstd = sb("ln_rstd", [P, ST])
        gates = sb("gates", [P, ST, 2 * NH])
        f_abs = sb("f_abs", [P, ST, NH])
        f_exp = sb("f_exp", [P, ST, NH])
        f_ln = sb("f_ln", [P, ST, NH])
        log_f = sb("log_f", [P, ST, NH])
        cum_f = sb("cum_f", [P, ST, NH])
        key_log = sb("key_log", [P, 2, ST, NH])
        key_row = sb("key_row", [NH, S])
        max_row = sb("max_row", [NH, S])
        max_mid = sb("max_mid", [NH, S], BF16)
        max_rest = sb("max_rest", [NH, S])
        max_parts = sb("max_parts", [P, 2, S], BF16)
        max_log = sb("max_log", [P, ST, NH])
        norm_floor = sb("norm_floor", [P, 2, ST, NH])
        decay = sb("decay", [P, 2, TRI])
        cmat = sb("cmat", [P, 2, TRI])
        norm = sb("norm", [P, 2, ST])
        norm_abs = sb("norm_abs", [P, 2, ST])
        norm_e = sb("norm_e", [P, 2, ST])
        norm_inv = sb("norm_inv", [P, 2, ST])
        heads = sb("heads", [P, ST, D])
        h_stat = sb("h_stat", [P, ST, 6])
        h_mv = sb("h_mv", [P, ST, 2])
        h_var = sb("h_var", [P, ST])
        h_rstd = sb("h_rstd", [P, ST])
        x2_stat = sb("x2_stat", [P, ST, 6])
        x2_mv = sb("x2_mv", [P, ST, 2])
        x2_var = sb("x2_var", [P, ST])
        x2_rstd = sb("x2_rstd", [P, ST])
        x2n = sb("x2n", [P, 2, ST, D])
        rows = x2n[0:E].rearrange("p a j d -> p (a j) d")
        gate_rows, router_rows = rows[:, 0:3, :].rearrange("p a d -> p (a d)"), rows[:, 3, :]
        x2nT = sb("x2nT", [P, DC, S])
        logits = sb("logits", [P, ST, E])
        top8 = sb("top8", [P, ST, 8])
        top8_at = sb("top8_at", [P, ST, 8], U32)
        top_at = sb("top_at", [P, ST, TOPK])
        one_hot = sb("one_hot", [P, ST, TOPK, E])
        gap = sb("gap", [P, ST])
        gap_exp = sb("gap_exp", [P, ST])
        gap_den = sb("gap_den", [P, ST])
        gap_inv = sb("gap_inv", [P, ST])
        top_w = sb("top_w", [P, ST, TOPK])
        chosen = sb("chosen", [P, ST, E], BF16)
        taken = sb("taken", [P, 2, E], BF16)
        taken_mid = sb("taken_mid", [P, E], BF16)
        place = sb("place", [P, ST, E])
        place_pick = sb("place_pick", [P, ST * TOPK, E])
        slot_f = sb("slot_f", [P, ST * TOPK])
        slot_u = sb("slot_u", [P, 2, ST * TOPK], U32)
        silu_t = sb("silu_t", [P, S])
        silu_g = sb("silu_g", [P, S])
        sh_actT = sb("sh_actT", [P, SC, S])
        base_out = sb("base_out", [P, NT, D])
        all_hot = sb("all_hot", [P, B, ST * TOPK, E], BF16)
        all_slot = sb("all_slot", [P, B, ST * TOPK])
        all_w = sb("all_w", [P, B, ST * TOPK])

        count = sb("count", [P, E])
        count_i = sb("count_i", [P, E], I32)
        tiles_i = sb("tiles_i", [P, E], I32)
        tiles_f = sb("tiles_f", [P, E])
        tile_end = sb("tile_end", [P, E])
        tile_first = sb("tile_first", [P, E])
        ended = sb("ended", [P, E])
        ended_at = sb("ended_at", [P, E])
        tile_info = sb("tile_info", [P, 4])
        pad_f = sb("pad_f", [P, E])
        pad_u = sb("pad_u", [P, E], U32)
        shift = sb("shift", [P, E])
        y_slot_f = sb("y_slot_f", [P, B * ST * TOPK])
        y_slot = sb("y_slot", [P, B * ST * TOPK], U32)
        first_tab = sb("first_tab", [1, E], I32)
        row_tab = sb("row_tab", [1, P], I32)
        expert_tab = sb("expert_tab", [1, P], I32)
        xt = xs[:, :, :, :].rearrange("p a j d -> p (a j) d")
        xtT = xnT[:, :, 0:2, :].rearrange("p a c s -> p a (c s)")
        act_t, act_g, act_a, act_aT = (ctxT[:, :, k, :] for k in range(4))
        y_out = cs_in[:, 0]
        hot_shift = cs_in[:, 1].rearrange("p j (n e) -> p (j n) e", e=E)
        zeros = xn[:, 0, :]

        y_at = sb("y_at", [P, 4, TOPK], U32)
        y_in = last_w[:, 0:4 * TOPK * D].rearrange("p (n k d) -> p n k d", n=4, k=TOPK)
        fin = last_w[:, 4 * TOPK * D:4 * (TOPK + 1) * D].rearrange("p (n d) -> p n d", n=4)

        small_in = event("small_in", 16)
        weights_in = event("weights_in", 16)
        pool_const = event("pool_const")
        stood = event("stood")
        act_const = event("act_const")
        wT_made = event("wT_made")
        wT_copied = event("wT_copied")
        x_in = [event(f"x_in{k}", 16) for k in range(2)]
        c_in = [event(f"c_in{k}", 16) for k in range(2)]
        v_made = event("v_made")
        ln_step = event("ln_step", 2 * ST)
        ln_var_made = event("ln_var_made")
        ln_rstd_made = event("ln_rstd_made")
        h_var_made = event("h_var_made")
        h_rstd_made = event("h_rstd_made")
        x2_var_made = event("x2_var_made")
        x2_rstd_made = event("x2_rstd_made")
        xn_made = event("xn_made", ST)
        ctx_turned = event("ctx_turned", ST)
        ctxT_made = event("ctxT_made", ST)
        xn_turned = event("xn_turned", ST)
        xnT_made = event("xnT_made", ST)
        gates_made = event("gates_made")
        gates_read = event("gates_read", 2)
        f_exp_made = event("f_exp_made")
        f_ln_made = event("f_ln_made")
        log_f_made = event("log_f_made")
        cum_made = event("cum_made")
        key_made = event("key_made", 2)
        key_turned = event("key_turned")
        max_step = event("max_step", 7)
        max_turned = event("max_turned")
        max_log_made = event("max_log_made")
        floor_made = event("floor_made")
        qk_made = event("qk_made", NH)
        max_spread = event("max_spread", NH)
        decay_made = event("decay_made", NH)
        c_made = event("c_made", NH)
        pv_made = event("pv_made", NH)
        norm_step = event("norm_step", 4 * NH // 2)
        heads_made = event("heads_made", NH // 2)
        post_step = event("post_step", 5 * ST)
        x2_made = event("x2_made", ST)
        x2n_made = event("x2n_made", ST)
        x2_turned = event("x2_turned", ST)
        x2nT_made = event("x2nT_made", ST)
        router_made = event("router_made")
        logits_made = event("logits_made")
        top_step = event("top_step", 2 * ST + 1)
        gap_made = event("gap_made")
        gap_exp_made = event("gap_exp_made")
        hot_made = event("hot_made", 2 * ST)
        w_step = event("w_step", 3)
        route_kept = event("route_kept", 3)
        chosen_made = event("chosen_made", 3)
        ranks_made = event("ranks_made")
        place_step = event("place_step", 3)
        slots_made = event("slots_made")
        scattered = [event(f"scattered{k}", 16 * ST * TOPK) for k in range(2)]
        sh_made = event("sh_made", SC)
        sh_tanh_made = event("sh_tanh_made", SC)
        sh_silu_made = event("sh_silu_made", SC)
        sh_act_made = event("sh_act_made", SC)
        sh_down_made = event("sh_down_made", ST)
        base_made = event("base_made", ST)

        counts_made = event("counts_made")
        table_step = event("table_step")
        tables_turned = event("tables_turned")
        tables_made = event("tables_made")
        pads_made = event("pads_made")
        padded = event("padded", 16)
        y_slots_made = event("y_slots_made")
        expert_dma = event("expert_dma", 48)
        expert_in = event("expert_in")
        xt_in = [event(f"xt_in{k}", 16) for k in range(XRING)]
        xt_turned = event("xt_turned")
        xtT_made = event("xtT_made")
        gu_made = event("gu_made")
        act_tanh_made = event("act_tanh_made")
        act_silu_made = event("act_silu_made")
        act_made = event("act_made")
        act_turned = event("act_turned")
        actT_made = event("actT_made")
        y_made = event("y_made", start=1)
        y_copied = event("y_copied")
        y_stored = [event(f"y_stored{k}", 16) for k in range(2)]

        y_at_made = event("y_at_made")
        y_got = [event(f"y_got{k}", 16 * TOPK) for k in range(4)]
        fin_step = event("fin_step")
        fin_made = event("fin_made")
        out_stored = [event(f"out_stored{k}", 16) for k in range(4)]

        N_SMALL = 8
        N_SHARED = 3


        def apart(eng):
            eng.sem_inc(stood.sem, 1)

        block = stack.enter_context(nc.Block())

        @block.sync
        def _(sp):
            def load_batch(b):
                sp.dma_start(xs[:, b.par, :, :], x_tok[bass.ds(b.n, 1)].rearrange("a p j d -> (a p) j d")
                             ).then_inc(x_in[b.par].sem, 16)
                sp.dma_start(cs_in[:, b.par, :, :], c_tok[bass.ds(b.n, 1)].rearrange("a p j d -> (a p) j d")
                             ).then_inc(c_in[b.par].sem, 16)

            load_batch(Item(0, 0))
            load_batch(Item(0, 1))
            with sp.Fori(0, (B - 2) // 2) as i:
                for u in range(2):
                    b = Item(i, 2 + u)
                    sp.wait_ge(x2_made.sem, x2_made.upto(b.n - 2))
                    apart(sp)
                    sp.wait_ge(ctxT_made.sem, ctxT_made.upto(b.n - 2))
                    apart(sp)
                    sp.wait_ge(v_made.sem, v_made.upto(b.n - 2))
                    apart(sp)
                    load_batch(b)

            def load_tile(n, k):
                row = sp.value_load(row_tab[0:1, bass.ds(n, 1)], min_val=0, max_val=DUMP)
                sp.dma_start(xt[:, k, :], routed_x[bass.ds(row, P), :]).then_inc(xt_in[k].sem, 16)

            sp.wait_ge(tables_made.sem, tables_made.upto(0))
            for par in range(2):
                sp.wait_ge(scattered[par].sem, scattered[par].upto(B // 2 - 1))
            sp.wait_ge(padded.sem, padded.upto(E))
            for n in range(XRING - 1):
                load_tile(n, n)

            def store_tile(t, par):
                sp.wait_ge(y_copied.sem, y_copied.upto(t))
                apart(sp)
                sp.dma_start(routed_y[bass.ds(t * P, P), :], y_out[:, par, :]).then_inc(y_stored[par].sem, 16)

            def turn(n, k, ahead=True):
                if ahead:
                    sp.wait_ge(xt_turned.sem, xt_turned.upto(n - 1))
                    apart(sp)
                    load_tile(n + XRING - 1, (k + XRING - 1) % XRING)
                store_tile(n, k % 2)

            turn(0, 0)
            turn(1, 1)
            turn(2, 2)
            turn(3, 3)
            with sp.Fori(0, (TILES - 2 * XRING) // XRING) as i:
                for k in range(XRING):
                    turn(i * XRING + XRING + k, k)
            for n in range(TILES - XRING, TILES):
                turn(n, n % XRING, n + XRING - 1 < TILES)

            with sp.Fori(0, NT // 4) as i:
                for k in range(4):
                    n = i * 4 + k
                    sp.wait_ge(fin_made.sem, fin_made.upto(n))
                    sp.dma_start(out_tok[bass.ds(n * P, P), :], fin[:, k, :]).then_inc(out_stored[k].sem, 16)
            for k in range(4):
                sp.wait_ge(out_stored[k].sem, out_stored[k].upto(NT // 4 - 1))

        @block.gpsimd
        def _(pool):
            g = nc.gpsimd
            made = [0]

            def const(ins):
                made[0] += 1
                ins.then_inc(pool_const.sem, 1)

            def settle():
                pool.wait_ge(pool_const.sem, made[0])

            def select(ap, fill, op, base, p_step, pattern):
                settle()
                const(g.affine_select(out=ap, in_=ap, compare_op=op, fill=fill, base=base,
                                      pattern=pattern, channel_multiplier=p_step))

            const(g.memset(ident[:], 0.0))
            const(g.memset(identb[:], 0.0))
            const(g.memset(upto_f[:], 1.0))
            const(g.memset(ones_f[:], 1.0))
            const(g.memset(before_b[:], 1.0))
            const(g.memset(ones_b[:], 1.0))
            const(g.memset(mask_b[:], 0.0))
            const(g.memset(head_sel[:], 0.0))
            const(g.memset(v_aug[:], 1.0))
            const(g.memset(taken[:], 0.0))
            const(g.memset(minus_half[:], -0.5))
            const(g.memset(max_parts[:], 0.0))
            select(ident[:], 1.0, ALU.not_equal, 0, 1, [[-1, P]])
            select(identb[:], 1.0, ALU.not_equal, 0, 1, [[-1, P]])
            select(upto_f[:], 0.0, ALU.is_ge, 0, -1, [[1, P]])
            select(before_b[:], 0.0, ALU.is_gt, 0, -1, [[1, P]])
            select(mask_b[:], MASK, ALU.is_ge, 0, -1, [[1, P]])
            for part in range(3):
                select(head_sel[:], 1.0, ALU.not_equal, -32 * part, 1, [[-1, NH], [0, P]])
            const(g.iota(expert_no[:], pattern=[[1, E]], base=0, channel_multiplier=0,
                         allow_small_or_imprecise_dtypes=True))
            const(g.iota(expert_row[:], pattern=[[CAP, E]], base=0, channel_multiplier=0,
                         allow_small_or_imprecise_dtypes=True))
            const(g.iota(part_no[:], pattern=[[0, 1]], base=0, channel_multiplier=1,
                         allow_small_or_imprecise_dtypes=True))
            assert made[0] == POOL_CONSTS
            settle()

            def load_expert(e, k):
                sides = (
                    (w_gu[:, k, :, 0:I], expert_gate, DC), (w_gu[:, k, :, I:2 * I], expert_up, DC),
                    (w_dn[:, k, :, :], expert_down, IC),
                )
                for to, of, c in sides:
                    src = of[bass.ds(e, 1)].rearrange("a (c p) i -> (a p) c i", p=P)
                    pool.dma_start(to, src).then_inc(expert_dma.sem, 16)

            for e in range(RING - 2):
                load_expert(e, e)

            def values(b):
                pool.wait_ge(c_in[b.par].sem, c_in[b.par].upto(b.half))
                pool.wait_ge(pv_made.sem, pv_made.upto(b.n - 2))
                apart(pool)
                g.tensor_copy(v_aug[:, b.par, :, :, 0:DH],
                              cs_in[:, b.par, :, :].rearrange("p j (h d) -> p j h d", h=NH)
                              ).then_inc(v_made.sem, 1)

            def scatter(b):
                pool.wait_ge(slots_made.sem, slots_made.upto(b.n))
                apart(pool)
                for j in range(ST):
                    for k in range(TOPK):
                        c = j * TOPK + k
                        pool.indirect_dma_start(
                            out=routed_x, in_=x2n[:, b.par, j, :], in_offset=None,
                            out_offset=bass.IndirectOffsetOnAxis(ap=slot_u[:, b.par, c:c + 1], axis=0),
                        ).then_inc(scattered[b.par].sem, 16)

            def rstd(b, made, var, to, told):
                pool.wait_ge(made.sem, made.upto(b.n))
                g.tensor_tensor(to[:, :], var[:, :], minus_half[:, :], ALU.pow).then_inc(told.sem, 1)

            def norm(b):
                rstd(b, ln_var_made, ln_var, ln_rstd, ln_rstd_made)
                values(b)

            def post(b):
                rstd(b, h_var_made, h_var, h_rstd, h_rstd_made)
                rstd(b, x2_var_made, x2_var, x2_rstd, x2_rstd_made)

            def step(t, front=True, attend=True, experts=True):
                F, A, G = t + 1, t, t + -1
                if front:
                    norm(F)
                if experts:
                    scatter(G)
                if attend:
                    post(A)

            step(Item(0, -1), attend=False, experts=False)
            step(Item(0, 0), experts=False)
            step(Item(0, 1))
            with pool.Fori(0, (B - 4) // 2) as i:
                step(Item(i, 2))
                step(Item(i, 3))
            step(Item(0, B - 2))
            step(Item(0, B - 1), front=False)
            step(Item(0, B), front=False, attend=False)

            pool.wait_ge(pads_made.sem, pads_made.upto(0))
            for e in range(E):
                pool.indirect_dma_start(
                    out=routed_x, in_=zeros[:, :], in_offset=None,
                    out_offset=bass.IndirectOffsetOnAxis(ap=pad_u[:, e:e + 1], axis=0),
                ).then_inc(padded.sem, 16)
            pool.dma_start(routed_x[DUMP:DUMP + P, :], zeros[:, :]).then_inc(padded.sem, 16)

            pool.wait_ge(sh_down_made.sem, sh_down_made.upto(B - 1))
            for e in range(RING - 2, RING):
                load_expert(e, e)
            pool.wait_ge(expert_dma.sem, expert_dma.upto(RING - 1))
            pool.sem_inc(expert_in.sem, RING)
            pool.wait_ge(tables_made.sem, tables_made.upto(0))
            with pool.Fori(0, (E - RING) // RING) as i:
                for k in range(RING):
                    e = i * RING + RING + k
                    used = pool.value_load(first_tab[0:1, bass.ds(e - (RING - 1), 1)],
                                           min_val=0, max_val=TILES)
                    pool.wait_ge(y_made.sem, used + y_made.start)
                    load_expert(e, k)
                    pool.wait_ge(expert_dma.sem, expert_dma.upto(e))
                    pool.sem_inc(expert_in.sem, 1)

            for par in range(2):
                pool.wait_ge(y_stored[par].sem, y_stored[par].upto(TILES // 2 - 1))

            def gather(n, k):
                pool.wait_ge(y_at_made.sem, y_at_made.upto(n))
                apart(pool)
                for c in range(TOPK):
                    pool.indirect_dma_start(
                        out=y_in[:, k, c, :], in_=routed_y, out_offset=None,
                        in_offset=bass.IndirectOffsetOnAxis(ap=y_at[:, k, c:c + 1], axis=0),
                    ).then_inc(y_got[k].sem, 16)

            for k in range(4):
                gather(k, k)
            with pool.Fori(1, NT // 4) as i:
                for k in range(4):
                    pool.wait_ge(fin_made.sem, fin_made.upto(i * 4 + k - 4))
                    gather(i * 4 + k, k)

        @block.scalar
        def _(act):
            s = nc.scalar
            small = [
                (gate_rows[0:NH, :], igate_w), (gate_rows[NH:2 * NH, :], fgate_w),
                (router_rows[:, :], router_w),
                (gate_bias[:, 0:NH], igate_b.partition_broadcast(P)),
                (gate_bias[:, NH:2 * NH], fgate_b.partition_broadcast(P)),
                (ln_row[:, :], ln_scale.partition_broadcast(P)),
                (g_col[:, 0:1], g_xattn.partition_broadcast(P)),
                (g_col[:, 1:2], g_ffn.partition_broadcast(P)),
            ]
            assert len(small) == N_SMALL
            for to, of in small:
                act.dma_start(to, of).then_inc(small_in.sem, 16)
            for to, of in ((sh_gate, shared_gate), (sh_up, shared_up), (sh_down, shared_down)):
                act.dma_start(to, of.rearrange("(c p) i -> p c i", p=P)).then_inc(weights_in.sem, 16)
            act.wait_ge(small_in.sem, small_in.upto(N_SMALL - 1))
            s.activation(tanh_g[:, :], g_col[:, :], ACT.Tanh).then_inc(act_const.sem, 1)

            def turn_out(j, to):
                return s.copy(to[:, :, j * P:(j + 1) * P], TP[:, :].rearrange("p (c t) -> p c t", c=DC))

            def turn_ctx(b, j):
                act.wait_ge(ctx_turned.sem, ctx_turned.upto(b.n, j + 1))
                act.wait_ge(qk_made.sem, qk_made.upto(b.n - 2))
                turn_out(j, ctxT[:, b.par]).then_inc(ctxT_made.sem, 1)

            def turn_x(b, j):
                act.wait_ge(xn_turned.sem, xn_turned.upto(b.n, j + 1))
                turn_out(j, xnT[:, b.par]).then_inc(xnT_made.sem, 1)

            def turn(b, j):
                act.wait_ge(x2_turned.sem, x2_turned.upto(b.n, j + 1))
                act.wait_ge(sh_made.sem, sh_made.upto(b.n - 1))
                turn_out(j, x2nT[:]).then_inc(x2nT_made.sem, 1)

            def gates_act(b):
                act.wait_ge(gates_read.sem, gates_read.upto(b.n))
                s.activation(f_exp[:, :, :], f_abs[:, :, :], ACT.Exp, scale=-1.0).then_inc(f_exp_made.sem, 1)
                act.wait_ge(f_exp_made.sem, f_exp_made.upto(b.n))
                s.activation(f_ln[:, :, :], f_exp[:, :, :], ACT.Ln, bias=1.0).then_inc(f_ln_made.sem, 1)

            def max_columns(b):
                act.wait_ge(max_log_made.sem, max_log_made.upto(b.n))
                act.wait_ge(heads_made.sem, heads_made.upto(b.n - 2))
                s.activation(norm_floor[:, b.par], max_log[:, :, :], ACT.Exp, scale=-1.0
                             ).then_inc(floor_made.sem, 1)

            def head(b, h):
                act.wait_ge(max_spread.sem, max_spread.upto(b.n, h + 1))
                act.wait_ge(c_made.sem, c_made.upto(b.n, h - 1))
                k = h % 2
                s.activation(decay[:, k, 0:S], MB[k][:, 0:S], ACT.Exp,
                             bias=key_log[:, b.par, 0, h:h + 1], scale=-1.0)
                s.activation(decay[:, k, S:TRI], MB[k][:, S:TRI], ACT.Exp,
                             bias=key_log[:, b.par, 1, h:h + 1], scale=-1.0).then_inc(decay_made.sem, 1)

            def router(b):
                act.wait_ge(gap_made.sem, gap_made.upto(b.n))
                s.activation(gap_exp[:, :], gap[:, :], ACT.Exp).then_inc(gap_exp_made.sem, 1)

            def shared(b, m):
                act.wait_ge(sh_made.sem, sh_made.upto(b.n, m + 1))
                act.wait_ge(sh_silu_made.sem, sh_silu_made.upto(b.n, m))
                s.activation(silu_t[:, :], FF[:, 0:S], ACT.Tanh, scale=0.5).then_inc(sh_tanh_made.sem, 1)

            def step(t, front=True, attend=True, experts=True):
                F, A, G = t + 1, t, t + -1
                if experts:
                    turn(G, 0)
                if attend:
                    head(A, 0)
                if experts:
                    turn(G, 1)
                if attend:
                    head(A, 1)
                if front:
                    turn_ctx(F, 0)
                if experts:
                    router(G)
                if attend:
                    head(A, 2)
                if front:
                    turn_ctx(F, 1)
                if experts:
                    shared(G, 0)
                if front:
                    turn_x(F, 0)
                if attend:
                    head(A, 3)
                if front:
                    turn_x(F, 1)
                if experts:
                    shared(G, 1)
                if front:
                    gates_act(F)
                if attend:
                    head(A, 4)
                if experts:
                    shared(G, 2)
                if attend:
                    head(A, 5)
                if experts:
                    shared(G, 3)
                if attend:
                    head(A, 6)
                if front:
                    max_columns(F)
                if attend:
                    head(A, 7)

            step(Item(0, -1), attend=False, experts=False)
            step(Item(0, 0), experts=False)
            step(Item(0, 1))
            with act.Fori(0, (B - 4) // 2) as i:
                step(Item(i, 2))
                step(Item(i, 3))
            step(Item(0, B - 2))
            step(Item(0, B - 1), front=False)
            step(Item(0, B), front=False, attend=False)

            def copy_x(t):
                act.wait_ge(xt_turned.sem, xt_turned.upto(t.n))
                s.copy(xtT[:, t.par, :], bank[t.par][:, :]).then_inc(xtT_made.sem, 1)

            def tanh_gate(t):
                act.wait_ge(gu_made.sem, gu_made.upto(t.n))
                s.activation(act_t[:, t.par, :], bank[2 + t.par][:, 0:I], ACT.Tanh, scale=0.5
                             ).then_inc(act_tanh_made.sem, 1)

            def copy_y(t):
                act.wait_ge(y_made.sem, y_made.upto(t.n))
                act.wait_ge(y_stored[t.par].sem, y_stored[t.par].upto(t.half - 1))
                s.copy(y_out[:, t.par, :], bank[5 + t.par][:, :]).then_inc(y_copied.sem, 1)

            def expert_step(t, ahead2=True, ahead1=True):
                if ahead2:
                    copy_x(t + 2)
                if ahead1:
                    tanh_gate(t + 1)
                copy_y(t)

            copy_x(Item(0, 0))
            copy_x(Item(0, 1))
            tanh_gate(Item(0, 0))
            expert_step(Item(0, 0))
            expert_step(Item(0, 1))
            with act.Fori(0, (TILES - 4) // 2) as i:
                expert_step(Item(i, 2))
                expert_step(Item(i, 3))
            expert_step(Item(0, TILES - 2), ahead2=False)
            expert_step(Item(0, TILES - 1), ahead2=False, ahead1=False)

        @block.tensor
        def _(pe):
            mm, tr = nc.tensor.matmul, nc.tensor.transpose

            pe.wait_ge(pool_const.sem, POOL_CONSTS)
            pe.wait_ge(small_in.sem, small_in.upto(N_SMALL - 1))
            for c in range(3 * DC):
                tr(SM[:, c * 16:(c + 1) * 16], gate_rows[:, c * P:(c + 1) * P], ident[0:2 * NH, 0:2 * NH])
            for c in range(DC):
                last = tr(SM[:, (3 * DC + c) * 16:(3 * DC + c + 1) * 16],
                          router_rows[:, c * P:(c + 1) * P], ident[0:E, 0:E])
            last.then_inc(wT_made.sem, 1)
            pe.wait_ge(wT_copied.sem, 3)

            def turn_tile(src):
                for c in range(DC):
                    last = tr(TP[:, c * P:(c + 1) * P], src[:, c * P:(c + 1) * P], ident[:, :])
                return last

            def turn(b, j, attend):
                pe.wait_ge(x2n_made.sem, x2n_made.upto(b.n, j + 1))
                if j == 0:
                    if attend:
                        pe.wait_ge(xnT_made.sem, xnT_made.upto(b.n + 1))
                    else:
                        pe.wait_ge(x2nT_made.sem, x2nT_made.upto(b.n - 1))
                else:
                    pe.wait_ge(x2nT_made.sem, x2nT_made.upto(b.n, j))
                turn_tile(x2n[:, b.par, j, :]).then_inc(x2_turned.sem, 1)

            def turn_ctx(b, j, experts, attend):
                pe.wait_ge(c_in[b.par].sem, c_in[b.par].upto(b.half))
                if j:
                    pe.wait_ge(ctxT_made.sem, ctxT_made.upto(b.n, j))
                elif experts:
                    pe.wait_ge(x2nT_made.sem, x2nT_made.upto(b.n - 2))
                elif attend:
                    pe.wait_ge(xnT_made.sem, xnT_made.upto(b.n - 1))
                turn_tile(cs_in[:, b.par, j, :]).then_inc(ctx_turned.sem, 1)

            def turn_x(b, j):
                pe.wait_ge(xn_made.sem, xn_made.upto(b.n, j + 1))
                if j:
                    pe.wait_ge(xnT_made.sem, xnT_made.upto(b.n, j))
                else:
                    pe.wait_ge(ctxT_made.sem, ctxT_made.upto(b.n))
                turn_tile(xn[:, j, :]).then_inc(xn_turned.sem, 1)

            def gates_pe(b, experts, attend):
                pe.wait_ge(xnT_made.sem, xnT_made.upto(b.n))
                pe.wait_ge(ctxT_made.sem, ctxT_made.upto(b.n))
                if experts:
                    pe.wait_ge(logits_made.sem, logits_made.upto(b.n - 2))
                elif attend:
                    pe.wait_ge(max_log_made.sem, max_log_made.upto(b.n - 1))
                for j in range(ST):
                    for c in range(2 * DC):
                        src = (xnT if c < DC else ctxT)[:, b.par, c % DC, j * P:(j + 1) * P]
                        last = mm(SM[:, j * 16:(j + 1) * 16], src, gate_wT[:, c, :],
                                  start=(c == 0), stop=(c == 2 * DC - 1))
                last.then_inc(gates_made.sem, 1)

            def cumulate(b, experts):
                pe.wait_ge(log_f_made.sem, log_f_made.upto(b.n))
                if experts:
                    pe.wait_ge(place_step.sem, place_step.upto(b.n - 2, 1))
                mm(SM[:, 0:NH], upto_f[:, :], log_f[:, 0, :], start=True, stop=True)
                mm(SM[:, NH:2 * NH], ones_f[:, :], log_f[:, 0, :], start=True, stop=False)
                mm(SM[:, NH:2 * NH], upto_f[:, :], log_f[:, 1, :], start=False, stop=True
                   ).then_inc(cum_made.sem, 1)

            def maximum(b):
                pe.wait_ge(key_made.sem, key_made.upto(b.n))
                for j in range(ST):
                    last = tr(SM[0:NH, j * P:(j + 1) * P], key_log[:, b.par, j, :], ident[:, :])
                last.then_inc(key_turned.sem, 1)

            def max_columns(b):
                pe.wait_ge(max_step.sem, max_step.upto(b.n, 2))
                apart(pe)
                for j in range(ST):
                    last = tr(SM[:, j * NH:(j + 1) * NH], max_row[:, j * P:(j + 1) * P], ident[0:NH, 0:NH])
                last.then_inc(max_turned.sem, 1)

            def head(b, h):
                k = h % 2
                rows = slice(DH * (h % 2), DH * (h % 2) + DH)
                c = h // 2
                pe.wait_ge(xnT_made.sem, xnT_made.upto(b.n))
                pe.wait_ge(ctxT_made.sem, ctxT_made.upto(b.n))
                pe.wait_ge(max_step.sem, max_step.upto(b.n))
                pe.wait_ge(c_made.sem, c_made.upto(b.n, h - 1))
                pe.wait_ge(decay_made.sem, decay_made.upto(b.n, h - 1))
                mm(QK[k][:, 0:S], ctxT[rows, b.par, c, 0:P], xnT[rows, b.par, c, 0:S],
                   start=True, stop=True)
                mm(QK[k][:, S:TRI], ctxT[rows, b.par, c, P:S], xnT[rows, b.par, c, P:S],
                   start=True, stop=True).then_inc(qk_made.sem, 1)
                for at, n in ((0, S), (S, P)):
                    mm(MB[k][:, at:at + n], head_sel[0:96, h, :], max_parts[0:96, b.par, S - n:S],
                       start=True, stop=False)
                    last = mm(MB[k][:, at:at + P], identb[:, :], mask_b[:, :], start=False, stop=True)
                last.then_inc(max_spread.sem, 1)

            def pv(b, h):
                k = h % 2
                pe.wait_ge(c_made.sem, c_made.upto(b.n, h + 1))
                pe.wait_ge(v_made.sem, v_made.upto(b.n))
                if h % 2 == 0:
                    pe.wait_ge(heads_made.sem, heads_made.upto(b.n, h // 2))
                r = 2 * k * VW
                mm(HO[:, r:r + VW], cmat[:, k, 0:P], v_aug[:, b.par, 0, h, :], start=True, stop=True)
                mm(HO[:, r + VW:r + 2 * VW], cmat[:, k, P:S], v_aug[:, b.par, 0, h, :],
                   start=True, stop=False)
                mm(HO[:, r + VW:r + 2 * VW], cmat[:, k, S:TRI], v_aug[:, b.par, 1, h, :],
                   start=False, stop=True).then_inc(pv_made.sem, 1)

            def router(b, attend):
                pe.wait_ge(x2nT_made.sem, x2nT_made.upto(b.n))
                if attend:
                    pe.wait_ge(max_log_made.sem, max_log_made.upto(b.n + 1))
                for j in range(ST):
                    for c in range(DC):
                        last = mm(SM[:, j * E:(j + 1) * E], x2nT[:, c, j * P:(j + 1) * P],
                                  router_wT[:, c, :], start=(c == 0), stop=(c == DC - 1))
                last.then_inc(router_made.sem, 1)

            def rank(b, front):
                pe.wait_ge(chosen_made.sem, chosen_made.upto(b.n, 2))
                if front:
                    pe.wait_ge(gates_read.sem, gates_read.upto(b.n + 2))
                mm(SM[:, 0:E], before_b[:, :], chosen[:, 0, :], start=True, stop=False)
                mm(SM[:, 0:E], ones_b[:, :], taken[:, b.par, :], start=False, stop=True)
                mm(SM[:, E:2 * E], before_b[:, :], chosen[:, 1, :], start=True, stop=False)
                mm(SM[:, E:2 * E], ones_b[:, :], taken_mid[:, :], start=False, stop=True
                   ).then_inc(ranks_made.sem, 1)

            def shared(b, m):
                pe.wait_ge(weights_in.sem, weights_in.upto(N_SHARED - 1))
                pe.wait_ge(x2nT_made.sem, x2nT_made.upto(b.n))
                if m:
                    pe.wait_ge(sh_act_made.sem, sh_act_made.upto(b.n, m))
                else:
                    pe.wait_ge(base_made.sem, base_made.upto(b.n - 1))
                for at, w in ((0, sh_gate), (S, sh_up)):
                    for c in range(DC):
                        last = mm(FF[:, at:at + S], w[:, c, m * P:(m + 1) * P], x2nT[:, c, :],
                                  start=(c == 0), stop=(c == DC - 1))
                last.then_inc(sh_made.sem, 1)

            def shared_down(b, j):
                pe.wait_ge(sh_act_made.sem, sh_act_made.upto(b.n))
                if j:
                    pe.wait_ge(base_made.sem, base_made.upto(b.n, j))
                for m in range(SC):
                    last = mm(FF[:, :], sh_actT[:, m, j * P:(j + 1) * P], sh_down[:, m, :],
                              start=(m == 0), stop=(m == SC - 1))
                last.then_inc(sh_down_made.sem, 1)

            def step(t, front=True, attend=True, experts=True):
                F, A, G = t + 1, t, t + -1
                if experts:
                    turn(G, 0, attend)
                if attend:
                    head(A, 0)
                if experts:
                    turn(G, 1, attend)
                if attend:
                    head(A, 1)
                    pv(A, 0)
                if front:
                    turn_ctx(F, 0, experts, attend)
                if experts:
                    router(G, attend)
                if attend:
                    head(A, 2)
                    pv(A, 1)
                if front:
                    turn_ctx(F, 1, experts, attend)
                if experts:
                    shared(G, 0)
                if front:
                    turn_x(F, 0)
                if attend:
                    head(A, 3)
                    pv(A, 2)
                if front:
                    turn_x(F, 1)
                if experts:
                    shared(G, 1)
                if front:
                    gates_pe(F, experts, attend)
                if experts:
                    rank(G, front)
                if attend:
                    head(A, 4)
                    pv(A, 3)
                if experts:
                    shared(G, 2)
                if front:
                    cumulate(F, experts)
                if attend:
                    head(A, 5)
                    pv(A, 4)
                if experts:
                    shared(G, 3)
                if front:
                    maximum(F)
                if attend:
                    head(A, 6)
                    pv(A, 5)
                if experts:
                    shared_down(G, 0)
                if front:
                    max_columns(F)
                if attend:
                    head(A, 7)
                    pv(A, 6)
                    pv(A, 7)
                if experts:
                    shared_down(G, 1)

            step(Item(0, -1), attend=False, experts=False)
            step(Item(0, 0), experts=False)
            step(Item(0, 1))
            with pe.Fori(0, (B - 4) // 2) as i:
                step(Item(i, 2))
                step(Item(i, 3))
            step(Item(0, B - 2))
            step(Item(0, B - 1), front=False)
            step(Item(0, B), front=False, attend=False)

            pe.wait_ge(chosen_made.sem, chosen_made.upto(B - 1))
            pe.wait_ge(place_step.sem, place_step.upto(B - 1, 1))
            mm(SM[:, 0:E], ones_b[:, :], taken[:, B % 2, :], start=True, stop=True).then_inc(counts_made.sem, 1)
            pe.wait_ge(table_step.sem, TABLE_STEPS)
            tr(SM[0:1, 0:P], tile_info[:, 2:3], ident[:, :])
            tr(SM[0:1, P:2 * P], tile_info[:, 3:4], ident[:, :]).then_inc(tables_turned.sem, 1)

            def turn_rows(n, t, k):
                pe.wait_ge(xt_in[k].sem, n)
                pe.wait_ge(xtT_made.sem, xtT_made.upto(t.n - 2))
                for c in range(DC):
                    last = tr(bank[t.par][:, c * P:(c + 1) * P], xt[:, k, c * P:(c + 1) * P], ident[:, :])
                last.then_inc(xt_turned.sem, 1)

            def expert_of(t):
                return pe.value_load(expert_tab[0:1, bass.ds(t.n, 1)], min_val=0, max_val=E - 1)

            def gate_up(t):
                e = expert_of(t)
                slot = pe.snap(e % RING)
                pe.wait_ge(expert_in.sem, e + 1)
                pe.wait_ge(xtT_made.sem, xtT_made.upto(t.n))
                pe.wait_ge(act_made.sem, act_made.upto(t.n - 2))
                for c in range(DC):
                    last = mm(bank[2 + t.par][:, :], xtT[:, t.par, c * P:(c + 1) * P],
                              w_gu[:, bass.ds(slot, 1), c, :].rearrange("p a i -> p (a i)"),
                              start=(c == 0), stop=(c == DC - 1))
                last.then_inc(gu_made.sem, 1)

            def turn_act(t):
                pe.wait_ge(act_made.sem, act_made.upto(t.n))
                pe.wait_ge(actT_made.sem, actT_made.upto(t.n - 1))
                for c in range(IC):
                    last = tr(bank[4][:, c * P:(c + 1) * P], act_a[:, t.par, c * P:(c + 1) * P], ident[:, :])
                last.then_inc(act_turned.sem, 1)

            def down(t):
                slot = pe.snap(expert_of(t) % RING)
                pe.wait_ge(actT_made.sem, actT_made.upto(t.n))
                pe.wait_ge(y_copied.sem, y_copied.upto(t.n - 2))
                for c in range(IC):
                    last = mm(bank[5 + t.par][:, :], act_aT[:, t.par, c * P:(c + 1) * P],
                              w_dn[:, bass.ds(slot, 1), c, :].rearrange("p a i -> p (a i)"),
                              start=(c == 0), stop=(c == IC - 1))
                last.then_inc(y_made.sem, 1)

            def expert_step(t, k, lap, ahead2=True, ahead1=True):
                if ahead2:
                    turn_rows(lap * 16 + 16, t + 2, k)
                turn_act(t)
                if ahead1:
                    gate_up(t + 1)
                down(t)

            pe.sem_inc(y_made.sem, y_made.start)
            pe.wait_ge(expert_in.sem, RING)
            pe.wait_ge(tables_made.sem, tables_made.upto(0))
            turn_rows(16, Item(0, 0), 0)
            turn_rows(16, Item(0, 1), 1)
            gate_up(Item(0, 0))
            expert_step(Item(0, 0), 2, 0)
            expert_step(Item(0, 1), 3, 0)
            with pe.Fori(0, (TILES - 4) // 4) as i:
                for u in range(4):
                    expert_step(Item(i * 2, 2 + u), u, i + 1)
            for n in range(TILES - 2, TILES):
                expert_step(Item(0, n), 0, 0, ahead2=False, ahead1=n + 1 < TILES)

        @block.vector
        def _(dve):
            v = nc.vector

            pe_w = SM[:, 0:(3 * DC + DC) * 16].rearrange("p (c n) -> p c n", n=16)
            dve.wait_ge(wT_made.sem, 1)
            v.tensor_copy(gate_wT[:, :, :], pe_w[:, 0:2 * DC, :]).then_inc(wT_copied.sem, 1)
            v.tensor_copy(router_wT[:, :, :], pe_w[:, 3 * DC:4 * DC, :]).then_inc(wT_copied.sem, 1)
            dve.wait_ge(wT_copied.sem, 2)
            v.tensor_tensor(gate_wT[:, DC:2 * DC, :], pe_w[:, 2 * DC:3 * DC, :], gate_wT[:, DC:2 * DC, :],
                            ALU.add).then_inc(wT_copied.sem, 1)
            dve.wait_ge(act_const.sem, 1)
            v.tensor_scalar(ln_row[:, :], ln_row[:, :], tanh_g[:, 0:1], None, ALU.mult
                            ).then_inc(wT_copied.sem, 1)
            dve.wait_ge(wT_copied.sem, 4)
            dve.wait_ge(pool_const.sem, POOL_CONSTS)

            def base_tile(b, j):
                return base_out[:, bass.ds(b.n * ST + j, 1), :].rearrange("p a d -> p (a d)")

            def norm_front(b):
                dve.wait_ge(x_in[b.par].sem, x_in[b.par].upto(b.half))
                apart(dve)
                for j in range(ST):
                    v.bn_stats(ln_stat[:, j, :], xs[:, b.par, j, :]).then_inc(ln_step.sem, 1)
                for j in range(ST):
                    dve.wait_ge(ln_step.sem, ln_step.upto(b.n, j + 1))
                    apart(dve)
                    v.bn_aggr(ln_mv[:, j, :], ln_stat[:, j, :]).then_inc(ln_step.sem, 1)
                dve.wait_ge(ln_step.sem, ln_step.upto(b.n))
                v.tensor_scalar(ln_var[:, :], ln_mv[:, :, 1], LN_EPS, None, ALU.add
                                ).then_inc(ln_var_made.sem, 1)
                dve.wait_ge(ln_rstd_made.sem, ln_rstd_made.upto(b.n))
                dve.wait_ge(xn_turned.sem, xn_turned.upto(b.n - 1))
                for j in range(ST):
                    v.tensor_scalar(xn[:, j, :], xs[:, b.par, j, :], ln_mv[:, j, 0:1], ln_rstd[:, j:j + 1],
                                    ALU.subtract, ALU.mult).then_inc(xn_made.sem, 1)

            def gates_dve(b):
                dve.wait_ge(gates_made.sem, gates_made.upto(b.n))
                v.tensor_tensor(gates[:, :, :], SM[:, 0:ST * 16].rearrange("p (j n) -> p j n", j=ST),
                                gate_bias[:, :].unsqueeze(1).to_broadcast([P, ST, 2 * NH]),
                                ALU.add).then_inc(gates_read.sem, 1)
                dve.wait_ge(gates_read.sem, gates_read.upto(b.n, 1))
                forget = gates[:, :, NH:2 * NH]
                v.scalar_tensor_tensor(f_abs[:, :, :], forget, -1.0, forget, ALU.mult, ALU.max
                                       ).then_inc(gates_read.sem, 1)
                dve.wait_ge(f_ln_made.sem, f_ln_made.upto(b.n))
                v.scalar_tensor_tensor(log_f[:, :, :], gates[:, :, NH:2 * NH], 0.0, f_ln[:, :, :],
                                       ALU.min, ALU.subtract).then_inc(log_f_made.sem, 1)

            def cumulate(b):
                dve.wait_ge(cum_made.sem, cum_made.upto(b.n))
                dve.wait_ge(decay_made.sem, decay_made.upto(b.n - 2))
                sums = SM[:, 0:ST * NH].rearrange("p (j n) -> p j n", j=ST)
                v.tensor_copy(cum_f[:, :, :], sums).then_inc(key_made.sem, 1)
                v.tensor_tensor(key_log[:, b.par], gates[:, :, 0:NH], sums, ALU.subtract
                                ).then_inc(key_made.sem, 1)

            def maximum(b):
                dve.wait_ge(key_turned.sem, key_turned.upto(b.n))
                v.tensor_copy(key_row[:, :], SM[0:NH, 0:S]).then_inc(max_step.sem, 1)
                dve.wait_ge(max_step.sem, max_step.upto(b.n, 1))
                v.tensor_tensor_scan(max_row[:, :], key_row[:, :], key_row[:, :], -3.0e38,
                                     ALU.max, ALU.max).then_inc(max_step.sem, 1)
                dve.wait_ge(max_step.sem, max_step.upto(b.n, 2))
                dve.wait_ge(max_spread.sem, max_spread.upto(b.n - 2))
                v.tensor_copy(max_parts[0:NH, b.par, :], max_row[:, :]).then_inc(max_step.sem, 1)
                dve.wait_ge(max_step.sem, max_step.upto(b.n, 3))
                v.tensor_tensor(max_rest[:, :], max_row[:, :], max_parts[0:NH, b.par, :], ALU.subtract
                                ).then_inc(max_step.sem, 1)
                dve.wait_ge(max_step.sem, max_step.upto(b.n, 4))
                v.tensor_copy(max_mid[:, :], max_rest[:, :]).then_inc(max_step.sem, 1)
                dve.wait_ge(max_step.sem, max_step.upto(b.n, 5))
                v.tensor_copy(max_parts[32:32 + NH, b.par, :], max_mid[:, :]).then_inc(max_step.sem, 1)
                v.tensor_tensor(max_parts[64:64 + NH, b.par, :], max_rest[:, :], max_mid[:, :],
                                ALU.subtract).then_inc(max_step.sem, 1)

            def max_columns(b):
                dve.wait_ge(max_turned.sem, max_turned.upto(b.n))
                v.tensor_tensor(max_log[:, :, :], SM[:, 0:ST * NH].rearrange("p (j n) -> p j n", j=ST),
                                cum_f[:, :, :], ALU.add).then_inc(max_log_made.sem, 1)

            def head(b, h):
                k = h % 2
                dve.wait_ge(qk_made.sem, qk_made.upto(b.n, h + 1))
                dve.wait_ge(decay_made.sem, decay_made.upto(b.n, h + 1))
                dve.wait_ge(pv_made.sem, pv_made.upto(b.n, h - 1))
                v.scalar_tensor_tensor(cmat[:, k, :], QK[k][:, 0:TRI], QK_SCALE, decay[:, k, :],
                                       ALU.mult, ALU.mult).then_inc(c_made.sem, 1)

            def out_pair(b, q):
                dve.wait_ge(pv_made.sem, pv_made.upto(b.n, 2 * q + 2))
                dve.wait_ge(floor_made.sem, floor_made.upto(b.n))
                pair = HO[:, 0:2 * ST * VW].rearrange("p (h j w) -> p h j w", h=2, w=VW)
                v.scalar_tensor_tensor(norm[:, :, :], pair[:, :, :, DH], -1.0,
                                       norm_floor[:, b.par, :, 2 * q:2 * q + 2].rearrange("p j h -> p h j"),
                                       ALU.mult, ALU.max).then_inc(norm_step.sem, 1)
                dve.wait_ge(norm_step.sem, norm_step.upto(b.n, 4 * q + 1))
                v.tensor_tensor(norm_abs[:, :, :], pair[:, :, :, DH], norm[:, :, :], ALU.max
                                ).then_inc(norm_step.sem, 1)
                dve.wait_ge(norm_step.sem, norm_step.upto(b.n, 4 * q + 2))
                v.tensor_scalar(norm_e[:, :, :], norm_abs[:, :, :], NORM_EPS, None, ALU.add
                                ).then_inc(norm_step.sem, 1)
                dve.wait_ge(norm_step.sem, norm_step.upto(b.n, 4 * q + 3))
                v.reciprocal(norm_inv[:, :, :], norm_e[:, :, :]).then_inc(norm_step.sem, 1)
                dve.wait_ge(norm_step.sem, norm_step.upto(b.n, 4 * q + 4))
                v.tensor_tensor(
                    heads[:, :, 2 * q * DH:(2 * q + 2) * DH].rearrange("p j (h d) -> p h j d", h=2),
                    pair[:, :, :, 0:DH], norm_inv[:, :, :].unsqueeze(3).to_broadcast([P, 2, ST, DH]),
                    ALU.mult).then_inc(heads_made.sem, 1)

            def post(b):
                dve.wait_ge(heads_made.sem, heads_made.upto(b.n))
                apart(dve)
                n = [0]

                def step(ins):
                    n[0] += 1
                    ins.then_inc(post_step.sem, 1)

                for j in range(ST):
                    step(v.bn_stats(h_stat[:, j, :], heads[:, j, :]))
                for j in range(ST):
                    dve.wait_ge(post_step.sem, post_step.upto(b.n, j + 1))
                    apart(dve)
                    step(v.bn_aggr(h_mv[:, j, :], h_stat[:, j, :]))
                dve.wait_ge(post_step.sem, post_step.upto(b.n, n[0]))
                v.tensor_scalar(h_var[:, :], h_mv[:, :, 1], LN_EPS, None, ALU.add).then_inc(h_var_made.sem, 1)
                for j in range(ST):
                    step(v.scalar_tensor_tensor(heads[:, j, :], heads[:, j, :], h_mv[:, j, 0:1],
                                                ln_row[:, :], ALU.subtract, ALU.mult))
                dve.wait_ge(post_step.sem, post_step.upto(b.n, n[0]))
                dve.wait_ge(h_rstd_made.sem, h_rstd_made.upto(b.n))
                for j in range(ST):
                    v.scalar_tensor_tensor(base_tile(b, j), heads[:, j, :], h_rstd[:, j:j + 1],
                                           xs[:, b.par, j, :], ALU.mult, ALU.add
                                           ).then_inc(x2_made.sem, 1)
                for j in range(ST):
                    dve.wait_ge(x2_made.sem, x2_made.upto(b.n, j + 1))
                    apart(dve)
                    step(v.bn_stats(x2_stat[:, j, :], base_tile(b, j)))
                for j in range(ST):
                    dve.wait_ge(post_step.sem, post_step.upto(b.n, 3 * ST + j + 1))
                    apart(dve)
                    step(v.bn_aggr(x2_mv[:, j, :], x2_stat[:, j, :]))
                dve.wait_ge(post_step.sem, post_step.upto(b.n, n[0]))
                v.tensor_scalar(x2_var[:, :], x2_mv[:, :, 1], LN_EPS, None, ALU.add
                                ).then_inc(x2_var_made.sem, 1)
                dve.wait_ge(x2_rstd_made.sem, x2_rstd_made.upto(b.n))
                dve.wait_ge(scattered[b.par].sem, scattered[b.par].upto(b.half - 1))
                for j in range(ST):
                    v.tensor_scalar(x2n[:, b.par, j, :], base_tile(b, j), x2_mv[:, j, 0:1],
                                    x2_rstd[:, j:j + 1], ALU.subtract, ALU.mult).then_inc(x2n_made.sem, 1)

            def router(b):
                dve.wait_ge(router_made.sem, router_made.upto(b.n))
                v.tensor_copy(logits[:, :, :], SM[:, 0:ST * E].rearrange("p (j n) -> p j n", j=ST)
                              ).then_inc(logits_made.sem, 1)
                dve.wait_ge(logits_made.sem, logits_made.upto(b.n))
                apart(dve)
                for j in range(ST):
                    v.max(top8[:, j, :], logits[:, j, :]).then_inc(top_step.sem, 1)
                    dve.wait_ge(top_step.sem, top_step.upto(b.n, 2 * j + 1))
                    apart(dve)
                    v.max_index(top8_at[:, j, :], top8[:, j, :], logits[:, j, :]).then_inc(top_step.sem, 1)
                v.tensor_tensor(gap[:, :], top8[:, :, 1], top8[:, :, 0], ALU.subtract
                                ).then_inc(gap_made.sem, 1)
                dve.wait_ge(top_step.sem, top_step.upto(b.n, 2 * ST))
                v.tensor_copy(top_at[:, :, :], top8_at[:, :, 0:TOPK]).then_inc(top_step.sem, 1)
                dve.wait_ge(top_step.sem, top_step.upto(b.n, 2 * ST + 1))
                for j in range(ST):
                    for k in range(TOPK):
                        v.tensor_scalar(one_hot[:, j, k, :], expert_no[:, :], top_at[:, j, k:k + 1], None,
                                        ALU.is_equal).then_inc(hot_made.sem, 1)
                dve.wait_ge(hot_made.sem, hot_made.upto(b.n))
                v.tensor_tensor(chosen[:, :, :], one_hot[:, :, 0, :], one_hot[:, :, 1, :], ALU.add
                                ).then_inc(chosen_made.sem, 1)
                dve.wait_ge(chosen_made.sem, chosen_made.upto(b.n, 1))
                v.tensor_tensor(taken_mid[:, :], taken[:, b.par, :], chosen[:, 0, :], ALU.add
                                ).then_inc(chosen_made.sem, 1)
                dve.wait_ge(chosen_made.sem, chosen_made.upto(b.n, 2))
                dve.wait_ge(ranks_made.sem, ranks_made.upto(b.n - 1))
                v.tensor_tensor(taken[:, 1 - b.par, :], taken_mid[:, :], chosen[:, 1, :], ALU.add
                                ).then_inc(chosen_made.sem, 1)
                dve.wait_ge(gap_exp_made.sem, gap_exp_made.upto(b.n))
                v.tensor_scalar(gap_den[:, :], gap_exp[:, :], 1.0, None, ALU.add).then_inc(w_step.sem, 1)
                dve.wait_ge(w_step.sem, w_step.upto(b.n, 1))
                v.reciprocal(top_w[:, :, 0], gap_den[:, :]).then_inc(w_step.sem, 1)
                dve.wait_ge(w_step.sem, w_step.upto(b.n, 2))
                v.tensor_tensor(top_w[:, :, 1], top_w[:, :, 0], gap_exp[:, :], ALU.mult
                                ).then_inc(w_step.sem, 1)
                dve.wait_ge(w_step.sem, w_step.upto(b.n, 3))
                v.tensor_scalar(all_w[:, bass.ds(b.n, 1), :].rearrange("p a n -> p (a n)"),
                                top_w[:, :, :].rearrange("p j k -> p (j k)"), tanh_g[:, 1:2], None,
                                ALU.mult).then_inc(route_kept.sem, 1)
                v.tensor_copy(all_hot[:, bass.ds(b.n, 1)].rearrange("p a n e -> p (a n e)"),
                              one_hot[:, :, :, :].rearrange("p j k e -> p (j k e)")
                              ).then_inc(route_kept.sem, 1)

            def rank(b):
                dve.wait_ge(ranks_made.sem, ranks_made.upto(b.n))
                v.tensor_tensor(place[:, :, :], SM[:, 0:ST * E].rearrange("p (j n) -> p j n", j=ST),
                                expert_row[:, :].unsqueeze(1).to_broadcast([P, ST, E]), ALU.add
                                ).then_inc(place_step.sem, 1)
                dve.wait_ge(place_step.sem, place_step.upto(b.n, 1))
                v.tensor_tensor(place_pick[:, :, :].rearrange("p (j k) e -> p j k e", j=ST), one_hot[:, :, :, :],
                                place[:, :, :].unsqueeze(2).to_broadcast([P, ST, TOPK, E]), ALU.mult
                                ).then_inc(place_step.sem, 1)
                dve.wait_ge(place_step.sem, place_step.upto(b.n, 2))
                v.tensor_reduce(slot_f[:, :], place_pick[:, :, :], AX_X, ALU.add).then_inc(place_step.sem, 1)
                dve.wait_ge(place_step.sem, place_step.upto(b.n, 3))
                dve.wait_ge(scattered[b.par].sem, scattered[b.par].upto(b.half - 1))
                v.tensor_copy(slot_u[:, b.par, :], slot_f[:, :]).then_inc(slots_made.sem, 1)
                v.tensor_copy(all_slot[:, bass.ds(b.n, 1), :].rearrange("p a n -> p (a n)"), slot_f[:, :]
                              ).then_inc(route_kept.sem, 1)

            def shared(b, m):
                dve.wait_ge(sh_tanh_made.sem, sh_tanh_made.upto(b.n, m + 1))
                dve.wait_ge(sh_act_made.sem, sh_act_made.upto(b.n, m))
                v.scalar_tensor_tensor(silu_g[:, :], silu_t[:, :], 1.0, FF[:, 0:S], ALU.add, ALU.mult
                                       ).then_inc(sh_silu_made.sem, 1)
                dve.wait_ge(sh_silu_made.sem, sh_silu_made.upto(b.n, m + 1))
                dve.wait_ge(sh_down_made.sem, sh_down_made.upto(b.n - 1))
                v.scalar_tensor_tensor(sh_actT[:, m, :], silu_g[:, :], 0.5, FF[:, S:2 * S], ALU.mult, ALU.mult
                                ).then_inc(sh_act_made.sem, 1)

            def shared_down(b, j):
                dve.wait_ge(sh_down_made.sem, sh_down_made.upto(b.n, j + 1))
                v.scalar_tensor_tensor(base_tile(b, j), FF[:, :], tanh_g[:, 1:2], base_tile(b, j),
                                       ALU.mult, ALU.add
                                       ).then_inc(base_made.sem, 1)

            def step(t, front=True, attend=True, experts=True):
                F, A, G = t + 1, t, t + -1
                if front:
                    norm_front(F)
                if attend:
                    head(A, 0)
                    head(A, 1)
                if experts:
                    router(G)
                if attend:
                    head(A, 2)
                    out_pair(A, 0)
                if experts:
                    shared(G, 0)
                if attend:
                    head(A, 3)
                if experts:
                    shared(G, 1)
                if front:
                    gates_dve(F)
                if experts:
                    rank(G)
                if attend:
                    head(A, 4)
                    out_pair(A, 1)
                if experts:
                    shared(G, 2)
                if front:
                    cumulate(F)
                if attend:
                    head(A, 5)
                if experts:
                    shared(G, 3)
                if front:
                    maximum(F)
                if attend:
                    head(A, 6)
                    out_pair(A, 2)
                if experts:
                    shared_down(G, 0)
                if front:
                    max_columns(F)
                if attend:
                    head(A, 7)
                    out_pair(A, 3)
                if experts:
                    shared_down(G, 1)
                if attend:
                    post(A)

            step(Item(0, -1), attend=False, experts=False)
            step(Item(0, 0), experts=False)
            step(Item(0, 1))
            with dve.Fori(0, (B - 4) // 2) as i:
                step(Item(i, 2))
                step(Item(i, 3))
            step(Item(0, B - 2))
            step(Item(0, B - 1), front=False)
            step(Item(0, B), front=False, attend=False)

            steps = [0]

            def then(ins):
                steps[0] += 1
                ins.then_inc(table_step.sem, 1)
                dve.wait_ge(table_step.sem, steps[0])

            then(v.memset(zeros, 0.0))
            dve.wait_ge(counts_made.sem, counts_made.upto(0))
            then(v.tensor_copy(count[:, :], SM[:, 0:E]))
            then(v.tensor_tensor(pad_f[:, :], count[:, :], expert_row[:, :], ALU.add))
            then(v.tensor_scalar(pad_f[:, :], pad_f[:, :], part_no[:, 0:1], None, ALU.add))
            v.tensor_copy(pad_u[:, :], pad_f[:, :]).then_inc(pads_made.sem, 1)
            then(v.tensor_scalar(count_i[:, :], count[:, :], float(P - 1), None, ALU.add))
            then(v.tensor_scalar(tiles_i[:, :], count_i[:, :], P.bit_length() - 1, None,
                                 ALU.arith_shift_right))
            then(v.tensor_copy(tiles_f[:, :], tiles_i[:, :]))
            then(v.tensor_tensor_scan(tile_end[:, :], tiles_f[:, :], zeros[:, 0:E], 0.0, ALU.add, ALU.add))
            then(v.tensor_tensor(tile_first[:, :], tile_end[:, :], tiles_f[:, :], ALU.subtract))
            then(v.tensor_scalar(ended[:, :], tile_end[:, :], part_no[:, 0:1], None, ALU.is_le))
            then(v.tensor_reduce(tile_info[:, 0:1], ended[:, :], AX_X, ALU.add))
            then(v.tensor_tensor(ended_at[:, :], ended[:, :], tile_end[:, :], ALU.mult))
            then(v.tensor_reduce(tile_info[:, 1:2], ended_at[:, :], AX_X, ALU.max))
            then(v.tensor_tensor(tile_info[:, 1:2], part_no[:, 0:1], tile_info[:, 1:2], ALU.subtract))
            then(v.tensor_scalar(tile_info[:, 1:2], tile_info[:, 1:2], float(P), None, ALU.mult))
            then(v.tensor_scalar(tile_info[:, 2:3], tile_info[:, 0:1], float(CAP), tile_info[:, 1:2],
                                 ALU.mult, ALU.add))
            then(v.tensor_scalar(tile_info[:, 2:3], tile_info[:, 2:3], float(DUMP), None, ALU.min))
            then(v.tensor_scalar(tile_info[:, 3:4], tile_info[:, 0:1], float(E - 1), None, ALU.min))
            assert steps[0] == TABLE_STEPS
            v.tensor_copy(first_tab[:, :], tile_first[0:1, :])
            dve.wait_ge(tables_turned.sem, tables_turned.upto(0))
            v.tensor_copy(row_tab[:, :], SM[0:1, 0:P])
            v.tensor_copy(expert_tab[:, :], SM[0:1, P:2 * P]).then_inc(tables_made.sem, 1)

            def silu(t):
                dve.wait_ge(act_tanh_made.sem, act_tanh_made.upto(t.n))
                v.scalar_tensor_tensor(act_g[:, t.par, :], act_t[:, t.par, :], 1.0,
                                       bank[2 + t.par][:, 0:I], ALU.add, ALU.mult
                                       ).then_inc(act_silu_made.sem, 1)
                dve.wait_ge(act_silu_made.sem, act_silu_made.upto(t.n))
                v.scalar_tensor_tensor(act_a[:, t.par, :], act_g[:, t.par, :], 0.5,
                                       bank[2 + t.par][:, I:2 * I], ALU.mult, ALU.mult
                                       ).then_inc(act_made.sem, 1)

            def copy_actT(t):
                dve.wait_ge(act_turned.sem, act_turned.upto(t.n))
                dve.wait_ge(y_made.sem, y_made.upto(t.n - 2))
                v.tensor_copy(act_aT[:, t.par, :], bank[4][:, 0:I]).then_inc(actT_made.sem, 1)

            def expert_step(t, ahead1=True):
                copy_actT(t)
                if ahead1:
                    silu(t + 1)

            silu(Item(0, 0))
            expert_step(Item(0, 0))
            expert_step(Item(0, 1))
            then(v.tensor_scalar(shift[:, :], tile_first[:, :], float(P), None, ALU.mult))
            then(v.tensor_tensor(shift[:, :], shift[:, :], expert_row[:, :], ALU.subtract))
            hot = all_hot[:, :, :, :].rearrange("p b n e -> p (b n) e")
            then(v.tensor_tensor(hot_shift, hot, shift[:, :].unsqueeze(1).to_broadcast([P, B * ST * TOPK, E]),
                                 ALU.mult))
            then(v.tensor_reduce(y_slot_f[:, :], hot_shift, AX_X, ALU.add))
            then(v.tensor_tensor(y_slot_f[:, :], y_slot_f[:, :],
                                 all_slot[:, :, :].rearrange("p b n -> p (b n)"), ALU.add))
            then(v.tensor_copy(y_slot[:, :], y_slot_f[:, :]))
            with dve.Fori(0, (TILES - 4) // 2) as i:
                expert_step(Item(i, 2))
                expert_step(Item(i, 3))
            expert_step(Item(0, TILES - 2))
            expert_step(Item(0, TILES - 1), ahead1=False)

            def place_rows(n, k):
                v.tensor_copy(y_at[:, k, :], y_slot[:, bass.ds(n * TOPK, TOPK)]).then_inc(y_at_made.sem, 1)

            weights = all_w[:, :, :].rearrange("p b n -> p (b n)")

            def combine(lap, k, more=True):
                n = lap * 4 + k
                dve.wait_ge(y_got[k].sem, y_got[k].upto(lap))
                v.scalar_tensor_tensor(y_in[:, k, 0, :], y_in[:, k, 0, :], weights[:, bass.ds(n * TOPK, 1)],
                                       base_out[:, bass.ds(n, 1), :].rearrange("p a d -> p (a d)"),
                                       ALU.mult, ALU.add).then_inc(fin_step.sem, 1)
                dve.wait_ge(fin_step.sem, fin_step.upto(n))
                dve.wait_ge(out_stored[k].sem, out_stored[k].upto(lap - 1))
                v.scalar_tensor_tensor(fin[:, k, :], y_in[:, k, 1, :], weights[:, bass.ds(n * TOPK + 1, 1)],
                                       y_in[:, k, 0, :], ALU.mult, ALU.add).then_inc(fin_made.sem, 1)
                if more:
                    place_rows(n + 4, k)

            dve.wait_ge(table_step.sem, table_step.upto(steps[0] - 1))
            for k in range(4):
                place_rows(k, k)
            for k in range(4):
                combine(0, k)
            with dve.Fori(1, NT // 4 - 1) as i:
                for k in range(4):
                    combine(i, k)
            for k in range(4):
                combine(NT // 4 - 1, k, more=False)


POOL_CONSTS = 23
TABLE_STEPS = 18


_INS = ['x', 'ctx_1024', 'g_xattn', 'g_ffn', 'L0_xattn_igate_w', 'L0_xattn_igate_b', 'L0_xattn_fgate_w',
        'L0_xattn_fgate_b', 'L0_xattn_ln_scale', 'L0_ffn_router_w', 'L0_ffn_expert_gate', 'L0_ffn_expert_up',
        'L0_ffn_expert_down', 'L0_ffn_shared_gate', 'L0_ffn_shared_up', 'L0_ffn_shared_down']
_OUTS = [((B, S, D), 'float32')]


def kernel(**inputs):
    import numpy as _np
    import concourse.bacc as _bacc
    from concourse import mybir as _mybir
    from concourse.bass_utils import run_bass_kernel_spmd as _run

    nc = _bacc.Bacc("TRN2", target_bir_lowering=False, num_devices=1)
    arrays, args = {}, []
    for name in _INS:
        a = _np.ascontiguousarray(inputs[name])
        arrays[f"in_{name}_dram"] = a
        args.append(nc.dram_tensor(f"in_{name}_dram", a.shape, _mybir.dt.from_np(a.dtype), kind="ExternalInput").ap())
    for i, (shape, dtype) in enumerate(_OUTS):
        dt = _mybir.dt.from_np(_np.dtype(dtype))
        args.append(nc.dram_tensor(f"out_{i}_dram", shape, dt, kind="ExternalOutput").ap())
    flamingo_kernel(nc, *args)
    r = _run(nc, [arrays], core_ids=[0])
    got = tuple(r.results[0][f"out_{i}_dram"] for i in range(len(_OUTS)))
    return got[0]
```

```python
from contextlib import ExitStack

import concourse.bass as bass
from concourse import mybir

F32 = mybir.dt.float32
BF16 = mybir.dt.bfloat16
I32 = mybir.dt.int32
U32 = mybir.dt.uint32
ALU = mybir.AluOpType
ACT = mybir.ActivationFunctionType
AX_X = mybir.AxisListType.X

P = 128
B, S, D = 16, 256, 512
NH, DH = 8, 64
E, I = 16, 256
IS = 512
FG = 32
TOPK = 2
T = B * S
ST = S // P
NT = T // P
DC = D // P
IC = I // P
SC = IS // P
LN_EPS = 1e-5
NORM_EPS = 1e-6
QK_SCALE = DH ** -0.5
MASK = 1e30
CAP = T + P
DUMP = E * CAP
TILES = (T * TOPK + E * (P - 1)) // P
TILES += TILES % 2
RING = 4
XRING = 4
TRI = S + P
VW = DH + 1


class Event:

    def __init__(self, sem, per=1, start=0):
        self.sem, self.per, self.start = sem, per, start

    def upto(self, n, k=None):
        value = n * self.per + (self.per if k is None else k)
        if isinstance(value, int) and value <= 0:
            return 0
        return value + self.start


class Item:

    def __init__(self, i, offset):
        self.i, self.offset = i, offset
        self.n = i * 2 + offset
        self.half = i + offset // 2
        self.par = offset % 2

    def __add__(self, k):
        return Item(self.i, self.offset + k)


def flamingo_kernel(nc, x, ctx_in, g_xattn, g_ffn, igate_w, igate_b, fgate_w, fgate_b, ln_scale,
                    router_w, expert_gate, expert_up, expert_down, shared_gate, shared_up,
                    shared_down, out):
    x_tok = x.rearrange("b (j p) d -> b p j d", p=P)
    c_tok = ctx_in.rearrange("b (j p) d -> b p j d", p=P)
    out_tok = out.rearrange("b s d -> (b s) d")
    routed_x = nc.dram_tensor("routed_x", (DUMP + P, D), F32).ap()
    routed_y = nc.dram_tensor("routed_y", (TILES * P, D), F32).ap()

    with ExitStack() as stack:
        def sb(name, shape, dt=F32):
            return stack.enter_context(nc.sbuf_tensor(name, shape, dt))

        def event(name, per=1, start=0):
            return Event(stack.enter_context(nc.semaphore(name)), per, start)

        bank = [stack.enter_context(nc.psum_tensor(f"bank{n}", [P, 512], F32)) for n in range(8)]
        TP, SM, MB, QK, HO, FF = bank[0], bank[1], bank[2:4], bank[4:6], bank[6], bank[7]
        row_columns = SM[:, 0:ST * (FG + NH)].rearrange("p (j n) -> p j n", j=ST)

        ident = sb("ident", [P, P])
        identb = sb("identb", [P, P], BF16)
        one = sb("one", [P, 1])
        before_b = sb("before_b", [P, P], BF16)
        ones_b = sb("ones_b", [P, P], BF16)
        mask_b = sb("mask_b", [P, P], BF16)
        head_sel = sb("head_sel", [P, NH, P], BF16)
        expert_no = sb("expert_no", [P, E])
        expert_row = sb("expert_row", [P, E])
        part_no = sb("part_no", [P, 1])
        minus_half = sb("minus_half", [P, ST])
        gate_wT = sb("gate_wT", [P, 2 * DC, FG + NH])
        router_wT = sb("router_wT", [P, DC, E])
        gate_bias = sb("gate_bias", [P, 1])
        ln_row = sb("ln_row", [P, D])
        g_col = sb("g_col", [P, 2])
        tanh_g = sb("tanh_g", [P, 2])
        EW = DC * 2 * I + IC * D
        w_ring = sb("w_ring", [P, RING, EW])
        w_gu = w_ring[:, :, 0:DC * 2 * I].rearrange("p r (c i) -> p r c i", c=DC)
        w_dn = w_ring[:, :, DC * 2 * I:EW].rearrange("p r (c d) -> p r c d", c=IC)
        sh_w = w_ring[:, 2:4, :].rearrange("p r n -> p (r n)").rearrange("p (w c i) -> p w c i", w=3, c=DC)
        sh_gate, sh_up, sh_down = (sh_w[:, k] for k in range(3))
        last_w = w_ring[:, 0:2, :].rearrange("p r n -> p (r n)")

        xt = sb("xt", [P, XRING, D])
        cs_in = sb("cs_in", [P, 2, ST, D])
        v_aug = sb("v_aug", [P, 2, ST, NH, VW])
        xn = sb("xn", [P, ST, D])
        xnT = sb("xnT", [P, 2, DC, S])
        ctxT = sb("ctxT", [P, 2, DC, S])
        ln_stat = sb("ln_stat", [P, ST, 6])
        ln_mv = sb("ln_mv", [P, ST, 2])
        ln_var = sb("ln_var", [P, ST])
        ln_rstd = sb("ln_rstd", [P, ST])
        gates = sb("gates", [FG + NH, S])
        f_row = sb("f_row", [FG + NH, S])
        cum_row = sb("cum_row", [NH, S])
        key_max = sb("key_max", [FG + NH, S])
        key_log = sb("key_log", [P, 2, ST, NH])
        max_row = sb("max_row", [NH, S])
        max_mid = sb("max_mid", [NH, S], BF16)
        max_rest = sb("max_rest", [NH, S])
        max_parts = sb("max_parts", [P, 2, S], BF16)
        max_log = sb("max_log", [P, ST, NH])
        norm_floor = sb("norm_floor", [P, 2, ST, NH])
        decay = sb("decay", [P, 2, TRI])
        cmat = sb("cmat", [P, 2, TRI])
        norm = sb("norm", [P, 2, ST])
        norm_abs = sb("norm_abs", [P, 2, ST])
        norm_e = sb("norm_e", [P, 2, ST])
        norm_inv = sb("norm_inv", [P, 2, ST])
        heads = sb("heads", [P, ST, D])
        h_stat = sb("h_stat", [P, ST, 6])
        h_mv = sb("h_mv", [P, ST, 2])
        h_var = sb("h_var", [P, ST])
        h_rstd = sb("h_rstd", [P, ST])
        x2_stat = sb("x2_stat", [P, ST, 6])
        x2_mv = sb("x2_mv", [P, ST, 2])
        x2_var = sb("x2_var", [P, ST])
        x2_rstd = sb("x2_rstd", [P, ST])
        x2n = sb("x2n", [P, 2, ST, D])
        rows = x2n[0:E].rearrange("p a j d -> p (a j) d")
        gate_rows, router_rows = rows[:, 0:3, :].rearrange("p a d -> p (a d)"), rows[:, 3, :]
        x2nT = sb("x2nT", [P, DC, S])
        logits = sb("logits", [P, ST, E])
        top8 = sb("top8", [P, ST, 8])
        top8_at = sb("top8_at", [P, ST, 8], U32)
        top_at = sb("top_at", [P, ST, TOPK])
        one_hot = sb("one_hot", [P, ST, TOPK, E])
        gap = sb("gap", [P, ST])
        gap_exp = sb("gap_exp", [P, ST])
        gap_den = sb("gap_den", [P, ST])
        gap_inv = sb("gap_inv", [P, ST])
        top_w = sb("top_w", [P, ST, TOPK])
        chosen = sb("chosen", [P, ST, E], BF16)
        taken = sb("taken", [P, 2, E], BF16)
        taken_mid = sb("taken_mid", [P, E], BF16)
        place = sb("place", [P, ST, E])
        place_pick = sb("place_pick", [P, ST * TOPK, E])
        slot_f = sb("slot_f", [P, ST * TOPK])
        slot_u = sb("slot_u", [P, 2, ST * TOPK], U32)
        silu_t = sb("silu_t", [P, S])
        silu_g = sb("silu_g", [P, S])
        sh_actT = sb("sh_actT", [P, SC, S])
        base_out = sb("base_out", [P, NT, D])
        all_hot = sb("all_hot", [P, B, ST * TOPK, E], BF16)
        all_slot = sb("all_slot", [P, B, ST * TOPK])
        all_w = sb("all_w", [P, B, ST * TOPK])

        count = sb("count", [P, E])
        count_i = sb("count_i", [P, E], I32)
        tiles_i = sb("tiles_i", [P, E], I32)
        tiles_f = sb("tiles_f", [P, E])
        tile_end = sb("tile_end", [P, E])
        tile_first = sb("tile_first", [P, E])
        ended = sb("ended", [P, E])
        ended_at = sb("ended_at", [P, E])
        tile_info = sb("tile_info", [P, 4])
        pad_f = sb("pad_f", [P, E])
        pad_tab = sb("pad_tab", [1, E], I32)
        shift = sb("shift", [P, E])
        y_slot_f = sb("y_slot_f", [P, B * ST * TOPK])
        y_slot = sb("y_slot", [P, B * ST * TOPK], U32)
        first_tab = sb("first_tab", [1, E], I32)
        row_tab = sb("row_tab", [1, P], I32)
        expert_tab = sb("expert_tab", [1, P], I32)
        xtT = xnT[:, :, 0:2, :].rearrange("p a c s -> p a (c s)")
        act_t, act_g, act_a, act_aT = (ctxT[:, :, k, :] for k in range(4))
        y_out = cs_in[:, 0]
        hot_shift = cs_in[:, 1].rearrange("p j (n e) -> p (j n) e", e=E)
        zeros = xn[:, 0, :]

        y_at = sb("y_at", [P, 4, TOPK], U32)
        y_in = last_w[:, 0:4 * TOPK * D].rearrange("p (n k d) -> p n k d", n=4, k=TOPK)
        fin = last_w[:, 4 * TOPK * D:4 * (TOPK + 1) * D].rearrange("p (n d) -> p n d", n=4)

        small_in = event("small_in", 16)
        weights_in = event("weights_in", 16)
        pool_const = event("pool_const")
        stood = event("stood")
        act_const = event("act_const")
        wT_made = event("wT_made")
        wT_copied = event("wT_copied")
        x_in = [event(f"x_in{k}", 16) for k in range(2)]
        c_in = [event(f"c_in{k}", 16) for k in range(2)]
        v_made = event("v_made")
        ln_step = event("ln_step", 2 * ST)
        ln_var_made = event("ln_var_made")
        ln_rstd_made = event("ln_rstd_made")
        h_var_made = event("h_var_made")
        h_rstd_made = event("h_rstd_made")
        x2_var_made = event("x2_var_made")
        x2_rstd_made = event("x2_rstd_made")
        xn_made = event("xn_made", ST)
        ctx_turned = event("ctx_turned", ST)
        ctxT_made = event("ctxT_made", ST)
        xn_turned = event("xn_turned", ST)
        xnT_made = event("xnT_made", ST)
        gates_made = event("gates_made")
        gates_read = event("gates_read", 2)
        f_abs_made = event("f_abs_made")
        f_exp_made = event("f_exp_made")
        f_ln_made = event("f_ln_made")
        key_made = event("key_made", 2)
        row_step = event("row_step", 10)
        columns_turned = event("columns_turned")
        floor_made = event("floor_made")
        qk_made = event("qk_made", NH)
        max_spread = event("max_spread", NH)
        decay_made = event("decay_made", NH)
        c_made = event("c_made", NH)
        pv_made = event("pv_made", NH)
        norm_step = event("norm_step", 4 * NH // 2)
        heads_made = event("heads_made", NH // 2)
        post_step = event("post_step", 5 * ST)
        x2_made = event("x2_made", ST)
        x2n_made = event("x2n_made", ST)
        x2_turned = event("x2_turned", ST)
        x2nT_made = event("x2nT_made", ST)
        router_made = event("router_made")
        logits_made = event("logits_made")
        top_step = event("top_step", 2 * ST + 1)
        gap_made = event("gap_made")
        gap_exp_made = event("gap_exp_made")
        hot_made = event("hot_made", 2 * ST)
        w_step = event("w_step", 3)
        route_kept = event("route_kept", 3)
        chosen_made = event("chosen_made", 3)
        ranks_made = event("ranks_made")
        place_step = event("place_step", 3)
        slots_made = event("slots_made")
        scattered = [event(f"scattered{k}", 16 * ST * TOPK) for k in range(2)]
        sh_made = event("sh_made", SC)
        sh_tanh_made = event("sh_tanh_made", SC)
        sh_silu_made = event("sh_silu_made", SC)
        sh_act_made = event("sh_act_made", SC)
        sh_down_made = event("sh_down_made", ST)
        base_made = event("base_made", ST)

        counts_made = event("counts_made")
        table_step = event("table_step")
        tables_turned = event("tables_turned")
        tables_made = event("tables_made")
        pads_made = event("pads_made")
        padded = event("padded", 16)
        y_slots_made = event("y_slots_made")
        expert_dma = event("expert_dma", 48)
        expert_in = event("expert_in")
        xt_in = [event(f"xt_in{k}", 16) for k in range(XRING)]
        xt_turned = event("xt_turned")
        xtT_made = event("xtT_made")
        gu_made = event("gu_made")
        act_tanh_made = event("act_tanh_made")
        act_silu_made = event("act_silu_made")
        act_made = event("act_made")
        act_turned = event("act_turned")
        actT_made = event("actT_made")
        y_made = event("y_made", start=1)
        y_copied = event("y_copied")
        y_stored = [event(f"y_stored{k}", 16) for k in range(2)]

        y_at_made = event("y_at_made")
        y_got = [event(f"y_got{k}", 16 * TOPK) for k in range(4)]
        fin_step = event("fin_step")
        fin_made = event("fin_made")
        out_stored = [event(f"out_stored{k}", 16) for k in range(4)]

        N_SMALL = 8
        N_SHARED = 3


        def apart(eng):
            eng.sem_inc(stood.sem, 1)

        block = stack.enter_context(nc.Block())

        @block.sync
        def _(sp):
            def load_x(b):
                sp.dma_start(base_out[:, bass.ds(b.n * ST, ST), :],
                             x_tok[bass.ds(b.n, 1)].rearrange("a p j d -> (a p) j d")).then_inc(x_in[b.par].sem, 16)

            def load_ctx(b):
                sp.dma_start(cs_in[:, b.par, :, :], c_tok[bass.ds(b.n, 1)].rearrange("a p j d -> (a p) j d")
                             ).then_inc(c_in[b.par].sem, 16)

            for n in range(2):
                load_x(Item(0, n))
                load_ctx(Item(0, n))
            with sp.Fori(0, (B - 2) // 2) as i:
                for u in range(2):
                    b = Item(i, 2 + u)
                    sp.wait_ge(ctxT_made.sem, ctxT_made.upto(b.n - 2))
                    apart(sp)
                    sp.wait_ge(v_made.sem, v_made.upto(b.n - 2))
                    apart(sp)
                    load_ctx(b)
                    sp.wait_ge(x_in[b.par].sem, x_in[b.par].upto(b.half - 1))
                    apart(sp)
                    load_x(b)

            def load_tile(n, k):
                row = sp.value_load(row_tab[0:1, bass.ds(n, 1)], min_val=0, max_val=DUMP)
                sp.dma_start(xt[:, k, :], routed_x[bass.ds(row, P), :]).then_inc(xt_in[k].sem, 16)

            sp.wait_ge(pads_made.sem, pads_made.upto(0))
            with sp.Fori(0, E) as e:
                row = sp.value_load(pad_tab[0:1, bass.ds(e, 1)], min_val=0, max_val=DUMP - P)
                sp.dma_start(routed_x[bass.ds(row, P), :], zeros[:, :]).then_inc(padded.sem, 16)
            sp.dma_start(routed_x[DUMP:DUMP + P, :], zeros[:, :]).then_inc(padded.sem, 16)

            sp.wait_ge(tables_made.sem, tables_made.upto(0))
            for par in range(2):
                sp.wait_ge(scattered[par].sem, scattered[par].upto(B // 2 - 1))
            sp.wait_ge(padded.sem, padded.upto(E))
            for n in range(XRING - 1):
                load_tile(n, n)

            def store_tile(t, par):
                sp.wait_ge(y_copied.sem, y_copied.upto(t))
                apart(sp)
                sp.dma_start(routed_y[bass.ds(t * P, P), :], y_out[:, par, :]).then_inc(y_stored[par].sem, 16)

            def turn(n, k, ahead=True):
                if ahead:
                    sp.wait_ge(xt_turned.sem, xt_turned.upto(n - 1))
                    apart(sp)
                    load_tile(n + XRING - 1, (k + XRING - 1) % XRING)
                store_tile(n, k % 2)

            turn(0, 0)
            turn(1, 1)
            turn(2, 2)
            turn(3, 3)
            with sp.Fori(0, (TILES - 2 * XRING) // XRING) as i:
                for k in range(XRING):
                    turn(i * XRING + XRING + k, k)
            for n in range(TILES - XRING, TILES):
                turn(n, n % XRING, n + XRING - 1 < TILES)

            with sp.Fori(0, NT // 4) as i:
                for k in range(4):
                    n = i * 4 + k
                    sp.wait_ge(fin_made.sem, fin_made.upto(n))
                    sp.dma_start(out_tok[bass.ds(n * P, P), :], fin[:, k, :]).then_inc(out_stored[k].sem, 16)
            for k in range(4):
                sp.wait_ge(out_stored[k].sem, out_stored[k].upto(NT // 4 - 1))

        @block.gpsimd
        def _(pool):
            g = nc.gpsimd
            made = [0]

            def const(ins):
                made[0] += 1
                ins.then_inc(pool_const.sem, 1)

            def settle():
                pool.wait_ge(pool_const.sem, made[0])

            def select(ap, fill, op, base, p_step, pattern):
                settle()
                const(g.affine_select(out=ap, in_=ap, compare_op=op, fill=fill, base=base,
                                      pattern=pattern, channel_multiplier=p_step))

            const(g.memset(ident[:], 0.0))
            const(g.memset(identb[:], 0.0))
            const(g.memset(one[:], 1.0))
            const(g.memset(gate_wT[:], 0.0))
            const(g.memset(key_max[:], 0.0))
            const(g.memset(before_b[:], 1.0))
            const(g.memset(ones_b[:], 1.0))
            const(g.memset(mask_b[:], 0.0))
            const(g.memset(head_sel[:], 0.0))
            const(g.memset(v_aug[:], 1.0))
            const(g.memset(taken[:], 0.0))
            const(g.memset(minus_half[:], -0.5))
            const(g.memset(max_parts[:], 0.0))
            select(ident[:], 1.0, ALU.not_equal, 0, 1, [[-1, P]])
            select(identb[:], 1.0, ALU.not_equal, 0, 1, [[-1, P]])
            select(before_b[:], 0.0, ALU.is_gt, 0, -1, [[1, P]])
            select(mask_b[:], MASK, ALU.is_ge, 0, -1, [[1, P]])
            for part in range(3):
                select(head_sel[:], 1.0, ALU.not_equal, -32 * part, 1, [[-1, NH], [0, P]])
            const(g.iota(expert_no[:], pattern=[[1, E]], base=0, channel_multiplier=0,
                         allow_small_or_imprecise_dtypes=True))
            const(g.iota(expert_row[:], pattern=[[CAP, E]], base=0, channel_multiplier=0,
                         allow_small_or_imprecise_dtypes=True))
            const(g.iota(part_no[:], pattern=[[0, 1]], base=0, channel_multiplier=1,
                         allow_small_or_imprecise_dtypes=True))
            assert made[0] == POOL_CONSTS
            settle()

            def load_expert(e, k):
                sides = (
                    (w_gu[:, k, :, 0:I], expert_gate, DC), (w_gu[:, k, :, I:2 * I], expert_up, DC),
                    (w_dn[:, k, :, :], expert_down, IC),
                )
                for to, of, c in sides:
                    src = of[bass.ds(e, 1)].rearrange("a (c p) i -> (a p) c i", p=P)
                    pool.dma_start(to, src).then_inc(expert_dma.sem, 16)

            for e in range(RING - 2):
                load_expert(e, e)

            def values(b):
                pool.wait_ge(c_in[b.par].sem, c_in[b.par].upto(b.half))
                pool.wait_ge(pv_made.sem, pv_made.upto(b.n - 2))
                apart(pool)
                g.tensor_copy(v_aug[:, b.par, :, :, 0:DH],
                              cs_in[:, b.par, :, :].rearrange("p j (h d) -> p j h d", h=NH)
                              ).then_inc(v_made.sem, 1)

            def scatter(b):
                pool.wait_ge(slots_made.sem, slots_made.upto(b.n))
                apart(pool)
                for j in range(ST):
                    for k in range(TOPK):
                        c = j * TOPK + k
                        pool.indirect_dma_start(
                            out=routed_x, in_=x2n[:, b.par, j, :], in_offset=None,
                            out_offset=bass.IndirectOffsetOnAxis(ap=slot_u[:, b.par, c:c + 1], axis=0),
                        ).then_inc(scattered[b.par].sem, 16)

            def rstd(b, made, var, to, told):
                pool.wait_ge(made.sem, made.upto(b.n))
                g.tensor_tensor(to[:, :], var[:, :], minus_half[:, :], ALU.pow).then_inc(told.sem, 1)

            def stats(b):
                rstd(b, ln_var_made, ln_var, ln_rstd, ln_rstd_made)

            def h_stats(b):
                rstd(b, h_var_made, h_var, h_rstd, h_rstd_made)

            def x2_stats(b):
                rstd(b, x2_var_made, x2_var, x2_rstd, x2_rstd_made)

            def step(t, front=True, attend=True, route=True, rest=True):
                F, A, G, H = t + 1, t, t + -1, t + -2
                if front:
                    stats(F)
                    values(F)
                if route:
                    x2_stats(G)
                if rest and route:
                    scatter(H)
                if route and not attend:
                    scatter(G)
                if attend:
                    h_stats(A)

            step(Item(0, -1), attend=False, route=False, rest=False)
            step(Item(0, 0), route=False, rest=False)
            step(Item(0, 1), rest=False)
            step(Item(0, 2))
            with pool.Fori(0, (B - 4) // 2) as i:
                step(Item(i, 3))
                step(Item(i, 4))
            step(Item(0, B - 1), front=False)
            step(Item(0, B), front=False, attend=False)
            step(Item(0, B + 1), front=False, attend=False, route=False)

            pool.wait_ge(expert_dma.sem, expert_dma.upto(RING - 3))
            pool.sem_inc(expert_in.sem, RING - 2)
            pool.wait_ge(sh_down_made.sem, sh_down_made.upto(B - 1))
            for e in range(RING - 2, RING):
                load_expert(e, e)
            pool.wait_ge(expert_dma.sem, expert_dma.upto(RING - 1))
            pool.sem_inc(expert_in.sem, 2)
            pool.wait_ge(tables_made.sem, tables_made.upto(0))
            with pool.Fori(0, (E - RING) // RING) as i:
                for k in range(RING):
                    e = i * RING + RING + k
                    used = pool.value_load(first_tab[0:1, bass.ds(e - (RING - 1), 1)],
                                           min_val=0, max_val=TILES)
                    pool.wait_ge(y_made.sem, used + y_made.start)
                    load_expert(e, k)
                    pool.wait_ge(expert_dma.sem, expert_dma.upto(e))
                    pool.sem_inc(expert_in.sem, 1)

            for par in range(2):
                pool.wait_ge(y_stored[par].sem, y_stored[par].upto(TILES // 2 - 1))

            def gather(n, k):
                pool.wait_ge(y_at_made.sem, y_at_made.upto(n))
                apart(pool)
                for c in range(TOPK):
                    pool.indirect_dma_start(
                        out=y_in[:, k, c, :], in_=routed_y, out_offset=None,
                        in_offset=bass.IndirectOffsetOnAxis(ap=y_at[:, k, c:c + 1], axis=0),
                    ).then_inc(y_got[k].sem, 16)

            for k in range(4):
                gather(k, k)
            with pool.Fori(1, NT // 4) as i:
                for k in range(4):
                    pool.wait_ge(fin_made.sem, fin_made.upto(i * 4 + k - 4))
                    gather(i * 4 + k, k)

        @block.scalar
        def _(act):
            s = nc.scalar
            small = [
                (gate_rows[0:NH, :], igate_w), (gate_rows[NH:2 * NH, :], fgate_w),
                (router_rows[:, :], router_w),
                (gate_bias[0:NH, :], igate_b.rearrange("(n o) -> n o", o=1)),
                (gate_bias[FG:FG + NH, :], fgate_b.rearrange("(n o) -> n o", o=1)),
                (ln_row[:, :], ln_scale.partition_broadcast(P)),
                (g_col[:, 0:1], g_xattn.partition_broadcast(P)),
                (g_col[:, 1:2], g_ffn.partition_broadcast(P)),
            ]
            assert len(small) == N_SMALL
            for to, of in small:
                act.dma_start(to, of).then_inc(small_in.sem, 16)
            for to, of in ((sh_gate, shared_gate), (sh_up, shared_up), (sh_down, shared_down)):
                act.dma_start(to, of.rearrange("(c p) i -> p c i", p=P)).then_inc(weights_in.sem, 16)
            act.wait_ge(small_in.sem, small_in.upto(N_SMALL - 1))
            s.activation(tanh_g[:, :], g_col[:, :], ACT.Tanh).then_inc(act_const.sem, 1)

            def turn_out(j, to):
                return s.copy(to[:, :, j * P:(j + 1) * P], TP[:, :].rearrange("p (c t) -> p c t", c=DC))

            def turn_ctx(b, j):
                act.wait_ge(ctx_turned.sem, ctx_turned.upto(b.n, j + 1))
                act.wait_ge(qk_made.sem, qk_made.upto(b.n - 2))
                turn_out(j, ctxT[:, b.par]).then_inc(ctxT_made.sem, 1)

            def turn_x(b, j):
                act.wait_ge(xn_turned.sem, xn_turned.upto(b.n, j + 1))
                turn_out(j, xnT[:, b.par]).then_inc(xnT_made.sem, 1)

            def turn(b, j):
                act.wait_ge(x2_turned.sem, x2_turned.upto(b.n, j + 1))
                act.wait_ge(sh_made.sem, sh_made.upto(b.n - 1))
                turn_out(j, x2nT[:]).then_inc(x2nT_made.sem, 1)

            def log_gates(b):
                act.wait_ge(f_abs_made.sem, f_abs_made.upto(b.n))
                s.activation(f_row[FG:, :], f_row[FG:, :], ACT.Exp, scale=-1.0).then_inc(f_exp_made.sem, 1)
                act.wait_ge(f_exp_made.sem, f_exp_made.upto(b.n))
                s.activation(f_row[FG:, :], f_row[FG:, :], ACT.Ln, bias=1.0).then_inc(f_ln_made.sem, 1)

            def columns(b):
                act.wait_ge(key_made.sem, key_made.upto(b.n))
                act.wait_ge(heads_made.sem, heads_made.upto(b.n - 2))
                s.activation(norm_floor[:, b.par], max_log[:, :, :], ACT.Exp, scale=-1.0
                             ).then_inc(floor_made.sem, 1)

            def head(b, h):
                act.wait_ge(key_made.sem, key_made.upto(b.n))
                act.wait_ge(max_spread.sem, max_spread.upto(b.n, h + 1))
                act.wait_ge(c_made.sem, c_made.upto(b.n, h - 1))
                k = h % 2
                s.activation(decay[:, k, 0:S], MB[k][:, 0:S], ACT.Exp,
                             bias=key_log[:, b.par, 0, h:h + 1], scale=-1.0)
                s.activation(decay[:, k, S:TRI], MB[k][:, S:TRI], ACT.Exp,
                             bias=key_log[:, b.par, 1, h:h + 1], scale=-1.0).then_inc(decay_made.sem, 1)

            def top(b):
                act.wait_ge(gap_made.sem, gap_made.upto(b.n))
                s.activation(gap_exp[:, :], gap[:, :], ACT.Exp).then_inc(gap_exp_made.sem, 1)

            def shared(b, m):
                act.wait_ge(sh_made.sem, sh_made.upto(b.n, m + 1))
                act.wait_ge(sh_silu_made.sem, sh_silu_made.upto(b.n, m))
                s.activation(silu_t[:, :], FF[:, 0:S], ACT.Tanh, scale=0.5).then_inc(sh_tanh_made.sem, 1)

            def step(t, front=True, attend=True, route=True, rest=True):
                F, A, G, H = t + 1, t, t + -1, t + -2
                if attend:
                    head(A, 0)
                if rest:
                    shared(H, 2)
                if attend:
                    head(A, 1)
                if front:
                    turn_ctx(F, 0)
                if rest:
                    shared(H, 3)
                if attend:
                    head(A, 2)
                if front:
                    turn_ctx(F, 1)
                if attend:
                    head(A, 3)
                if front:
                    turn_x(F, 0)
                if attend:
                    head(A, 4)
                if front:
                    turn_x(F, 1)
                if rest and route:
                    top(H)
                if attend:
                    head(A, 5)
                if route:
                    turn(G, 0)
                if attend:
                    head(A, 6)
                if route:
                    turn(G, 1)
                if front:
                    log_gates(F)
                if route and not attend:
                    top(G)
                if route:
                    shared(G, 0)
                if attend:
                    head(A, 7)
                if route:
                    shared(G, 1)
                if front:
                    columns(F)

            step(Item(0, -1), attend=False, route=False, rest=False)
            step(Item(0, 0), route=False, rest=False)
            step(Item(0, 1), rest=False)
            step(Item(0, 2))
            with act.Fori(0, (B - 4) // 2) as i:
                step(Item(i, 3))
                step(Item(i, 4))
            step(Item(0, B - 1), front=False)
            step(Item(0, B), front=False, attend=False)
            step(Item(0, B + 1), front=False, attend=False, route=False)

            def copy_x(t):
                act.wait_ge(xt_turned.sem, xt_turned.upto(t.n))
                s.copy(xtT[:, t.par, :], bank[t.par][:, :]).then_inc(xtT_made.sem, 1)

            def tanh_gate(t):
                act.wait_ge(gu_made.sem, gu_made.upto(t.n))
                s.activation(act_t[:, t.par, :], bank[2 + t.par][:, 0:I], ACT.Tanh, scale=0.5
                             ).then_inc(act_tanh_made.sem, 1)

            def copy_y(t):
                act.wait_ge(y_made.sem, y_made.upto(t.n))
                act.wait_ge(y_stored[t.par].sem, y_stored[t.par].upto(t.half - 1))
                s.copy(y_out[:, t.par, :], bank[5 + t.par][:, :]).then_inc(y_copied.sem, 1)

            def expert_step(t, ahead2=True, ahead1=True):
                if ahead2:
                    copy_x(t + 2)
                if ahead1:
                    tanh_gate(t + 1)
                copy_y(t)

            copy_x(Item(0, 0))
            copy_x(Item(0, 1))
            tanh_gate(Item(0, 0))
            expert_step(Item(0, 0))
            expert_step(Item(0, 1))
            with act.Fori(0, (TILES - 4) // 2) as i:
                expert_step(Item(i, 2))
                expert_step(Item(i, 3))
            expert_step(Item(0, TILES - 2), ahead2=False)
            expert_step(Item(0, TILES - 1), ahead2=False, ahead1=False)

        @block.tensor
        def _(pe):
            mm, tr = nc.tensor.matmul, nc.tensor.transpose

            pe.wait_ge(pool_const.sem, POOL_CONSTS)
            pe.wait_ge(small_in.sem, small_in.upto(N_SMALL - 1))
            for c in range(3 * DC):
                tr(SM[:, c * 16:(c + 1) * 16], gate_rows[:, c * P:(c + 1) * P], ident[0:2 * NH, 0:2 * NH])
            for c in range(DC):
                last = tr(SM[:, (3 * DC + c) * 16:(3 * DC + c + 1) * 16],
                          router_rows[:, c * P:(c + 1) * P], ident[0:E, 0:E])
            last.then_inc(wT_made.sem, 1)
            pe.wait_ge(wT_copied.sem, 5)

            def turn_tile(src):
                for c in range(DC):
                    last = tr(TP[:, c * P:(c + 1) * P], src[:, c * P:(c + 1) * P], ident[:, :])
                return last

            def turn(b, j, front):
                pe.wait_ge(x2n_made.sem, x2n_made.upto(b.n, j + 1))
                pe.wait_ge(x2nT_made.sem, x2nT_made.upto(b.n, j))
                if front:
                    pe.wait_ge(xnT_made.sem, xnT_made.upto(b.n + 2))
                else:
                    pe.wait_ge(xnT_made.sem, xnT_made.upto(B - 1))
                turn_tile(x2n[:, b.par, j, :]).then_inc(x2_turned.sem, 1)

            def turn_ctx(b, j):
                pe.wait_ge(c_in[b.par].sem, c_in[b.par].upto(b.half))
                pe.wait_ge(ctxT_made.sem, ctxT_made.upto(b.n, j))
                pe.wait_ge(xnT_made.sem, xnT_made.upto(b.n - 1))
                pe.wait_ge(x2nT_made.sem, x2nT_made.upto(b.n - 3))
                turn_tile(cs_in[:, b.par, j, :]).then_inc(ctx_turned.sem, 1)

            def turn_x(b, j):
                pe.wait_ge(xn_made.sem, xn_made.upto(b.n, j + 1))
                pe.wait_ge(ctxT_made.sem, ctxT_made.upto(b.n))
                pe.wait_ge(xnT_made.sem, xnT_made.upto(b.n, j))
                turn_tile(xn[:, j, :]).then_inc(xn_turned.sem, 1)

            def gates_pe(b):
                pe.wait_ge(xnT_made.sem, xnT_made.upto(b.n))
                pe.wait_ge(ctxT_made.sem, ctxT_made.upto(b.n))
                pe.wait_ge(key_made.sem, key_made.upto(b.n - 1))
                for c in range(2 * DC):
                    src = (xnT if c < DC else ctxT)[:, b.par, c % DC, :]
                    last = mm(SM[0:FG + NH, 0:S], gate_wT[:, c, :], src, start=(c == 0), stop=(c == 2 * DC - 1))
                last.then_inc(gates_made.sem, 1)

            def columns(b, route):
                pe.wait_ge(row_step.sem, row_step.upto(b.n, 5))
                if route:
                    pe.wait_ge(logits_made.sem, logits_made.upto(b.n - 2))
                else:
                    pe.wait_ge(gates_read.sem, gates_read.upto(b.n))
                apart(pe)
                for j in range(ST):
                    last = tr(row_columns[:, j, :], key_max[:, j * P:(j + 1) * P], ident[0:FG + NH, 0:FG + NH])
                last.then_inc(columns_turned.sem, 1)

            def head(b, h):
                k = h % 2
                rows = slice(DH * (h % 2), DH * (h % 2) + DH)
                c = h // 2
                pe.wait_ge(xnT_made.sem, xnT_made.upto(b.n))
                pe.wait_ge(ctxT_made.sem, ctxT_made.upto(b.n))
                pe.wait_ge(row_step.sem, row_step.upto(b.n))
                pe.wait_ge(c_made.sem, c_made.upto(b.n, h - 1))
                pe.wait_ge(decay_made.sem, decay_made.upto(b.n, h - 1))
                mm(QK[k][:, 0:S], ctxT[rows, b.par, c, 0:P], xnT[rows, b.par, c, 0:S],
                   start=True, stop=True)
                mm(QK[k][:, S:TRI], ctxT[rows, b.par, c, P:S], xnT[rows, b.par, c, P:S],
                   start=True, stop=True).then_inc(qk_made.sem, 1)
                for at, n in ((0, S), (S, P)):
                    mm(MB[k][:, at:at + n], head_sel[0:96, h, :], max_parts[0:96, b.par, S - n:S],
                       start=True, stop=False)
                    last = mm(MB[k][:, at:at + P], identb[:, :], mask_b[:, :], start=False, stop=True)
                last.then_inc(max_spread.sem, 1)

            def pv(b, h):
                k = h % 2
                pe.wait_ge(c_made.sem, c_made.upto(b.n, h + 1))
                pe.wait_ge(v_made.sem, v_made.upto(b.n))
                if h % 2 == 0:
                    pe.wait_ge(heads_made.sem, heads_made.upto(b.n, h // 2))
                r = 2 * k * VW
                mm(HO[:, r:r + VW], cmat[:, k, 0:P], v_aug[:, b.par, 0, h, :], start=True, stop=True)
                mm(HO[:, r + VW:r + 2 * VW], cmat[:, k, P:S], v_aug[:, b.par, 0, h, :],
                   start=True, stop=False)
                mm(HO[:, r + VW:r + 2 * VW], cmat[:, k, S:TRI], v_aug[:, b.par, 1, h, :],
                   start=False, stop=True).then_inc(pv_made.sem, 1)

            def rank(b, front, attend):
                pe.wait_ge(chosen_made.sem, chosen_made.upto(b.n, 2))
                if front:
                    pe.wait_ge(gates_read.sem, gates_read.upto(b.n + 3))
                elif attend:
                    pe.wait_ge(key_made.sem, key_made.upto(b.n + 2))
                mm(SM[:, 0:E], before_b[:, :], chosen[:, 0, :], start=True, stop=False)
                mm(SM[:, 0:E], ones_b[:, :], taken[:, b.par, :], start=False, stop=True)
                mm(SM[:, E:2 * E], before_b[:, :], chosen[:, 1, :], start=True, stop=False)
                mm(SM[:, E:2 * E], ones_b[:, :], taken_mid[:, :], start=False, stop=True
                   ).then_inc(ranks_made.sem, 1)

            def shared(b, m, front):
                pe.wait_ge(weights_in.sem, weights_in.upto(N_SHARED - 1))
                pe.wait_ge(x2nT_made.sem, x2nT_made.upto(b.n))
                if m:
                    pe.wait_ge(sh_act_made.sem, sh_act_made.upto(b.n, m))
                else:
                    pe.wait_ge(base_made.sem, base_made.upto(b.n - 1))
                if m == 0:
                    pe.wait_ge(place_step.sem, place_step.upto(b.n - 1, 1))
                    if front:
                        pe.wait_ge(gates_read.sem, gates_read.upto(b.n + 2))
                for n, (at, w) in enumerate(((0, sh_gate), (S, sh_up))):
                    for c in range(DC):
                        last = mm(FF[:, at:at + S], w[:, c, m * P:(m + 1) * P], x2nT[:, c, :],
                                  start=(c == 0), stop=(c == DC - 1))
                        if m == 0:
                            logit = mm(SM[:, n * E:(n + 1) * E], x2nT[:, c, n * P:(n + 1) * P],
                                       router_wT[:, c, :], start=(c == 0), stop=(c == DC - 1))
                    if m == 0 and n == 1:
                        logit.then_inc(router_made.sem, 1)
                last.then_inc(sh_made.sem, 1)

            def shared_down(b, j):
                pe.wait_ge(sh_act_made.sem, sh_act_made.upto(b.n))
                if j:
                    pe.wait_ge(base_made.sem, base_made.upto(b.n, j))
                for m in range(SC):
                    last = mm(FF[:, :], sh_actT[:, m, j * P:(j + 1) * P], sh_down[:, m, :],
                              start=(m == 0), stop=(m == SC - 1))
                last.then_inc(sh_down_made.sem, 1)

            def step(t, front=True, attend=True, route=True, rest=True):
                F, A, G, H = t + 1, t, t + -1, t + -2
                if attend:
                    head(A, 0)
                if rest:
                    shared(H, 2, front)
                if attend:
                    head(A, 1)
                    pv(A, 0)
                if front:
                    turn_ctx(F, 0)
                if rest:
                    shared(H, 3, front)
                if attend:
                    head(A, 2)
                    pv(A, 1)
                if front:
                    turn_ctx(F, 1)
                if rest:
                    shared_down(H, 0)
                if attend:
                    head(A, 3)
                if front:
                    turn_x(F, 0)
                if attend:
                    pv(A, 2)
                    head(A, 4)
                if front:
                    turn_x(F, 1)
                if attend:
                    pv(A, 3)
                if rest:
                    shared_down(H, 1)
                if front:
                    gates_pe(F)
                if attend:
                    head(A, 5)
                if route:
                    turn(G, 0, front)
                if attend:
                    pv(A, 4)
                    head(A, 6)
                if route:
                    turn(G, 1, front)
                if rest and route:
                    rank(H, front, attend)
                if attend:
                    pv(A, 5)
                if route:
                    shared(G, 0, front)
                if route and not attend:
                    rank(G, front, attend)
                if attend:
                    head(A, 7)
                    pv(A, 6)
                if route:
                    shared(G, 1, front)
                if front:
                    columns(F, route)
                if attend:
                    pv(A, 7)

            step(Item(0, -1), attend=False, route=False, rest=False)
            step(Item(0, 0), route=False, rest=False)
            step(Item(0, 1), rest=False)
            step(Item(0, 2))
            with pe.Fori(0, (B - 4) // 2) as i:
                step(Item(i, 3))
                step(Item(i, 4))
            step(Item(0, B - 1), front=False)
            step(Item(0, B), front=False, attend=False)
            pe.wait_ge(chosen_made.sem, chosen_made.upto(B - 1))
            pe.wait_ge(place_step.sem, place_step.upto(B - 1, 1))
            mm(SM[:, 0:E], ones_b[:, :], taken[:, B % 2, :], start=True, stop=True).then_inc(counts_made.sem, 1)
            pe.wait_ge(table_step.sem, TABLE_STEPS)
            tr(SM[0:1, 0:P], tile_info[:, 2:3], ident[:, :])
            tr(SM[0:1, P:2 * P], tile_info[:, 3:4], ident[:, :]).then_inc(tables_turned.sem, 1)

            step(Item(0, B + 1), front=False, attend=False, route=False)

            def turn_rows(n, t, k):
                pe.wait_ge(xt_in[k].sem, n)
                pe.wait_ge(xtT_made.sem, xtT_made.upto(t.n - 2))
                for c in range(DC):
                    last = tr(bank[t.par][:, c * P:(c + 1) * P], xt[:, k, c * P:(c + 1) * P], ident[:, :])
                last.then_inc(xt_turned.sem, 1)

            def expert_of(t):
                return pe.value_load(expert_tab[0:1, bass.ds(t.n, 1)], min_val=0, max_val=E - 1)

            def gate_up(t, e, slot):
                pe.wait_ge(expert_in.sem, e + 1)
                pe.wait_ge(xtT_made.sem, xtT_made.upto(t.n))
                pe.wait_ge(act_made.sem, act_made.upto(t.n - 2))
                for c in range(DC):
                    last = mm(bank[2 + t.par][:, :], xtT[:, t.par, c * P:(c + 1) * P],
                              w_gu[:, bass.ds(slot, 1), c, :].rearrange("p a i -> p (a i)"),
                              start=(c == 0), stop=(c == DC - 1))
                last.then_inc(gu_made.sem, 1)

            def turn_act(t):
                pe.wait_ge(act_made.sem, act_made.upto(t.n))
                pe.wait_ge(actT_made.sem, actT_made.upto(t.n - 1))
                for c in range(IC):
                    last = tr(bank[4][:, c * P:(c + 1) * P], act_a[:, t.par, c * P:(c + 1) * P], ident[:, :])
                last.then_inc(act_turned.sem, 1)

            def down(t):
                slot = pe.snap(expert_of(t) % RING)
                pe.wait_ge(actT_made.sem, actT_made.upto(t.n))
                pe.wait_ge(y_copied.sem, y_copied.upto(t.n - 2))
                for c in range(IC):
                    last = mm(bank[5 + t.par][:, :], act_aT[:, t.par, c * P:(c + 1) * P],
                              w_dn[:, bass.ds(slot, 1), c, :].rearrange("p a i -> p (a i)"),
                              start=(c == 0), stop=(c == IC - 1))
                last.then_inc(y_made.sem, 1)

            def expert_step(t, k, lap, ahead2=True, ahead1=True):
                if ahead1:
                    e = expert_of(t + 1)
                    slot = pe.snap(e % RING)
                if ahead2:
                    turn_rows(lap * 16 + 16, t + 2, k)
                turn_act(t)
                if ahead1:
                    gate_up(t + 1, e, slot)
                down(t)

            pe.sem_inc(y_made.sem, y_made.start)
            pe.wait_ge(tables_made.sem, tables_made.upto(0))
            turn_rows(16, Item(0, 0), 0)
            turn_rows(16, Item(0, 1), 1)
            e = expert_of(Item(0, 0))
            gate_up(Item(0, 0), e, pe.snap(e % RING))
            expert_step(Item(0, 0), 2, 0)
            expert_step(Item(0, 1), 3, 0)
            with pe.Fori(0, (TILES - 4) // 4) as i:
                for u in range(4):
                    expert_step(Item(i * 2, 2 + u), u, i + 1)
            for n in range(TILES - 2, TILES):
                expert_step(Item(0, n), 0, 0, ahead2=False, ahead1=n + 1 < TILES)

        @block.vector
        def _(dve):
            v = nc.vector

            pe_w = SM[:, 0:(3 * DC + DC) * 16].rearrange("p (c n) -> p c n", n=16)
            dve.wait_ge(wT_made.sem, 1)
            for k in range(2):
                v.tensor_copy(gate_wT[:, :, k * FG:k * FG + NH], pe_w[:, 0:2 * DC, k * NH:(k + 1) * NH]
                              ).then_inc(wT_copied.sem, 1)
            v.tensor_copy(router_wT[:, :, :], pe_w[:, 3 * DC:4 * DC, :]).then_inc(wT_copied.sem, 1)
            dve.wait_ge(wT_copied.sem, 3)
            for k in range(2):
                both = gate_wT[:, DC:2 * DC, k * FG:k * FG + NH]
                v.tensor_tensor(both, pe_w[:, 2 * DC:3 * DC, k * NH:(k + 1) * NH], both, ALU.add
                                ).then_inc(wT_copied.sem, 1)
            dve.wait_ge(act_const.sem, 1)
            v.tensor_scalar(ln_row[:, :], ln_row[:, :], tanh_g[:, 0:1], None, ALU.mult
                            ).then_inc(wT_copied.sem, 1)
            dve.wait_ge(wT_copied.sem, 6)
            dve.wait_ge(pool_const.sem, POOL_CONSTS)

            def base_tile(b, j):
                return base_out[:, bass.ds(b.n * ST + j, 1), :].rearrange("p a d -> p (a d)")

            def stats(b):
                dve.wait_ge(x_in[b.par].sem, x_in[b.par].upto(b.half))
                apart(dve)
                for j in range(ST):
                    v.bn_stats(ln_stat[:, j, :], base_tile(b, j)).then_inc(ln_step.sem, 1)
                for j in range(ST):
                    dve.wait_ge(ln_step.sem, ln_step.upto(b.n, j + 1))
                    apart(dve)
                    v.bn_aggr(ln_mv[:, j, :], ln_stat[:, j, :]).then_inc(ln_step.sem, 1)
                dve.wait_ge(ln_step.sem, ln_step.upto(b.n))
                v.tensor_scalar(ln_var[:, :], ln_mv[:, :, 1], LN_EPS, None, ALU.add
                                ).then_inc(ln_var_made.sem, 1)

            def norm_front(b):
                dve.wait_ge(ln_rstd_made.sem, ln_rstd_made.upto(b.n))
                dve.wait_ge(xn_turned.sem, xn_turned.upto(b.n - 1))
                for j in range(ST):
                    v.tensor_scalar(xn[:, j, :], base_tile(b, j), ln_mv[:, j, 0:1], ln_rstd[:, j:j + 1],
                                    ALU.subtract, ALU.mult).then_inc(xn_made.sem, 1)

            def gates_dve(b):
                dve.wait_ge(gates_made.sem, gates_made.upto(b.n))
                for k in range(2):
                    rows = slice(k * FG, k * FG + NH)
                    v.tensor_scalar(gates[rows, :], SM[rows, 0:S], gate_bias[rows, :], None, ALU.add
                                    ).then_inc(gates_read.sem, 1)
                dve.wait_ge(gates_read.sem, gates_read.upto(b.n))
                v.scalar_tensor_tensor(f_row[FG:, :], gates[FG:, :], -1.0, gates[FG:, :], ALU.mult, ALU.max
                                       ).then_inc(f_abs_made.sem, 1)

            def rows(b):
                dve.wait_ge(f_ln_made.sem, f_ln_made.upto(b.n))
                v.scalar_tensor_tensor(f_row[FG:, :], gates[FG:, :], 0.0, f_row[FG:, :],
                                       ALU.min, ALU.subtract).then_inc(row_step.sem, 1)
                dve.wait_ge(row_step.sem, row_step.upto(b.n, 1))
                v.tensor_tensor_scan(cum_row[:, :], one[FG:FG + NH, :].to_broadcast([NH, S]), f_row[FG:, :],
                                     0.0, ALU.mult, ALU.add).then_inc(row_step.sem, 1)
                dve.wait_ge(row_step.sem, row_step.upto(b.n, 2))
                v.tensor_tensor(key_max[0:NH, :], gates[0:NH, :], cum_row[:, :], ALU.subtract
                                ).then_inc(row_step.sem, 1)
                dve.wait_ge(row_step.sem, row_step.upto(b.n, 3))
                v.tensor_tensor_scan(max_row[:, :], key_max[0:NH, :], key_max[0:NH, :], -3.0e38,
                                     ALU.max, ALU.max).then_inc(row_step.sem, 1)
                dve.wait_ge(row_step.sem, row_step.upto(b.n, 4))
                v.tensor_tensor(key_max[FG:, :], max_row[:, :], cum_row[:, :], ALU.add
                                ).then_inc(row_step.sem, 1)
                dve.wait_ge(max_spread.sem, max_spread.upto(b.n - 2))
                v.tensor_copy(max_parts[0:NH, b.par, :], max_row[:, :]).then_inc(row_step.sem, 1)
                dve.wait_ge(row_step.sem, row_step.upto(b.n, 6))
                v.tensor_tensor(max_rest[:, :], max_row[:, :], max_parts[0:NH, b.par, :], ALU.subtract
                                ).then_inc(row_step.sem, 1)
                dve.wait_ge(row_step.sem, row_step.upto(b.n, 7))
                v.tensor_copy(max_mid[:, :], max_rest[:, :]).then_inc(row_step.sem, 1)
                dve.wait_ge(row_step.sem, row_step.upto(b.n, 8))
                v.tensor_copy(max_parts[32:32 + NH, b.par, :], max_mid[:, :]).then_inc(row_step.sem, 1)
                v.tensor_tensor(max_parts[64:64 + NH, b.par, :], max_rest[:, :], max_mid[:, :],
                                ALU.subtract).then_inc(row_step.sem, 1)

            def columns(b):
                dve.wait_ge(columns_turned.sem, columns_turned.upto(b.n))
                dve.wait_ge(decay_made.sem, decay_made.upto(b.n - 2))
                v.tensor_copy(key_log[:, b.par], row_columns[:, :, 0:NH]).then_inc(key_made.sem, 1)
                v.tensor_copy(max_log[:, :, :], row_columns[:, :, FG:]).then_inc(key_made.sem, 1)

            def head(b, h):
                k = h % 2
                dve.wait_ge(qk_made.sem, qk_made.upto(b.n, h + 1))
                dve.wait_ge(decay_made.sem, decay_made.upto(b.n, h + 1))
                dve.wait_ge(pv_made.sem, pv_made.upto(b.n, h - 1))
                v.scalar_tensor_tensor(cmat[:, k, :], QK[k][:, 0:TRI], QK_SCALE, decay[:, k, :],
                                       ALU.mult, ALU.mult).then_inc(c_made.sem, 1)

            def out_pair(b, q):
                dve.wait_ge(pv_made.sem, pv_made.upto(b.n, 2 * q + 2))
                dve.wait_ge(floor_made.sem, floor_made.upto(b.n))
                pair = HO[:, 0:2 * ST * VW].rearrange("p (h j w) -> p h j w", h=2, w=VW)
                v.scalar_tensor_tensor(norm[:, :, :], pair[:, :, :, DH], -1.0,
                                       norm_floor[:, b.par, :, 2 * q:2 * q + 2].rearrange("p j h -> p h j"),
                                       ALU.mult, ALU.max).then_inc(norm_step.sem, 1)
                dve.wait_ge(norm_step.sem, norm_step.upto(b.n, 4 * q + 1))
                v.tensor_tensor(norm_abs[:, :, :], pair[:, :, :, DH], norm[:, :, :], ALU.max
                                ).then_inc(norm_step.sem, 1)
                dve.wait_ge(norm_step.sem, norm_step.upto(b.n, 4 * q + 2))
                v.tensor_scalar(norm_e[:, :, :], norm_abs[:, :, :], NORM_EPS, None, ALU.add
                                ).then_inc(norm_step.sem, 1)
                dve.wait_ge(norm_step.sem, norm_step.upto(b.n, 4 * q + 3))
                v.reciprocal(norm_inv[:, :, :], norm_e[:, :, :]).then_inc(norm_step.sem, 1)
                dve.wait_ge(norm_step.sem, norm_step.upto(b.n, 4 * q + 4))
                v.tensor_tensor(
                    heads[:, :, 2 * q * DH:(2 * q + 2) * DH].rearrange("p j (h d) -> p h j d", h=2),
                    pair[:, :, :, 0:DH], norm_inv[:, :, :].unsqueeze(3).to_broadcast([P, 2, ST, DH]),
                    ALU.mult).then_inc(heads_made.sem, 1)

            def h_stats(b):
                dve.wait_ge(heads_made.sem, heads_made.upto(b.n))
                apart(dve)
                for j in range(ST):
                    v.bn_stats(h_stat[:, j, :], heads[:, j, :]).then_inc(post_step.sem, 1)
                for j in range(ST):
                    dve.wait_ge(post_step.sem, post_step.upto(b.n, j + 1))
                    apart(dve)
                    v.bn_aggr(h_mv[:, j, :], h_stat[:, j, :]).then_inc(post_step.sem, 1)
                dve.wait_ge(post_step.sem, post_step.upto(b.n, 2 * ST))
                v.tensor_scalar(h_var[:, :], h_mv[:, :, 1], LN_EPS, None, ALU.add).then_inc(h_var_made.sem, 1)

            def center(b):
                for j in range(ST):
                    v.scalar_tensor_tensor(heads[:, j, :], heads[:, j, :], h_mv[:, j, 0:1], ln_row[:, :],
                                           ALU.subtract, ALU.mult).then_inc(post_step.sem, 1)

            def x2_add(b):
                dve.wait_ge(post_step.sem, post_step.upto(b.n, 3 * ST))
                dve.wait_ge(h_rstd_made.sem, h_rstd_made.upto(b.n))
                for j in range(ST):
                    v.scalar_tensor_tensor(base_tile(b, j), heads[:, j, :], h_rstd[:, j:j + 1],
                                           base_tile(b, j), ALU.mult, ALU.add
                                           ).then_inc(x2_made.sem, 1)

            def x2_stats(b):
                for j in range(ST):
                    dve.wait_ge(x2_made.sem, x2_made.upto(b.n, j + 1))
                    apart(dve)
                    v.bn_stats(x2_stat[:, j, :], base_tile(b, j)).then_inc(post_step.sem, 1)
                for j in range(ST):
                    dve.wait_ge(post_step.sem, post_step.upto(b.n, 3 * ST + j + 1))
                    apart(dve)
                    v.bn_aggr(x2_mv[:, j, :], x2_stat[:, j, :]).then_inc(post_step.sem, 1)
                dve.wait_ge(post_step.sem, post_step.upto(b.n))
                v.tensor_scalar(x2_var[:, :], x2_mv[:, :, 1], LN_EPS, None, ALU.add
                                ).then_inc(x2_var_made.sem, 1)

            def post_norm(b):
                dve.wait_ge(x2_rstd_made.sem, x2_rstd_made.upto(b.n))
                dve.wait_ge(scattered[b.par].sem, scattered[b.par].upto(b.half - 1))
                for j in range(ST):
                    v.tensor_scalar(x2n[:, b.par, j, :], base_tile(b, j), x2_mv[:, j, 0:1],
                                    x2_rstd[:, j:j + 1], ALU.subtract, ALU.mult).then_inc(x2n_made.sem, 1)

            def router(b):
                dve.wait_ge(router_made.sem, router_made.upto(b.n))
                v.tensor_copy(logits[:, :, :], SM[:, 0:ST * E].rearrange("p (j n) -> p j n", j=ST)
                              ).then_inc(logits_made.sem, 1)

            def top(b):
                dve.wait_ge(logits_made.sem, logits_made.upto(b.n))
                apart(dve)
                for j in range(ST):
                    v.max(top8[:, j, :], logits[:, j, :]).then_inc(top_step.sem, 1)
                    dve.wait_ge(top_step.sem, top_step.upto(b.n, 2 * j + 1))
                    apart(dve)
                    v.max_index(top8_at[:, j, :], top8[:, j, :], logits[:, j, :]).then_inc(top_step.sem, 1)
                v.tensor_tensor(gap[:, :], top8[:, :, 1], top8[:, :, 0], ALU.subtract
                                ).then_inc(gap_made.sem, 1)
                dve.wait_ge(top_step.sem, top_step.upto(b.n, 2 * ST))
                v.tensor_copy(top_at[:, :, :], top8_at[:, :, 0:TOPK]).then_inc(top_step.sem, 1)
                dve.wait_ge(top_step.sem, top_step.upto(b.n, 2 * ST + 1))
                for j in range(ST):
                    for k in range(TOPK):
                        v.tensor_scalar(one_hot[:, j, k, :], expert_no[:, :], top_at[:, j, k:k + 1], None,
                                        ALU.is_equal).then_inc(hot_made.sem, 1)
                dve.wait_ge(hot_made.sem, hot_made.upto(b.n))
                v.tensor_tensor(chosen[:, :, :], one_hot[:, :, 0, :], one_hot[:, :, 1, :], ALU.add
                                ).then_inc(chosen_made.sem, 1)
                dve.wait_ge(chosen_made.sem, chosen_made.upto(b.n, 1))
                v.tensor_tensor(taken_mid[:, :], taken[:, b.par, :], chosen[:, 0, :], ALU.add
                                ).then_inc(chosen_made.sem, 1)
                dve.wait_ge(chosen_made.sem, chosen_made.upto(b.n, 2))
                dve.wait_ge(ranks_made.sem, ranks_made.upto(b.n - 1))
                v.tensor_tensor(taken[:, 1 - b.par, :], taken_mid[:, :], chosen[:, 1, :], ALU.add
                                ).then_inc(chosen_made.sem, 1)
                dve.wait_ge(gap_exp_made.sem, gap_exp_made.upto(b.n))
                v.tensor_scalar(gap_den[:, :], gap_exp[:, :], 1.0, None, ALU.add).then_inc(w_step.sem, 1)
                dve.wait_ge(w_step.sem, w_step.upto(b.n, 1))
                v.reciprocal(top_w[:, :, 0], gap_den[:, :]).then_inc(w_step.sem, 1)
                dve.wait_ge(w_step.sem, w_step.upto(b.n, 2))
                v.tensor_tensor(top_w[:, :, 1], top_w[:, :, 0], gap_exp[:, :], ALU.mult
                                ).then_inc(w_step.sem, 1)
                dve.wait_ge(w_step.sem, w_step.upto(b.n, 3))
                v.tensor_scalar(all_w[:, bass.ds(b.n, 1), :].rearrange("p a n -> p (a n)"),
                                top_w[:, :, :].rearrange("p j k -> p (j k)"), tanh_g[:, 1:2], None,
                                ALU.mult).then_inc(route_kept.sem, 1)
                v.tensor_copy(all_hot[:, bass.ds(b.n, 1)].rearrange("p a n e -> p (a n e)"),
                              one_hot[:, :, :, :].rearrange("p j k e -> p (j k e)")
                              ).then_inc(route_kept.sem, 1)

            def rank(b):
                dve.wait_ge(ranks_made.sem, ranks_made.upto(b.n))
                v.tensor_tensor(place[:, :, :], SM[:, 0:ST * E].rearrange("p (j n) -> p j n", j=ST),
                                expert_row[:, :].unsqueeze(1).to_broadcast([P, ST, E]), ALU.add
                                ).then_inc(place_step.sem, 1)
                dve.wait_ge(place_step.sem, place_step.upto(b.n, 1))
                v.tensor_tensor(place_pick[:, :, :].rearrange("p (j k) e -> p j k e", j=ST), one_hot[:, :, :, :],
                                place[:, :, :].unsqueeze(2).to_broadcast([P, ST, TOPK, E]), ALU.mult
                                ).then_inc(place_step.sem, 1)
                dve.wait_ge(place_step.sem, place_step.upto(b.n, 2))
                v.tensor_reduce(slot_f[:, :], place_pick[:, :, :], AX_X, ALU.add).then_inc(place_step.sem, 1)
                dve.wait_ge(place_step.sem, place_step.upto(b.n, 3))
                dve.wait_ge(scattered[b.par].sem, scattered[b.par].upto(b.half - 1))
                v.tensor_copy(slot_u[:, b.par, :], slot_f[:, :]).then_inc(slots_made.sem, 1)
                v.tensor_copy(all_slot[:, bass.ds(b.n, 1), :].rearrange("p a n -> p (a n)"), slot_f[:, :]
                              ).then_inc(route_kept.sem, 1)

            def shared(b, m):
                dve.wait_ge(sh_tanh_made.sem, sh_tanh_made.upto(b.n, m + 1))
                dve.wait_ge(sh_act_made.sem, sh_act_made.upto(b.n, m))
                v.scalar_tensor_tensor(silu_g[:, :], silu_t[:, :], 1.0, FF[:, 0:S], ALU.add, ALU.mult
                                       ).then_inc(sh_silu_made.sem, 1)
                dve.wait_ge(sh_silu_made.sem, sh_silu_made.upto(b.n, m + 1))
                dve.wait_ge(sh_down_made.sem, sh_down_made.upto(b.n - 1))
                v.scalar_tensor_tensor(sh_actT[:, m, :], silu_g[:, :], 0.5, FF[:, S:2 * S], ALU.mult, ALU.mult
                                ).then_inc(sh_act_made.sem, 1)

            def shared_down(b, j):
                dve.wait_ge(sh_down_made.sem, sh_down_made.upto(b.n, j + 1))
                v.scalar_tensor_tensor(base_tile(b, j), FF[:, :], tanh_g[:, 1:2], base_tile(b, j),
                                       ALU.mult, ALU.add
                                       ).then_inc(base_made.sem, 1)

            def step(t, front=True, attend=True, route=True, rest=True):
                F, A, G, H = t + 1, t, t + -1, t + -2
                if attend:
                    head(A, 0)
                if rest:
                    shared(H, 2)
                if attend:
                    head(A, 1)
                if route:
                    center(G)
                if front:
                    stats(F)
                if rest:
                    shared(H, 3)
                if attend:
                    head(A, 2)
                if front:
                    norm_front(F)
                if route:
                    x2_add(G)
                if attend:
                    out_pair(A, 0)
                if rest:
                    shared_down(H, 0)
                if attend:
                    head(A, 3)
                    head(A, 4)
                    out_pair(A, 1)
                if route:
                    x2_stats(G)
                if rest and route:
                    top(H)
                if route:
                    post_norm(G)
                if rest:
                    shared_down(H, 1)
                if front:
                    gates_dve(F)
                if attend:
                    head(A, 5)
                    head(A, 6)
                if rest and route:
                    rank(H)
                if attend:
                    out_pair(A, 2)
                if route:
                    router(G)
                if route and not attend:
                    top(G)
                if route:
                    shared(G, 0)
                if route and not attend:
                    rank(G)
                if attend:
                    head(A, 7)
                if front:
                    rows(F)
                if route:
                    shared(G, 1)
                if front:
                    columns(F)
                if attend:
                    out_pair(A, 3)
                    h_stats(A)

            step(Item(0, -1), attend=False, route=False, rest=False)
            step(Item(0, 0), route=False, rest=False)
            step(Item(0, 1), rest=False)
            step(Item(0, 2))
            with dve.Fori(0, (B - 4) // 2) as i:
                step(Item(i, 3))
                step(Item(i, 4))
            step(Item(0, B - 1), front=False)
            step(Item(0, B), front=False, attend=False)
            steps = [0]

            def then(ins):
                steps[0] += 1
                ins.then_inc(table_step.sem, 1)
                dve.wait_ge(table_step.sem, steps[0])

            then(v.memset(zeros, 0.0))
            dve.wait_ge(counts_made.sem, counts_made.upto(0))
            then(v.tensor_copy(count[:, :], SM[:, 0:E]))
            then(v.tensor_tensor(pad_f[:, :], count[:, :], expert_row[:, :], ALU.add))
            v.tensor_copy(pad_tab[:, :], pad_f[0:1, :]).then_inc(pads_made.sem, 1)
            then(v.tensor_scalar(count_i[:, :], count[:, :], float(P - 1), None, ALU.add))
            then(v.tensor_scalar(tiles_i[:, :], count_i[:, :], P.bit_length() - 1, None,
                                 ALU.arith_shift_right))
            then(v.tensor_copy(tiles_f[:, :], tiles_i[:, :]))
            then(v.tensor_tensor_scan(tile_end[:, :], tiles_f[:, :], zeros[:, 0:E], 0.0, ALU.add, ALU.add))
            then(v.tensor_tensor(tile_first[:, :], tile_end[:, :], tiles_f[:, :], ALU.subtract))
            then(v.tensor_scalar(ended[:, :], tile_end[:, :], part_no[:, 0:1], None, ALU.is_le))
            then(v.tensor_reduce(tile_info[:, 0:1], ended[:, :], AX_X, ALU.add))
            then(v.tensor_tensor(ended_at[:, :], ended[:, :], tile_end[:, :], ALU.mult))
            then(v.tensor_reduce(tile_info[:, 1:2], ended_at[:, :], AX_X, ALU.max))
            then(v.tensor_tensor(tile_info[:, 1:2], part_no[:, 0:1], tile_info[:, 1:2], ALU.subtract))
            then(v.tensor_scalar(tile_info[:, 1:2], tile_info[:, 1:2], float(P), None, ALU.mult))
            then(v.tensor_scalar(tile_info[:, 2:3], tile_info[:, 0:1], float(CAP), tile_info[:, 1:2],
                                 ALU.mult, ALU.add))
            then(v.tensor_scalar(tile_info[:, 2:3], tile_info[:, 2:3], float(DUMP), None, ALU.min))
            then(v.tensor_scalar(tile_info[:, 3:4], tile_info[:, 0:1], float(E - 1), None, ALU.min))
            assert steps[0] == TABLE_STEPS
            v.tensor_copy(first_tab[:, :], tile_first[0:1, :])
            dve.wait_ge(tables_turned.sem, tables_turned.upto(0))
            v.tensor_copy(row_tab[:, :], SM[0:1, 0:P])
            v.tensor_copy(expert_tab[:, :], SM[0:1, P:2 * P]).then_inc(tables_made.sem, 1)

            step(Item(0, B + 1), front=False, attend=False, route=False)

            def silu(t):
                dve.wait_ge(act_tanh_made.sem, act_tanh_made.upto(t.n))
                v.scalar_tensor_tensor(act_g[:, t.par, :], act_t[:, t.par, :], 1.0,
                                       bank[2 + t.par][:, 0:I], ALU.add, ALU.mult
                                       ).then_inc(act_silu_made.sem, 1)
                dve.wait_ge(act_silu_made.sem, act_silu_made.upto(t.n))
                v.scalar_tensor_tensor(act_a[:, t.par, :], act_g[:, t.par, :], 0.5,
                                       bank[2 + t.par][:, I:2 * I], ALU.mult, ALU.mult
                                       ).then_inc(act_made.sem, 1)

            def copy_actT(t):
                dve.wait_ge(act_turned.sem, act_turned.upto(t.n))
                dve.wait_ge(y_made.sem, y_made.upto(t.n - 2))
                v.tensor_copy(act_aT[:, t.par, :], bank[4][:, 0:I]).then_inc(actT_made.sem, 1)

            def expert_step(t, ahead1=True):
                copy_actT(t)
                if ahead1:
                    silu(t + 1)

            silu(Item(0, 0))
            expert_step(Item(0, 0))
            expert_step(Item(0, 1))
            then(v.tensor_scalar(shift[:, :], tile_first[:, :], float(P), None, ALU.mult))
            then(v.tensor_tensor(shift[:, :], shift[:, :], expert_row[:, :], ALU.subtract))
            hot = all_hot[:, :, :, :].rearrange("p b n e -> p (b n) e")
            then(v.tensor_tensor(hot_shift, hot, shift[:, :].unsqueeze(1).to_broadcast([P, B * ST * TOPK, E]),
                                 ALU.mult))
            then(v.tensor_reduce(y_slot_f[:, :], hot_shift, AX_X, ALU.add))
            then(v.tensor_tensor(y_slot_f[:, :], y_slot_f[:, :],
                                 all_slot[:, :, :].rearrange("p b n -> p (b n)"), ALU.add))
            then(v.tensor_copy(y_slot[:, :], y_slot_f[:, :]))
            with dve.Fori(0, (TILES - 4) // 2) as i:
                expert_step(Item(i, 2))
                expert_step(Item(i, 3))
            expert_step(Item(0, TILES - 2))
            expert_step(Item(0, TILES - 1), ahead1=False)

            def place_rows(n, k):
                v.tensor_copy(y_at[:, k, :], y_slot[:, bass.ds(n * TOPK, TOPK)]).then_inc(y_at_made.sem, 1)

            weights = all_w[:, :, :].rearrange("p b n -> p (b n)")

            def combine(lap, k, more=True):
                n = lap * 4 + k
                dve.wait_ge(y_got[k].sem, y_got[k].upto(lap))
                v.scalar_tensor_tensor(y_in[:, k, 0, :], y_in[:, k, 0, :], weights[:, bass.ds(n * TOPK, 1)],
                                       base_out[:, bass.ds(n, 1), :].rearrange("p a d -> p (a d)"),
                                       ALU.mult, ALU.add).then_inc(fin_step.sem, 1)
                dve.wait_ge(fin_step.sem, fin_step.upto(n))
                dve.wait_ge(out_stored[k].sem, out_stored[k].upto(lap - 1))
                v.scalar_tensor_tensor(fin[:, k, :], y_in[:, k, 1, :], weights[:, bass.ds(n * TOPK + 1, 1)],
                                       y_in[:, k, 0, :], ALU.mult, ALU.add).then_inc(fin_made.sem, 1)
                if more:
                    place_rows(n + 4, k)

            dve.wait_ge(table_step.sem, table_step.upto(steps[0] - 1))
            for k in range(4):
                place_rows(k, k)
            for k in range(4):
                combine(0, k)
            with dve.Fori(1, NT // 4 - 1) as i:
                for k in range(4):
                    combine(i, k)
            for k in range(4):
                combine(NT // 4 - 1, k, more=False)


POOL_CONSTS = 23
TABLE_STEPS = 17


_INS = ['x', 'ctx_1024', 'g_xattn', 'g_ffn', 'L0_xattn_igate_w', 'L0_xattn_igate_b', 'L0_xattn_fgate_w',
        'L0_xattn_fgate_b', 'L0_xattn_ln_scale', 'L0_ffn_router_w', 'L0_ffn_expert_gate', 'L0_ffn_expert_up',
        'L0_ffn_expert_down', 'L0_ffn_shared_gate', 'L0_ffn_shared_up', 'L0_ffn_shared_down']
_OUTS = [((B, S, D), 'float32')]


def kernel(**inputs):
    import numpy as _np
    import concourse.bacc as _bacc
    from concourse import mybir as _mybir
    from concourse.bass_utils import run_bass_kernel_spmd as _run

    nc = _bacc.Bacc("TRN2", target_bir_lowering=False, num_devices=1)
    arrays, args = {}, []
    for name in _INS:
        a = _np.ascontiguousarray(inputs[name])
        arrays[f"in_{name}_dram"] = a
        args.append(nc.dram_tensor(f"in_{name}_dram", a.shape, _mybir.dt.from_np(a.dtype), kind="ExternalInput").ap())
    for i, (shape, dtype) in enumerate(_OUTS):
        dt = _mybir.dt.from_np(_np.dtype(dtype))
        args.append(nc.dram_tensor(f"out_{i}_dram", shape, dt, kind="ExternalOutput").ap())
    flamingo_kernel(nc, *args)
    r = _run(nc, [arrays], core_ids=[0])
    got = tuple(r.results[0][f"out_{i}_dram"] for i in range(len(_OUTS)))
    return got[0]
```

```python
from contextlib import ExitStack

import concourse.bass as bass
from concourse import mybir

F32 = mybir.dt.float32
F32R = mybir.dt.float32r
BF16 = mybir.dt.bfloat16
I32 = mybir.dt.int32
U32 = mybir.dt.uint32
ALU = mybir.AluOpType
ACT = mybir.ActivationFunctionType
AX_X = mybir.AxisListType.X

P = 128
B, S, D = 16, 256, 512
NH, DH = 8, 64
E, I = 16, 256
IS = 512
PARTS = ((0, 0), (0, 1), (1, 0))
FG = 32
TOPK = 2
T = B * S
ST = S // P
NT = T // P
DC = D // P
IC = I // P
SC = IS // P
LN_EPS = 1e-5
NORM_EPS = 1e-6
QK_SCALE = DH ** -0.5
MASK = 1e30
CAP = T + P
DUMP = E * CAP
TILES = (T * TOPK + E * (P - 1)) // P
TILES += TILES % 2
RING = 2
XRING = 4
TRI = S + P
VW = DH + 1


class Event:

    def __init__(self, sem, per=1, start=0):
        self.sem, self.per, self.start = sem, per, start

    def upto(self, n, k=None):
        value = n * self.per + (self.per if k is None else k)
        if isinstance(value, int) and value <= 0:
            return 0
        return value + self.start


class Item:

    def __init__(self, i, offset):
        self.i, self.offset = i, offset
        self.n = i * 2 + offset
        self.half = i + offset // 2
        self.par = offset % 2

    def __add__(self, k):
        return Item(self.i, self.offset + k)


def flamingo_kernel(nc, x, ctx_in, g_xattn, g_ffn, igate_w, igate_b, fgate_w, fgate_b, ln_scale,
                    router_w, expert_gate, expert_up, expert_down, shared_gate, shared_up,
                    shared_down, out):
    x_tok = x.rearrange("b (j p) d -> b p j d", p=P)
    c_tok = ctx_in.rearrange("b (j p) d -> b p j d", p=P)
    out_tok = out.rearrange("b s d -> (b s) d")
    routed_x = nc.dram_tensor("routed_x", (DUMP + P, D), F32).ap()
    routed_y = nc.dram_tensor("routed_y", (TILES * P, D), F32).ap()

    with ExitStack() as stack:
        def sb(name, shape, dt=F32):
            return stack.enter_context(nc.sbuf_tensor(name, shape, dt))

        def event(name, per=1, start=0):
            return Event(stack.enter_context(nc.semaphore(name)), per, start)

        bank = [stack.enter_context(nc.psum_tensor(f"bank{n}", [P, 512], F32)) for n in range(8)]
        TP, SM, MB, QK, HO, FF = bank[0], bank[1], bank[2:4], bank[4:6], bank[6], bank[7]
        GU = [FF, TP, FF, FF]
        row_columns = SM[:, 0:ST * (FG + NH)].rearrange("p (j n) -> p j n", j=ST)

        ident = sb("ident", [P, P])
        identb = sb("identb", [P, P], BF16)
        one = sb("one", [P, 1])
        before_b = sb("before_b", [P, P], BF16)
        ones_b = sb("ones_b", [P, P], BF16)
        mask_b = sb("mask_b", [P, P], BF16)
        head_sel = sb("head_sel", [P, NH, P], BF16)
        expert_no = sb("expert_no", [P, E])
        expert_row = sb("expert_row", [P, E])
        part_no = sb("part_no", [P, 1])
        minus_half = sb("minus_half", [P, ST])
        gate_wT = sb("gate_wT", [P, 2 * DC, FG + NH])
        router_wT = sb("router_wT", [P, 2, DC, P], F32R)
        gate_bias = sb("gate_bias", [P, 1])
        ln_row = sb("ln_row", [P, D])
        g_col = sb("g_col", [P, 2])
        tanh_g = sb("tanh_g", [P, 2])
        EW = DC * 2 * I + IC * D
        w_ring = sb("w_ring", [P, RING, 2, EW], F32R)
        w_gu = w_ring[:, :, :, 0:DC * 2 * I].rearrange("p r h (c i) -> p r h c i", c=DC)
        w_dn = w_ring[:, :, :, DC * 2 * I:EW].rearrange("p r h (c d) -> p r h c d", c=IC)
        sh_flat = w_ring[:, :, :, :].rearrange("p r h n -> p r (h n)")
        sh_w = sh_flat.rearrange("p r (w c i) -> p r w c i", w=3, c=DC)
        sh_gate, sh_up, sh_down = (sh_w[:, :, k] for k in range(3))

        area = [sb("area0", [P, EW]), sb("area1", [P, 2 * ST * NH * VW + 4 * TRI])]
        assert 2 * ST * NH * VW + 4 * TRI >= EW and 2 * DC * S + ST * D == EW
        cs_in = sb("cs_in", [P, 2, ST, D])
        v_aug = area[1][:, 0:2 * ST * NH * VW].rearrange("p (a j h w) -> p a j h w", a=2, j=ST, h=NH)
        xn = sb("xn", [P, D])
        xnT = area[0][:, 0:2 * DC * S].rearrange("p (a c s) -> p a c s", a=2, c=DC)
        ctxT = sb("ctxT", [P, 2, DC, S])
        ln_stat = sb("ln_stat", [P, ST, 6])
        ln_mv = sb("ln_mv", [P, 2, ST, 2])
        ln_var = sb("ln_var", [P, 2, ST])
        ln_rstd = sb("ln_rstd", [P, 2, ST])
        gates = sb("gates", [FG + NH, S])
        f_row = sb("f_row", [FG + NH, S])
        cum_row = f_row[0:NH, :]
        key_max_rest = sb("key_max_rest", [2 * FG + NH, S])
        key_max = key_max_rest[0:FG + NH, :]
        max_rest = key_max_rest[2 * FG:2 * FG + NH, :]
        logit_row = sb("logit_row", [E, S])
        key_log = sb("key_log", [P, 2, ST, NH])
        max_row = sb("max_row", [NH, S])
        max_mid = sb("max_mid", [2 * FG + NH, S], BF16)[2 * FG:2 * FG + NH, :]
        max_parts = sb("max_parts", [P, 2, S], BF16)
        max_log = sb("max_log", [P, ST, NH])
        norm_floor = sb("norm_floor", [P, 2, ST, NH])
        scores = area[1][:, 2 * ST * NH * VW:].rearrange("p (a n) -> p a n", a=4)
        decay, cmat = scores[:, 0:2], scores[:, 2:4]
        norm = sb("norm", [P, 2, ST])
        norm_abs = sb("norm_abs", [P, 2, ST])
        norm_e = sb("norm_e", [P, 2, ST])
        norm_inv = sb("norm_inv", [P, 2, ST])
        heads = area[0][:, 2 * DC * S:EW].rearrange("p (j d) -> p j d", j=ST)
        h_stat = sb("h_stat", [P, ST, 6])
        h_mv = sb("h_mv", [P, ST, 2])
        h_var = sb("h_var", [P, ST])
        h_rstd = sb("h_rstd", [P, ST])
        x2_stat = sb("x2_stat", [P, ST, 6])
        x2_mv = sb("x2_mv", [P, ST, 2])
        x2_var = sb("x2_var", [P, ST])
        x2_rstd = sb("x2_rstd", [P, ST])
        x2n = sb("x2n", [P, 2, ST, D])
        rows = x2n[0:E].rearrange("p a j d -> p (a j) d")
        gate_rows, router_rows = rows[:, 0:3, :].rearrange("p a d -> p (a d)"), rows[:, 3, :]
        x2nT = sb("x2nT", [P, 2, DC, S], F32R)
        logits = sb("logits", [P, ST, E])
        top8 = sb("top8", [P, ST, 8])
        top8_at = sb("top8_at", [P, ST, 8], U32)
        top_at = sb("top_at", [P, ST, TOPK])
        one_hot = sb("one_hot", [P, ST, TOPK, E])
        gap = sb("gap", [P, ST])
        gap_exp = sb("gap_exp", [P, ST])
        gap_den = sb("gap_den", [P, ST])
        top_w = sb("top_w", [P, ST, TOPK])
        chosen = sb("chosen", [P, ST, E], BF16)
        taken = sb("taken", [P, 2, E], BF16)
        taken_mid = sb("taken_mid", [P, E], BF16)
        place = sb("place", [P, ST, E])
        place_pick = sb("place_pick", [P, ST * TOPK, E])
        slot_f = sb("slot_f", [P, ST * TOPK])
        slot_u = sb("slot_u", [P, 2, ST * TOPK], U32)
        silu_t = sb("silu_t", [P, S])
        sh_act = sb("sh_act", [P, 2, S])
        sh_actT = sb("sh_actT", [P, 2, SC, S], F32R)
        base_out = sb("base_out", [P, NT, D])
        sh_in = base_out[:, NT - 3 * DC * D // D:NT, :].rearrange("p a d -> p (a d)")
        all_hot = sb("all_hot", [P, B, ST * TOPK, E], BF16)
        all_slot = sb("all_slot", [P, B, ST * TOPK])
        all_w = sb("all_w", [P, B, ST * TOPK])

        count = sb("count", [P, E])
        count_i = sb("count_i", [P, E], I32)
        tiles_i = sb("tiles_i", [P, E], I32)
        tiles_f = sb("tiles_f", [P, E])
        tile_end = sb("tile_end", [P, E])
        tile_first = sb("tile_first", [P, E])
        ended = sb("ended", [P, E])
        ended_at = sb("ended_at", [P, E])
        tile_info = sb("tile_info", [P, 4])
        pad_f = sb("pad_f", [P, E])
        pad_tab = sb("pad_tab", [1, E], I32)
        shift = sb("shift", [P, E])
        y_slot_f = sb("y_slot_f", [P, B * ST * TOPK])
        y_slot = sb("y_slot", [P, B * ST * TOPK], U32)
        first_tab = sb("first_tab", [1, E], I32)
        row_tab = sb("row_tab", [1, P], I32)
        expert_tab = sb("expert_tab", [1, P], I32)
        xt = x2n[:, :, :, :].rearrange("p a j d -> p (a j) d")
        xtT = x2nT[:, :, :, :].rearrange("p h c s -> p h (c s)").rearrange("p h (a n) -> p h a n", a=2)
        act_t, act_g, act_a = (ctxT[:, :, k, :] for k in range(3))
        act_aT = sh_actT[:, :, 0:2, :]
        stage = [area[k][:, 0:EW] for k in range(2)]
        y_out = cs_in[:, 0]
        hot_shift = cs_in[:, 1].rearrange("p j (n e) -> p (j n) e", e=E)
        zeros = xn[:, :]

        y_at = sb("y_at", [P, 4, TOPK], U32)
        y_in = [area[k // 2][:, k % 2 * TOPK * D:(k % 2 + 1) * TOPK * D].rearrange("p (k d) -> p k d", k=TOPK)
                for k in range(4)]
        fin = [area[k // 2][:, (4 + k % 2) * D:(5 + k % 2) * D] for k in range(4)]

        small_in = event("small_in", 16)
        weights_in = event("weights_in", 16)
        pool_const = event("pool_const")
        stood = event("stood")
        act_const = event("act_const")
        wT_made = event("wT_made")
        wT_copied = event("wT_copied")
        x_in = [event(f"x_in{k}", 16) for k in range(2)]
        c_in = [event(f"c_in{k}", 16) for k in range(2)]
        v_made = event("v_made")
        ln_step = event("ln_step", 2 * ST)
        ln_var_made = event("ln_var_made")
        ln_rstd_made = event("ln_rstd_made")
        h_var_made = event("h_var_made")
        h_rstd_made = event("h_rstd_made")
        x2_var_made = event("x2_var_made")
        x2_rstd_made = event("x2_rstd_made")
        xn_made = event("xn_made", ST)
        ctx_turned = event("ctx_turned", ST)
        ctxT_made = event("ctxT_made", ST)
        xn_turned = event("xn_turned", ST)
        xnT_made = event("xnT_made", ST)
        gates_made = event("gates_made")
        gates_read = event("gates_read", 2)
        f_abs_made = event("f_abs_made")
        f_exp_made = event("f_exp_made")
        f_ln_made = event("f_ln_made")
        key_made = event("key_made", 2)
        row_step = event("row_step", 10)
        columns_turned = event("columns_turned")
        floor_made = event("floor_made")
        qk_made = event("qk_made", NH)
        max_spread = event("max_spread", NH)
        decay_made = event("decay_made", NH)
        c_made = event("c_made", NH)
        pv_made = event("pv_made", NH)
        norm_step = event("norm_step", 4 * NH // 2)
        heads_made = event("heads_made", NH // 2)
        post_step = event("post_step", 5 * ST)
        x2_made = event("x2_made", ST)
        x2n_made = event("x2n_made", ST)
        x2_turned = event("x2_turned", ST)
        x2nT_made = event("x2nT_made", ST)
        x2lo_made = event("x2lo_made", ST)
        sh_hi_made = event("sh_hi_made", SC)
        sh_lo_made = event("sh_lo_made", SC)
        shared_hi_in = event("shared_hi_in")
        shared_in = event("shared_in")
        router_made = event("router_made")
        logit_row_made = event("logit_row_made")
        logits_turned = event("logits_turned")
        logits_made = event("logits_made")
        top_step = event("top_step", 2 * ST + 1)
        gap_made = event("gap_made")
        gap_exp_made = event("gap_exp_made")
        hot_made = event("hot_made", 2 * ST)
        w_step = event("w_step", 3)
        route_kept = event("route_kept", 3)
        chosen_made = event("chosen_made", 3)
        ranks_made = event("ranks_made")
        place_step = event("place_step", 3)
        slots_made = event("slots_made")
        scattered = [event(f"scattered{k}", 16 * ST * TOPK) for k in range(2)]
        sh_made = event("sh_made", SC)
        sh_tanh_made = event("sh_tanh_made", SC)
        sh_silu_made = event("sh_silu_made", SC)
        sh_act_made = event("sh_act_made", SC)
        sh_down_made = event("sh_down_made", ST)
        base_made = event("base_made", ST)

        counts_made = event("counts_made")
        table_step = event("table_step")
        tables_turned = event("tables_turned")
        tables_made = event("tables_made")
        pads_made = event("pads_made")
        padded = event("padded", 16)
        padded_by_pool = event("padded_by_pool", 16)
        y_slots_made = event("y_slots_made")
        expert_dma = [event(f"expert_dma{k}", 48) for k in range(2)]
        expert_hi_in = event("expert_hi_in")
        expert0_hi_in = event("expert0_hi_in")
        expert_in = event("expert_in")
        xt_in = [event(f"xt_in{k}", 16) for k in range(XRING)]
        xt_turned = event("xt_turned")
        xtT_made = event("xtT_made")
        xt_lo_made = event("xt_lo_made")
        aT_hi_made = event("aT_hi_made")
        gu_made = event("gu_made")
        act_tanh_made = event("act_tanh_made")
        act_silu_made = event("act_silu_made")
        act_made = event("act_made")
        act_turned = event("act_turned")
        actT_made = event("actT_made")
        y_made = event("y_made", start=1)
        y_copied = event("y_copied")
        y_stored = [event(f"y_stored{k}", 16) for k in range(2)]

        y_at_made = event("y_at_made")
        y_got = [event(f"y_got{k}", 16 * TOPK) for k in range(4)]
        fin_step = event("fin_step")
        fin_made = event("fin_made")
        out_stored = [event(f"out_stored{k}", 16) for k in range(4)]

        N_SMALL = 8
        N_SHARED = 3


        def apart(eng):
            eng.sem_inc(stood.sem, 1)

        block = stack.enter_context(nc.Block())

        @block.sync
        def _(sp):
            def load_x(b):
                sp.dma_start(base_out[:, bass.ds(b.n * ST, ST), :],
                             x_tok[bass.ds(b.n, 1)].rearrange("a p j d -> (a p) j d")).then_inc(x_in[b.par].sem, 16)

            def load_ctx(b):
                sp.dma_start(cs_in[:, b.par, :, :], c_tok[bass.ds(b.n, 1)].rearrange("a p j d -> (a p) j d")
                             ).then_inc(c_in[b.par].sem, 16)

            for n in range(2):
                load_x(Item(0, n))
                load_ctx(Item(0, n))
            for n in range(2, 4):
                sp.wait_ge(x_in[n % 2].sem, x_in[n % 2].upto(0))
                load_x(Item(0, n))
            sp.wait_ge(shared_in.sem, shared_in.upto(0))

            def load_next(b, more=True):
                sp.wait_ge(ctxT_made.sem, ctxT_made.upto(b.n - 2))
                apart(sp)
                sp.wait_ge(v_made.sem, v_made.upto(b.n - 2))
                apart(sp)
                load_ctx(b)
                if more:
                    sp.wait_ge(x_in[b.par].sem, x_in[b.par].upto(b.half))
                    apart(sp)
                    load_x(b + 2)

            with sp.Fori(0, (B - 4) // 2) as i:
                for u in range(2):
                    load_next(Item(i, 2 + u))
            for n in range(B - 2, B):
                load_next(Item(0, n), more=False)

            def load_tile(n, k):
                row = sp.value_load(row_tab[0:1, bass.ds(n, 1)], min_val=0, max_val=DUMP)
                sp.dma_start(xt[:, k, :], routed_x[bass.ds(row, P), :]).then_inc(xt_in[k].sem, 16)

            sp.wait_ge(pads_made.sem, pads_made.upto(0))
            with sp.Fori(0, E // 2) as e:
                row = sp.value_load(pad_tab[0:1, bass.ds(e, 1)], min_val=0, max_val=DUMP - P)
                sp.dma_start(routed_x[bass.ds(row, P), :], zeros[:, :]).then_inc(padded.sem, 16)
            sp.dma_start(routed_x[DUMP:DUMP + P, :], zeros[:, :]).then_inc(padded.sem, 16)

            sp.wait_ge(tables_made.sem, tables_made.upto(0))
            for par in range(2):
                sp.wait_ge(scattered[par].sem, scattered[par].upto(B // 2 - 1))
            sp.wait_ge(padded.sem, padded.upto(3 * E // 4))
            sp.wait_ge(padded_by_pool.sem, padded_by_pool.upto(E // 4 - 1))
            for n in range(XRING):
                load_tile(n, n)
            with sp.Fori(1, TILES // XRING) as lap:
                for k in range(XRING):
                    n = lap * XRING + k
                    sp.wait_ge(xt_turned.sem, xt_turned.upto(n - XRING))
                    apart(sp)
                    load_tile(n, k)

            with sp.Fori(0, NT // 4) as i:
                for k in range(4):
                    n = i * 4 + k
                    sp.wait_ge(fin_made.sem, fin_made.upto(n))
                    sp.dma_start(out_tok[bass.ds(n * P, P), :], fin[k]).then_inc(out_stored[k].sem, 16)
            for k in range(4):
                sp.wait_ge(out_stored[k].sem, out_stored[k].upto(NT // 4 - 1))

        @block.gpsimd
        def _(pool):
            g = nc.gpsimd
            made = [0]

            def const(ins):
                made[0] += 1
                ins.then_inc(pool_const.sem, 1)

            def settle():
                pool.wait_ge(pool_const.sem, made[0])

            def select(ap, fill, op, base, p_step, pattern):
                settle()
                const(g.affine_select(out=ap, in_=ap, compare_op=op, fill=fill, base=base,
                                      pattern=pattern, channel_multiplier=p_step))

            const(g.memset(ident[:], 0.0))
            const(g.memset(gate_wT[:], 0.0))
            const(g.memset(minus_half[:], -0.5))
            const(g.memset(one[:], 1.0))
            select(ident[:], 1.0, ALU.not_equal, 0, 1, [[-1, P]])
            assert made[0] == FIRST_CONSTS
            settle()

            def other_constants():
                const(g.memset(identb[:], 0.0))
                const(g.memset(key_max[:], 0.0))
                const(g.memset(before_b[:], 1.0))
                const(g.memset(ones_b[:], 1.0))
                const(g.memset(mask_b[:], 0.0))
                const(g.memset(head_sel[:], 0.0))
                const(g.memset(v_aug[:], 1.0))
                const(g.memset(taken[:], 0.0))
                const(g.memset(max_parts[:], 0.0))
                select(identb[:], 1.0, ALU.not_equal, 0, 1, [[-1, P]])
                select(before_b[:], 0.0, ALU.is_gt, 0, -1, [[1, P]])
                select(mask_b[:], MASK, ALU.is_ge, 0, -1, [[1, P]])
                for part in range(3):
                    select(head_sel[:], 1.0, ALU.not_equal, -32 * part, 1, [[-1, NH], [0, P]])
                const(g.iota(expert_no[:], pattern=[[1, E]], base=0, channel_multiplier=0,
                             allow_small_or_imprecise_dtypes=True))
                const(g.iota(expert_row[:], pattern=[[CAP, E]], base=0, channel_multiplier=0,
                             allow_small_or_imprecise_dtypes=True))
                const(g.iota(part_no[:], pattern=[[0, 1]], base=0, channel_multiplier=1,
                             allow_small_or_imprecise_dtypes=True))
                assert made[0] == POOL_CONSTS
                settle()

            def load_expert(e, k):
                gu = stage[k][:, 0:DC * 2 * I].rearrange("p (c i) -> p c i", c=DC)
                dn = stage[k][:, DC * 2 * I:EW].rearrange("p (c d) -> p c d", c=IC)
                sides = ((gu[:, :, 0:I], expert_gate, DC), (gu[:, :, I:2 * I], expert_up, DC), (dn, expert_down, IC))
                for to, of, c in sides:
                    src = of[bass.ds(e, 1)].rearrange("a (c p) i -> (a p) c i", p=P)
                    pool.dma_start(to, src).then_inc(expert_dma[k].sem, 16)

            def values(b):
                pool.wait_ge(c_in[b.par].sem, c_in[b.par].upto(b.half))
                pool.wait_ge(pv_made.sem, pv_made.upto(b.n - 2))
                apart(pool)
                g.tensor_copy(v_aug[:, b.par, :, :, 0:DH],
                              cs_in[:, b.par, :, :].rearrange("p j (h d) -> p j h d", h=NH)
                              ).then_inc(v_made.sem, 1)

            def scatter(b):
                pool.wait_ge(slots_made.sem, slots_made.upto(b.n))
                apart(pool)
                for j in range(ST):
                    for k in range(TOPK):
                        c = j * TOPK + k
                        pool.indirect_dma_start(
                            out=routed_x, in_=x2n[:, b.par, j, :], in_offset=None,
                            out_offset=bass.IndirectOffsetOnAxis(ap=slot_u[:, b.par, c:c + 1], axis=0),
                        ).then_inc(scattered[b.par].sem, 16)

            def rstd(b, made, var, to, told):
                pool.wait_ge(made.sem, made.upto(b.n))
                g.tensor_tensor(to[:, :], var[:, :], minus_half[:, :], ALU.pow).then_inc(told.sem, 1)

            def stats(b):
                rstd(b, ln_var_made, ln_var[:, b.par], ln_rstd[:, b.par], ln_rstd_made)

            def h_stats(b):
                rstd(b, h_var_made, h_var, h_rstd, h_rstd_made)

            def x2_stats(b):
                rstd(b, x2_var_made, x2_var, x2_rstd, x2_rstd_made)

            def keep(b, m):
                pool.wait_ge(sh_hi_made.sem, sh_hi_made.upto(b.n, m + 1))
                apart(pool)
                g.tensor_tensor(sh_actT[:, 1, m, :], sh_act[:, m % 2, :], sh_actT[:, 0, m, :], ALU.subtract
                                ).then_inc(sh_lo_made.sem, 1)

            def split_shared():
                pool.wait_ge(weights_in.sem, weights_in.upto(N_SHARED - 1))
                g.tensor_tensor(sh_flat[:, 0, :], sh_in, one[:, :].to_broadcast([P, 2 * EW]), ALU.mult
                                ).then_inc(shared_hi_in.sem, 1)
                pool.wait_ge(shared_hi_in.sem, shared_hi_in.upto(0))
                g.tensor_tensor(sh_flat[:, 1, :], sh_in, sh_flat[:, 0, :], ALU.subtract
                                ).then_inc(shared_in.sem, 1)

            def load_first(e):
                pool.wait_ge(pv_made.sem, pv_made.upto(B - 1))
                if e == 0:
                    pool.wait_ge(x2_made.sem, x2_made.upto(B - 1))
                load_expert(e, e)

            def pad_rows():
                pool.wait_ge(pads_made.sem, pads_made.upto(0))
                with pool.Fori(3 * E // 4, E) as e:
                    row = pool.value_load(pad_tab[0:1, bass.ds(e, 1)], min_val=0, max_val=DUMP - P)
                    pool.dma_start(routed_x[bass.ds(row, P), :], zeros[:, :]).then_inc(padded_by_pool.sem, 16)

            def step(t, ahead=True, front=True, attend=True, route=True, rest=True):
                N, F, A, G, H = t + 2, t + 1, t, t + -1, t + -2
                if rest:
                    keep(H, 1)
                if route:
                    h_stats(G)
                if rest:
                    keep(H, 2)
                if ahead:
                    stats(N)
                if rest:
                    keep(H, 3)
                if route:
                    x2_stats(G)
                if front:
                    values(F)
                if rest and route:
                    scatter(H)
                if route:
                    keep(G, 0)

            def drain(G, H):
                keep(H, 1)
                h_stats(G)
                x2_stats(G)
                keep(H, 2)
                keep(H, 3)
                scatter(H)
                scatter(G)
                keep(G, 0)

            stats(Item(0, 0))
            other_constants()
            step(Item(0, -1), attend=False, route=False, rest=False)
            split_shared()
            step(Item(0, 0), route=False, rest=False)
            step(Item(0, 1), rest=False)
            step(Item(0, 2))
            with pool.Fori(0, (B - 6) // 2) as i:
                step(Item(i, 3))
                step(Item(i, 4))
            step(Item(0, B - 3))
            step(Item(0, B - 2), ahead=False)
            step(Item(0, B - 1), ahead=False, front=False)
            load_first(1)
            drain(Item(0, B - 1), Item(0, B - 2))
            pad_rows()
            load_first(0)
            step(Item(0, B + 1), ahead=False, front=False, attend=False, route=False)

            pool.wait_ge(sh_down_made.sem, sh_down_made.upto(B - 1))
            pool.wait_ge(expert_dma[1].sem, expert_dma[1].upto(0))
            g.tensor_tensor(w_ring[:, 1, 0, :], stage[1], one[:, :].to_broadcast([P, EW]), ALU.mult).then_inc(expert_hi_in.sem, 1)
            pool.wait_ge(expert_hi_in.sem, expert_hi_in.upto(0))
            pool.wait_ge(expert_in.sem, expert_in.upto(0))
            g.tensor_tensor(w_ring[:, 1, 1, :], stage[1], w_ring[:, 1, 0, :], ALU.subtract
                            ).then_inc(expert_in.sem, 1)
            load_expert(2, 0)
            pool.wait_ge(expert_in.sem, expert_in.upto(1))
            load_expert(3, 1)
            pool.wait_ge(tables_made.sem, tables_made.upto(0))

            def split_expert(e, k, lap):
                used = pool.value_load(first_tab[0:1, bass.ds(e - 1, 1)], min_val=0, max_val=TILES)
                pool.wait_ge(y_made.sem, used + y_made.start)
                apart(pool)
                pool.wait_ge(expert_dma[k].sem, expert_dma[k].upto(lap))
                apart(pool)
                g.tensor_tensor(w_ring[:, k, 0, :], stage[k], one[:, :].to_broadcast([P, EW]), ALU.mult).then_inc(expert_hi_in.sem, 1)
                pool.wait_ge(expert_hi_in.sem, expert_hi_in.upto(e - 1))
                apart(pool)
                g.tensor_tensor(w_ring[:, k, 1, :], stage[k], w_ring[:, k, 0, :], ALU.subtract
                                ).then_inc(expert_in.sem, 1)

            with pool.Fori(1, E // 2 - 1) as lap:
                for k in range(2):
                    split_expert(lap * 2 + k, k, lap)
                    pool.wait_ge(expert_in.sem, expert_in.upto(lap * 2 + k))
                    apart(pool)
                    load_expert(lap * 2 + k + 2, k)
            for k in range(2):
                split_expert(E - 2 + k, k, E // 2 - 1)

            for par in range(2):
                pool.wait_ge(y_stored[par].sem, y_stored[par].upto(TILES // 2 - 1))

            def gather(n, k):
                pool.wait_ge(y_at_made.sem, y_at_made.upto(n))
                apart(pool)
                for c in range(TOPK):
                    pool.indirect_dma_start(
                        out=y_in[k][:, c, :], in_=routed_y, out_offset=None,
                        in_offset=bass.IndirectOffsetOnAxis(ap=y_at[:, k, c:c + 1], axis=0),
                    ).then_inc(y_got[k].sem, 16)

            for k in range(4):
                gather(k, k)
            with pool.Fori(1, NT // 4) as i:
                for k in range(4):
                    pool.wait_ge(fin_made.sem, fin_made.upto(i * 4 + k - 4))
                    gather(i * 4 + k, k)

        @block.scalar
        def _(act):
            s = nc.scalar
            small = [
                (gate_rows[0:NH, :], igate_w), (gate_rows[NH:2 * NH, :], fgate_w),
                (router_rows[:, :], router_w),
                (gate_bias[0:NH, :], igate_b.rearrange("(n o) -> n o", o=1)),
                (gate_bias[FG:FG + NH, :], fgate_b.rearrange("(n o) -> n o", o=1)),
                (ln_row[:, :], ln_scale.partition_broadcast(P)),
                (g_col[:, 0:1], g_xattn.partition_broadcast(P)),
                (g_col[:, 1:2], g_ffn.partition_broadcast(P)),
            ]
            assert len(small) == N_SMALL
            for to, of in small:
                act.dma_start(to, of).then_inc(small_in.sem, 16)
            for k, of in enumerate((shared_gate, shared_up, shared_down)):
                to = sh_in[:, k * DC * D:(k + 1) * DC * D].rearrange("p (c i) -> p c i", c=DC)
                act.dma_start(to, of.rearrange("(c p) i -> p c i", p=P)).then_inc(weights_in.sem, 16)
            act.wait_ge(small_in.sem, small_in.upto(N_SMALL - 1))
            s.activation(tanh_g[:, :], g_col[:, :], ACT.Tanh).then_inc(act_const.sem, 1)

            def turn_out(j, to):
                return s.copy(to[:, :, j * P:(j + 1) * P], TP[:, :].rearrange("p (c t) -> p c t", c=DC))

            def turn_ctx(b, j):
                act.wait_ge(ctx_turned.sem, ctx_turned.upto(b.n, j + 1))
                act.wait_ge(qk_made.sem, qk_made.upto(b.n - 2))
                turn_out(j, ctxT[:, b.par]).then_inc(ctxT_made.sem, 1)

            def turn_x(b, j):
                act.wait_ge(xn_turned.sem, xn_turned.upto(b.n, j + 1))
                turn_out(j, xnT[:, b.par]).then_inc(xnT_made.sem, 1)

            def turn(b, j):
                act.wait_ge(x2_turned.sem, x2_turned.upto(b.n, j + 1))
                act.wait_ge(sh_made.sem, sh_made.upto(b.n - 1))
                turn_out(j, x2nT[:, 0]).then_inc(x2nT_made.sem, 1)

            def log_gates(b):
                act.wait_ge(f_abs_made.sem, f_abs_made.upto(b.n))
                s.activation(f_row[FG:, :], f_row[FG:, :], ACT.Exp, scale=-1.0).then_inc(f_exp_made.sem, 1)
                act.wait_ge(f_exp_made.sem, f_exp_made.upto(b.n))
                s.activation(f_row[FG:, :], f_row[FG:, :], ACT.Ln, bias=1.0).then_inc(f_ln_made.sem, 1)

            def columns(b):
                act.wait_ge(key_made.sem, key_made.upto(b.n))
                act.wait_ge(heads_made.sem, heads_made.upto(b.n - 2))
                s.activation(norm_floor[:, b.par], max_log[:, :, :], ACT.Exp, scale=-1.0
                             ).then_inc(floor_made.sem, 1)

            def head(b, h):
                act.wait_ge(key_made.sem, key_made.upto(b.n))
                act.wait_ge(max_spread.sem, max_spread.upto(b.n, h + 1))
                act.wait_ge(c_made.sem, c_made.upto(b.n, h - 1))
                k = h % 2
                s.activation(decay[:, k, 0:S], MB[k][:, 0:S], ACT.Exp,
                             bias=key_log[:, b.par, 0, h:h + 1], scale=-1.0)
                s.activation(decay[:, k, S:TRI], MB[k][:, S:TRI], ACT.Exp,
                             bias=key_log[:, b.par, 1, h:h + 1], scale=-1.0).then_inc(decay_made.sem, 1)

            def top(b):
                act.wait_ge(gap_made.sem, gap_made.upto(b.n))
                s.activation(gap_exp[:, :], gap[:, :], ACT.Exp).then_inc(gap_exp_made.sem, 1)

            def shared(b, m):
                act.wait_ge(sh_made.sem, sh_made.upto(b.n, m + 1))
                act.wait_ge(sh_silu_made.sem, sh_silu_made.upto(b.n, m))
                s.activation(silu_t[:, :], GU[m][:, 0:S], ACT.Tanh, scale=0.5).then_inc(sh_tanh_made.sem, 1)

            def keep(b, m):
                act.wait_ge(sh_act_made.sem, sh_act_made.upto(b.n, m + 1))
                act.wait_ge(sh_down_made.sem, sh_down_made.upto(b.n - 1))
                s.copy(sh_actT[:, 0, m, :], sh_act[:, m % 2, :]).then_inc(sh_hi_made.sem, 1)

            def pad_rows():
                act.wait_ge(pads_made.sem, pads_made.upto(0))
                with act.Fori(E // 2, 3 * E // 4) as e:
                    row = act.value_load(pad_tab[0:1, bass.ds(e, 1)], min_val=0, max_val=DUMP - P)
                    act.dma_start(routed_x[bass.ds(row, P), :], zeros[:, :]).then_inc(padded.sem, 16)

            def step(t, front=True, attend=True, route=True, rest=True):
                F, A, G, H = t + 1, t, t + -1, t + -2
                if attend:
                    head(A, 0)
                if rest:
                    keep(H, 1)
                    shared(H, 2)
                if attend:
                    head(A, 1)
                if front:
                    turn_ctx(F, 0)
                if rest:
                    keep(H, 2)
                    shared(H, 3)
                if attend:
                    head(A, 2)
                if front:
                    turn_ctx(F, 1)
                if rest:
                    keep(H, 3)
                if attend:
                    head(A, 3)
                if front:
                    turn_x(F, 0)
                if attend:
                    head(A, 4)
                if front:
                    turn_x(F, 1)
                if rest and route:
                    top(H)
                if attend:
                    head(A, 5)
                if route:
                    turn(G, 0)
                if attend:
                    head(A, 6)
                if route:
                    turn(G, 1)
                if attend:
                    head(A, 7)
                if front:
                    log_gates(F)
                if route:
                    shared(G, 0)
                    keep(G, 0)
                    shared(G, 1)
                if front:
                    columns(F)

            def drain(G, H):
                keep(H, 1)
                shared(H, 2)
                keep(H, 2)
                top(H)
                shared(H, 3)
                keep(H, 3)
                turn(G, 0)
                turn(G, 1)
                top(G)
                shared(G, 0)
                keep(G, 0)
                shared(G, 1)

            step(Item(0, -1), attend=False, route=False, rest=False)
            step(Item(0, 0), route=False, rest=False)
            step(Item(0, 1), rest=False)
            step(Item(0, 2))
            with act.Fori(0, (B - 6) // 2) as i:
                step(Item(i, 3))
                step(Item(i, 4))
            step(Item(0, B - 3))
            step(Item(0, B - 2))
            step(Item(0, B - 1), front=False)
            drain(Item(0, B - 1), Item(0, B - 2))
            pad_rows()
            step(Item(0, B + 1), front=False, attend=False, route=False)

            act.wait_ge(expert_dma[0].sem, expert_dma[0].upto(0))
            act.wait_ge(sh_made.sem, sh_made.upto(B - 1))
            s.copy(w_ring[:, 0, 0, :], stage[0]).then_inc(expert0_hi_in.sem, 1)

            def copy_x(t):
                act.wait_ge(xt_turned.sem, xt_turned.upto(t.n))
                s.copy(xtT[:, 0, t.par, :], bank[t.par][:, :]).then_inc(xtT_made.sem, 1)

            def tanh_gate(t):
                act.wait_ge(gu_made.sem, gu_made.upto(t.n))
                s.activation(act_t[:, t.par, :], bank[2 + t.par][:, 0:I], ACT.Tanh, scale=0.5
                             ).then_inc(act_tanh_made.sem, 1)

            def copy_y(t):
                act.wait_ge(y_made.sem, y_made.upto(t.n))
                act.wait_ge(y_stored[t.par].sem, y_stored[t.par].upto(t.half - 1))
                s.copy(y_out[:, t.par, :], bank[5 + t.par][:, :]).then_inc(y_copied.sem, 1)

            def store_y(t):
                act.wait_ge(y_copied.sem, y_copied.upto(t.n))
                apart(act)
                act.dma_start(routed_y[bass.ds(t.n * P, P), :], y_out[:, t.par, :]
                              ).then_inc(y_stored[t.par].sem, 16)

            def expert_step(t, before=True, ahead2=True, ahead1=True):
                if ahead2:
                    copy_x(t + 2)
                if before:
                    store_y(t + -1)
                if ahead1:
                    tanh_gate(t + 1)
                copy_y(t)

            copy_x(Item(0, 0))
            copy_x(Item(0, 1))
            tanh_gate(Item(0, 0))
            expert_step(Item(0, 0), before=False)
            expert_step(Item(0, 1))
            with act.Fori(0, (TILES - 4) // 2) as i:
                expert_step(Item(i, 2))
                expert_step(Item(i, 3))
            expert_step(Item(0, TILES - 2), ahead2=False)
            expert_step(Item(0, TILES - 1), ahead2=False, ahead1=False)
            store_y(Item(0, TILES - 1))

        @block.tensor
        def _(pe):
            mm, tr = nc.tensor.matmul, nc.tensor.transpose

            pe.wait_ge(pool_const.sem, FIRST_CONSTS)
            pe.wait_ge(small_in.sem, small_in.upto(N_SMALL - 1))
            for c in range(3 * DC):
                tr(SM[:, c * 16:(c + 1) * 16], gate_rows[:, c * P:(c + 1) * P], ident[0:2 * NH, 0:2 * NH])
            for c in range(DC):
                last = tr(SM[:, (3 * DC + c) * 16:(3 * DC + c + 1) * 16],
                          router_rows[:, c * P:(c + 1) * P], ident[0:E, 0:E])
            last.then_inc(wT_made.sem, 1)
            pe.wait_ge(wT_copied.sem, 7)

            def turn_tile(src):
                for c in range(DC):
                    last = tr(TP[:, c * P:(c + 1) * P], src[:, c * P:(c + 1) * P], ident[:, :])
                return last

            def turn(b, j, front):
                pe.wait_ge(x2n_made.sem, x2n_made.upto(b.n, j + 1))
                pe.wait_ge(x2lo_made.sem, x2lo_made.upto(b.n, j))
                if front:
                    pe.wait_ge(xnT_made.sem, xnT_made.upto(b.n + 2))
                else:
                    pe.wait_ge(xnT_made.sem, xnT_made.upto(B - 1))
                turn_tile(x2n[:, b.par, j, :]).then_inc(x2_turned.sem, 1)

            def turn_ctx(b, j):
                pe.wait_ge(c_in[b.par].sem, c_in[b.par].upto(b.half))
                pe.wait_ge(ctxT_made.sem, ctxT_made.upto(b.n, j))
                pe.wait_ge(xnT_made.sem, xnT_made.upto(b.n - 1))
                pe.wait_ge(x2lo_made.sem, x2lo_made.upto(b.n - 3))
                pe.wait_ge(sh_act_made.sem, sh_act_made.upto(b.n - 3, 2))
                turn_tile(cs_in[:, b.par, j, :]).then_inc(ctx_turned.sem, 1)

            def turn_x(b, j):
                pe.wait_ge(xn_made.sem, xn_made.upto(b.n, j + 1))
                pe.wait_ge(ctxT_made.sem, ctxT_made.upto(b.n))
                pe.wait_ge(xnT_made.sem, xnT_made.upto(b.n, j))
                turn_tile(xn[:, :]).then_inc(xn_turned.sem, 1)

            def gates_pe(b):
                pe.wait_ge(xnT_made.sem, xnT_made.upto(b.n))
                pe.wait_ge(ctxT_made.sem, ctxT_made.upto(b.n))
                pe.wait_ge(key_made.sem, key_made.upto(b.n - 1))
                for c in range(2 * DC):
                    src = (xnT if c < DC else ctxT)[:, b.par, c % DC, :]
                    last = mm(SM[0:FG + NH, 0:S], gate_wT[:, c, :], src, start=(c == 0), stop=(c == 2 * DC - 1))
                last.then_inc(gates_made.sem, 1)

            def columns(b, route):
                pe.wait_ge(pool_const.sem, POOL_CONSTS)
                pe.wait_ge(row_step.sem, row_step.upto(b.n, 5))
                if route:
                    pe.wait_ge(logits_made.sem, logits_made.upto(b.n - 2))
                else:
                    pe.wait_ge(gates_read.sem, gates_read.upto(b.n))
                apart(pe)
                for j in range(ST):
                    last = tr(row_columns[:, j, :], key_max[:, j * P:(j + 1) * P], ident[0:FG + NH, 0:FG + NH])
                last.then_inc(columns_turned.sem, 1)

            def head(b, h):
                k = h % 2
                rows = slice(DH * (h % 2), DH * (h % 2) + DH)
                c = h // 2
                pe.wait_ge(xnT_made.sem, xnT_made.upto(b.n))
                pe.wait_ge(ctxT_made.sem, ctxT_made.upto(b.n))
                pe.wait_ge(row_step.sem, row_step.upto(b.n))
                pe.wait_ge(c_made.sem, c_made.upto(b.n, h - 1))
                pe.wait_ge(decay_made.sem, decay_made.upto(b.n, h - 1))
                mm(QK[k][:, 0:S], ctxT[rows, b.par, c, 0:P], xnT[rows, b.par, c, 0:S],
                   start=True, stop=True)
                mm(QK[k][:, S:TRI], ctxT[rows, b.par, c, P:S], xnT[rows, b.par, c, P:S],
                   start=True, stop=True).then_inc(qk_made.sem, 1)
                for at, n in ((0, S), (S, P)):
                    mm(MB[k][:, at:at + n], head_sel[0:96, h, :], max_parts[0:96, b.par, S - n:S],
                       start=True, stop=False)
                    last = mm(MB[k][:, at:at + P], identb[:, :], mask_b[:, :], start=False, stop=True)
                last.then_inc(max_spread.sem, 1)

            def pv(b, h):
                k = h % 2
                pe.wait_ge(c_made.sem, c_made.upto(b.n, h + 1))
                pe.wait_ge(v_made.sem, v_made.upto(b.n))
                if h % 2 == 0:
                    pe.wait_ge(heads_made.sem, heads_made.upto(b.n, h // 2))
                r = 2 * k * VW
                mm(HO[:, r:r + VW], cmat[:, k, 0:P], v_aug[:, b.par, 0, h, :], start=True, stop=True)
                mm(HO[:, r + VW:r + 2 * VW], cmat[:, k, P:S], v_aug[:, b.par, 0, h, :],
                   start=True, stop=False)
                mm(HO[:, r + VW:r + 2 * VW], cmat[:, k, S:TRI], v_aug[:, b.par, 1, h, :],
                   start=False, stop=True).then_inc(pv_made.sem, 1)

            def rank(b, front, attend):
                pe.wait_ge(chosen_made.sem, chosen_made.upto(b.n, 2))
                if front:
                    pe.wait_ge(gates_read.sem, gates_read.upto(b.n + 3))
                elif attend:
                    pe.wait_ge(key_made.sem, key_made.upto(b.n + 2))
                mm(SM[:, 0:E], before_b[:, :], chosen[:, 0, :], start=True, stop=False)
                mm(SM[:, 0:E], ones_b[:, :], taken[:, b.par, :], start=False, stop=True)
                mm(SM[:, E:2 * E], before_b[:, :], chosen[:, 1, :], start=True, stop=False)
                mm(SM[:, E:2 * E], ones_b[:, :], taken_mid[:, :], start=False, stop=True
                   ).then_inc(ranks_made.sem, 1)

            def router(b, front):
                pe.wait_ge(x2lo_made.sem, x2lo_made.upto(b.n))
                pe.wait_ge(place_step.sem, place_step.upto(b.n - 1, 1))
                if front:
                    pe.wait_ge(gates_read.sem, gates_read.upto(b.n + 2))
                for c in range(DC):
                    for p, (w_part, x_part) in enumerate(PARTS):
                        last = mm(SM[:, 0:S], router_wT[:, w_part, c, :], x2nT[:, x_part, c, :],
                                  start=(c + p == 0), stop=(c == DC - 1 and p == 2))
                last.then_inc(router_made.sem, 1)

            def logits_pe(b):
                pe.wait_ge(logit_row_made.sem, logit_row_made.upto(b.n))
                apart(pe)
                for j in range(ST):
                    last = tr(SM[:, j * E:(j + 1) * E], logit_row[:, j * P:(j + 1) * P], ident[0:E, 0:E])
                last.then_inc(logits_turned.sem, 1)

            def shared(b, m):
                pe.wait_ge(shared_in.sem, shared_in.upto(0))
                pe.wait_ge(x2lo_made.sem, x2lo_made.upto(b.n))
                if m == 0:
                    pe.wait_ge(base_made.sem, base_made.upto(b.n - 1))
                elif m > 1:
                    pe.wait_ge(sh_act_made.sem, sh_act_made.upto(b.n, 1 if m == 2 else 3))
                for at, w in ((0, sh_gate), (S, sh_up)):
                    for c in range(DC):
                        for p, (w_part, x_part) in enumerate(PARTS):
                            last = mm(GU[m][:, at:at + S], w[:, w_part, c, m * P:(m + 1) * P], x2nT[:, x_part, c, :],
                                      start=(c + p == 0), stop=(c == DC - 1 and p == 2))
                last.then_inc(sh_made.sem, 1)

            def shared_down(b, j):
                pe.wait_ge(sh_act_made.sem, sh_act_made.upto(b.n))
                if j:
                    pe.wait_ge(base_made.sem, base_made.upto(b.n, j))
                for m in range(SC):
                    pe.wait_ge(sh_lo_made.sem, sh_lo_made.upto(b.n, m + 1))
                    for p, (w_part, x_part) in enumerate(PARTS):
                        last = mm(FF[:, :], sh_actT[:, x_part, m, j * P:(j + 1) * P], sh_down[:, w_part, m, :],
                                  start=(m + p == 0), stop=(m == SC - 1 and p == 2))
                last.then_inc(sh_down_made.sem, 1)

            def count_rows(b):
                pe.wait_ge(chosen_made.sem, chosen_made.upto(B - 1))
                pe.wait_ge(place_step.sem, place_step.upto(B - 1, 1))
                mm(SM[:, 0:E], ones_b[:, :], taken[:, B % 2, :], start=True, stop=True).then_inc(counts_made.sem, 1)

            def step(t, front=True, attend=True, route=True, rest=True):
                F, A, G, H = t + 1, t, t + -1, t + -2
                if attend:
                    head(A, 0)
                if rest:
                    shared(H, 2)
                if attend:
                    head(A, 1)
                    pv(A, 0)
                if front:
                    turn_ctx(F, 0)
                if rest:
                    shared(H, 3)
                if attend:
                    head(A, 2)
                    pv(A, 1)
                if front:
                    turn_ctx(F, 1)
                if rest:
                    shared_down(H, 0)
                if attend:
                    head(A, 3)
                if front:
                    turn_x(F, 0)
                if attend:
                    pv(A, 2)
                    head(A, 4)
                if front:
                    turn_x(F, 1)
                if attend:
                    pv(A, 3)
                if rest:
                    shared_down(H, 1)
                if front:
                    gates_pe(F)
                if attend:
                    head(A, 5)
                if route:
                    turn(G, 0, front)
                if attend:
                    pv(A, 4)
                    head(A, 6)
                if route:
                    turn(G, 1, front)
                if rest and route:
                    rank(H, front, attend)
                if attend:
                    pv(A, 5)
                    head(A, 7)
                if route:
                    router(G, front)
                    shared(G, 0)
                    logits_pe(G)
                if attend:
                    pv(A, 6)
                if route:
                    shared(G, 1)
                if front:
                    columns(F, route)
                if attend:
                    pv(A, 7)

            def drain(G, H):
                shared(H, 2)
                shared(H, 3)
                turn(G, 0, False)
                shared_down(H, 0)
                turn(G, 1, False)
                rank(H, False, False)
                router(G, False)
                shared_down(H, 1)
                logits_pe(G)
                rank(G, False, False)
                count_rows(G)
                shared(G, 0)
                shared(G, 1)

            step(Item(0, -1), attend=False, route=False, rest=False)
            step(Item(0, 0), route=False, rest=False)
            step(Item(0, 1), rest=False)
            step(Item(0, 2))
            with pe.Fori(0, (B - 6) // 2) as i:
                step(Item(i, 3))
                step(Item(i, 4))
            step(Item(0, B - 3))
            step(Item(0, B - 2))
            step(Item(0, B - 1), front=False)
            drain(Item(0, B - 1), Item(0, B - 2))
            pe.wait_ge(table_step.sem, TABLE_STEPS)
            tr(SM[0:1, 0:P], tile_info[:, 2:3], ident[:, :])
            tr(SM[0:1, P:2 * P], tile_info[:, 3:4], ident[:, :]).then_inc(tables_turned.sem, 1)

            step(Item(0, B + 1), front=False, attend=False, route=False)

            def turn_rows(n, t, k):
                pe.wait_ge(xt_in[k].sem, n)
                pe.wait_ge(xt_lo_made.sem, xt_lo_made.upto(t.n - 2))
                for c in range(DC):
                    last = tr(bank[t.par][:, c * P:(c + 1) * P], xt[:, k, c * P:(c + 1) * P], ident[:, :])
                last.then_inc(xt_turned.sem, 1)

            def expert_of(t):
                return pe.value_load(expert_tab[0:1, bass.ds(t.n, 1)], min_val=0, max_val=E - 1)

            def gate_up(t, e, slot):
                pe.wait_ge(expert_in.sem, e + 1)
                pe.wait_ge(xt_lo_made.sem, xt_lo_made.upto(t.n))
                pe.wait_ge(act_made.sem, act_made.upto(t.n - 2))
                for c in range(DC):
                    for p, (w_part, x_part) in enumerate(PARTS):
                        last = mm(bank[2 + t.par][:, :], xtT[:, x_part, t.par, c * P:(c + 1) * P],
                                  w_gu[:, bass.ds(slot, 1), w_part, c, :].rearrange("p a i -> p (a i)"),
                                  start=(c + p == 0), stop=(c == DC - 1 and p == 2))
                last.then_inc(gu_made.sem, 1)

            def turn_act(t):
                pe.wait_ge(act_made.sem, act_made.upto(t.n))
                pe.wait_ge(actT_made.sem, actT_made.upto(t.n - 1))
                for c in range(IC):
                    last = tr(bank[4][:, c * P:(c + 1) * P], act_a[:, t.par, c * P:(c + 1) * P], ident[:, :])
                last.then_inc(act_turned.sem, 1)

            def down(t):
                slot = pe.snap(expert_of(t) % RING)
                pe.wait_ge(actT_made.sem, actT_made.upto(t.n))
                pe.wait_ge(y_copied.sem, y_copied.upto(t.n - 2))
                for c in range(IC):
                    for p, (w_part, x_part) in enumerate(PARTS):
                        last = mm(bank[5 + t.par][:, :], act_aT[:, x_part, t.par, c * P:(c + 1) * P],
                                  w_dn[:, bass.ds(slot, 1), w_part, c, :].rearrange("p a i -> p (a i)"),
                                  start=(c + p == 0), stop=(c == IC - 1 and p == 2))
                last.then_inc(y_made.sem, 1)

            def expert_step(t, k, lap, ahead2=True, ahead1=True):
                if ahead1:
                    e = expert_of(t + 1)
                    slot = pe.snap(e % RING)
                if ahead2:
                    turn_rows(lap * 16 + 16, t + 2, k)
                turn_act(t)
                if ahead1:
                    gate_up(t + 1, e, slot)
                down(t)

            pe.sem_inc(y_made.sem, y_made.start)
            pe.wait_ge(tables_made.sem, tables_made.upto(0))
            turn_rows(16, Item(0, 0), 0)
            turn_rows(16, Item(0, 1), 1)
            e = expert_of(Item(0, 0))
            gate_up(Item(0, 0), e, pe.snap(e % RING))
            expert_step(Item(0, 0), 2, 0)
            expert_step(Item(0, 1), 3, 0)
            with pe.Fori(0, (TILES - 4) // 4) as i:
                for u in range(4):
                    expert_step(Item(i * 2, 2 + u), u, i + 1)
            for n in range(TILES - 2, TILES):
                expert_step(Item(0, n), 0, 0, ahead2=False, ahead1=n + 1 < TILES)

        @block.vector
        def _(dve):
            v = nc.vector

            pe_w = SM[:, 0:(3 * DC + DC) * 16].rearrange("p (c n) -> p c n", n=16)
            dve.wait_ge(wT_made.sem, 1)
            for k in range(2):
                v.tensor_copy(gate_wT[:, :, k * FG:k * FG + NH], pe_w[:, 0:2 * DC, k * NH:(k + 1) * NH]
                              ).then_inc(wT_copied.sem, 1)
            v.memset(router_wT[:, :, :, :].bitcast(F32), 0.0).then_inc(wT_copied.sem, 1)
            dve.wait_ge(wT_copied.sem, 3)
            v.tensor_copy(router_wT[:, 0, :, 0:E], pe_w[:, 3 * DC:4 * DC, :]).then_inc(wT_copied.sem, 1)
            dve.wait_ge(wT_copied.sem, 4)
            v.tensor_tensor(router_wT[:, 1, :, 0:E], pe_w[:, 3 * DC:4 * DC, :], router_wT[:, 0, :, 0:E], ALU.subtract
                            ).then_inc(wT_copied.sem, 1)
            for k in range(2):
                both = gate_wT[:, DC:2 * DC, k * FG:k * FG + NH]
                v.tensor_tensor(both, pe_w[:, 2 * DC:3 * DC, k * NH:(k + 1) * NH], both, ALU.add
                                ).then_inc(wT_copied.sem, 1)
            dve.wait_ge(act_const.sem, 1)
            v.tensor_scalar(ln_row[:, :], ln_row[:, :], tanh_g[:, 0:1], None, ALU.mult
                            ).then_inc(wT_copied.sem, 1)
            dve.wait_ge(wT_copied.sem, 8)
            dve.wait_ge(pool_const.sem, FIRST_CONSTS)

            def base_tile(b, j):
                return base_out[:, bass.ds(b.n * ST + j, 1), :].rearrange("p a d -> p (a d)")

            def stats(b):
                dve.wait_ge(x_in[b.par].sem, x_in[b.par].upto(b.half))
                apart(dve)
                for j in range(ST):
                    v.bn_stats(ln_stat[:, j, :], base_tile(b, j)).then_inc(ln_step.sem, 1)
                for j in range(ST):
                    dve.wait_ge(ln_step.sem, ln_step.upto(b.n, j + 1))
                    apart(dve)
                    v.bn_aggr(ln_mv[:, b.par, j, :], ln_stat[:, j, :]).then_inc(ln_step.sem, 1)
                dve.wait_ge(ln_step.sem, ln_step.upto(b.n))
                v.tensor_scalar(ln_var[:, b.par], ln_mv[:, b.par, :, 1], LN_EPS, None, ALU.add
                                ).then_inc(ln_var_made.sem, 1)

            def norm_front(b, j):
                dve.wait_ge(ln_rstd_made.sem, ln_rstd_made.upto(b.n))
                dve.wait_ge(xn_turned.sem, xn_turned.upto(b.n, j))
                v.tensor_scalar(xn[:, :], base_tile(b, j), ln_mv[:, b.par, j, 0:1], ln_rstd[:, b.par, j:j + 1],
                                ALU.subtract, ALU.mult).then_inc(xn_made.sem, 1)

            def read_gates(b):
                dve.wait_ge(gates_made.sem, gates_made.upto(b.n))
                for k in range(2):
                    rows = slice(k * FG, k * FG + NH)
                    v.tensor_scalar(gates[rows, :], SM[rows, 0:S], gate_bias[rows, :], None, ALU.add
                                    ).then_inc(gates_read.sem, 1)
                dve.wait_ge(gates_read.sem, gates_read.upto(b.n))
                v.scalar_tensor_tensor(f_row[FG:, :], gates[FG:, :], -1.0, gates[FG:, :], ALU.mult, ALU.max
                                       ).then_inc(f_abs_made.sem, 1)

            def rows(b):
                dve.wait_ge(pool_const.sem, POOL_CONSTS)
                dve.wait_ge(f_ln_made.sem, f_ln_made.upto(b.n))
                v.scalar_tensor_tensor(f_row[FG:, :], gates[FG:, :], 0.0, f_row[FG:, :],
                                       ALU.min, ALU.subtract).then_inc(row_step.sem, 1)
                dve.wait_ge(row_step.sem, row_step.upto(b.n, 1))
                v.tensor_tensor_scan(cum_row[:, :], one[FG:FG + NH, :].to_broadcast([NH, S]), f_row[FG:, :],
                                     0.0, ALU.mult, ALU.add).then_inc(row_step.sem, 1)
                dve.wait_ge(row_step.sem, row_step.upto(b.n, 2))
                v.tensor_tensor(key_max[0:NH, :], gates[0:NH, :], cum_row[:, :], ALU.subtract
                                ).then_inc(row_step.sem, 1)
                dve.wait_ge(row_step.sem, row_step.upto(b.n, 3))
                v.tensor_tensor_scan(max_row[:, :], key_max[0:NH, :], key_max[0:NH, :], -3.0e38,
                                     ALU.max, ALU.max).then_inc(row_step.sem, 1)
                dve.wait_ge(row_step.sem, row_step.upto(b.n, 4))
                v.tensor_tensor(key_max[FG:, :], max_row[:, :], cum_row[:, :], ALU.add
                                ).then_inc(row_step.sem, 1)
                dve.wait_ge(max_spread.sem, max_spread.upto(b.n - 2))
                v.tensor_copy(max_parts[0:NH, b.par, :], max_row[:, :]).then_inc(row_step.sem, 1)
                dve.wait_ge(row_step.sem, row_step.upto(b.n, 6))
                v.tensor_tensor(max_rest[:, :], max_row[:, :], max_parts[0:NH, b.par, :], ALU.subtract
                                ).then_inc(row_step.sem, 1)
                dve.wait_ge(row_step.sem, row_step.upto(b.n, 7))
                v.tensor_copy(max_mid[:, :], max_rest[:, :]).then_inc(row_step.sem, 1)
                dve.wait_ge(row_step.sem, row_step.upto(b.n, 8))
                v.tensor_copy(max_parts[32:32 + NH, b.par, :], max_mid[:, :]).then_inc(row_step.sem, 1)
                v.tensor_tensor(max_parts[64:64 + NH, b.par, :], max_rest[:, :], max_mid[:, :],
                                ALU.subtract).then_inc(row_step.sem, 1)

            def columns(b):
                dve.wait_ge(columns_turned.sem, columns_turned.upto(b.n))
                dve.wait_ge(decay_made.sem, decay_made.upto(b.n - 2))
                v.tensor_copy(key_log[:, b.par], row_columns[:, :, 0:NH]).then_inc(key_made.sem, 1)
                v.tensor_copy(max_log[:, :, :], row_columns[:, :, FG:]).then_inc(key_made.sem, 1)

            def head(b, h):
                k = h % 2
                dve.wait_ge(qk_made.sem, qk_made.upto(b.n, h + 1))
                dve.wait_ge(decay_made.sem, decay_made.upto(b.n, h + 1))
                dve.wait_ge(pv_made.sem, pv_made.upto(b.n, h - 1))
                v.scalar_tensor_tensor(cmat[:, k, :], QK[k][:, 0:TRI], QK_SCALE, decay[:, k, :],
                                       ALU.mult, ALU.mult).then_inc(c_made.sem, 1)

            def out_pair(b, q):
                dve.wait_ge(pv_made.sem, pv_made.upto(b.n, 2 * q + 2))
                dve.wait_ge(floor_made.sem, floor_made.upto(b.n))
                pair = HO[:, 0:2 * ST * VW].rearrange("p (h j w) -> p h j w", h=2, w=VW)
                v.scalar_tensor_tensor(norm[:, :, :], pair[:, :, :, DH], -1.0,
                                       norm_floor[:, b.par, :, 2 * q:2 * q + 2].rearrange("p j h -> p h j"),
                                       ALU.mult, ALU.max).then_inc(norm_step.sem, 1)
                dve.wait_ge(norm_step.sem, norm_step.upto(b.n, 4 * q + 1))
                v.tensor_tensor(norm_abs[:, :, :], pair[:, :, :, DH], norm[:, :, :], ALU.max
                                ).then_inc(norm_step.sem, 1)
                dve.wait_ge(norm_step.sem, norm_step.upto(b.n, 4 * q + 2))
                v.tensor_scalar(norm_e[:, :, :], norm_abs[:, :, :], NORM_EPS, None, ALU.add
                                ).then_inc(norm_step.sem, 1)
                dve.wait_ge(norm_step.sem, norm_step.upto(b.n, 4 * q + 3))
                v.reciprocal(norm_inv[:, :, :], norm_e[:, :, :]).then_inc(norm_step.sem, 1)
                dve.wait_ge(norm_step.sem, norm_step.upto(b.n, 4 * q + 4))
                v.tensor_tensor(
                    heads[:, :, 2 * q * DH:(2 * q + 2) * DH].rearrange("p j (h d) -> p h j d", h=2),
                    pair[:, :, :, 0:DH], norm_inv[:, :, :].unsqueeze(3).to_broadcast([P, 2, ST, DH]),
                    ALU.mult).then_inc(heads_made.sem, 1)

            def h_stats(b):
                dve.wait_ge(heads_made.sem, heads_made.upto(b.n))
                apart(dve)
                for j in range(ST):
                    v.bn_stats(h_stat[:, j, :], heads[:, j, :]).then_inc(post_step.sem, 1)
                for j in range(ST):
                    dve.wait_ge(post_step.sem, post_step.upto(b.n, j + 1))
                    apart(dve)
                    v.bn_aggr(h_mv[:, j, :], h_stat[:, j, :]).then_inc(post_step.sem, 1)
                dve.wait_ge(post_step.sem, post_step.upto(b.n, 2 * ST))
                v.tensor_scalar(h_var[:, :], h_mv[:, :, 1], LN_EPS, None, ALU.add).then_inc(h_var_made.sem, 1)

            def center(b):
                for j in range(ST):
                    v.scalar_tensor_tensor(heads[:, j, :], heads[:, j, :], h_mv[:, j, 0:1], ln_row[:, :],
                                           ALU.subtract, ALU.mult).then_inc(post_step.sem, 1)

            def x2_add(b):
                dve.wait_ge(post_step.sem, post_step.upto(b.n, 3 * ST))
                dve.wait_ge(h_rstd_made.sem, h_rstd_made.upto(b.n))
                for j in range(ST):
                    v.scalar_tensor_tensor(base_tile(b, j), heads[:, j, :], h_rstd[:, j:j + 1],
                                           base_tile(b, j), ALU.mult, ALU.add
                                           ).then_inc(x2_made.sem, 1)

            def x2_stats(b):
                for j in range(ST):
                    dve.wait_ge(x2_made.sem, x2_made.upto(b.n, j + 1))
                    apart(dve)
                    v.bn_stats(x2_stat[:, j, :], base_tile(b, j)).then_inc(post_step.sem, 1)
                for j in range(ST):
                    dve.wait_ge(post_step.sem, post_step.upto(b.n, 3 * ST + j + 1))
                    apart(dve)
                    v.bn_aggr(x2_mv[:, j, :], x2_stat[:, j, :]).then_inc(post_step.sem, 1)
                dve.wait_ge(post_step.sem, post_step.upto(b.n))
                v.tensor_scalar(x2_var[:, :], x2_mv[:, :, 1], LN_EPS, None, ALU.add
                                ).then_inc(x2_var_made.sem, 1)

            def post_norm(b):
                dve.wait_ge(x2_rstd_made.sem, x2_rstd_made.upto(b.n))
                dve.wait_ge(scattered[b.par].sem, scattered[b.par].upto(b.half - 1))
                for j in range(ST):
                    v.tensor_scalar(x2n[:, b.par, j, :], base_tile(b, j), x2_mv[:, j, 0:1],
                                    x2_rstd[:, j:j + 1], ALU.subtract, ALU.mult).then_inc(x2n_made.sem, 1)

            def router(b):
                dve.wait_ge(router_made.sem, router_made.upto(b.n))
                v.tensor_copy(logit_row[:, :], SM[0:E, 0:S]).then_inc(logit_row_made.sem, 1)

            def keep_logits(b):
                dve.wait_ge(logits_turned.sem, logits_turned.upto(b.n))
                v.tensor_copy(logits[:, :, :], SM[:, 0:ST * E].rearrange("p (j n) -> p j n", j=ST)
                              ).then_inc(logits_made.sem, 1)

            def top(b):
                dve.wait_ge(logits_made.sem, logits_made.upto(b.n))
                apart(dve)
                for j in range(ST):
                    v.max(top8[:, j, :], logits[:, j, :]).then_inc(top_step.sem, 1)
                    dve.wait_ge(top_step.sem, top_step.upto(b.n, 2 * j + 1))
                    apart(dve)
                    v.max_index(top8_at[:, j, :], top8[:, j, :], logits[:, j, :]).then_inc(top_step.sem, 1)
                v.tensor_tensor(gap[:, :], top8[:, :, 1], top8[:, :, 0], ALU.subtract
                                ).then_inc(gap_made.sem, 1)
                dve.wait_ge(top_step.sem, top_step.upto(b.n, 2 * ST))
                v.tensor_copy(top_at[:, :, :], top8_at[:, :, 0:TOPK]).then_inc(top_step.sem, 1)
                dve.wait_ge(top_step.sem, top_step.upto(b.n, 2 * ST + 1))
                for j in range(ST):
                    for k in range(TOPK):
                        v.tensor_scalar(one_hot[:, j, k, :], expert_no[:, :], top_at[:, j, k:k + 1], None,
                                        ALU.is_equal).then_inc(hot_made.sem, 1)
                dve.wait_ge(hot_made.sem, hot_made.upto(b.n))
                v.tensor_tensor(chosen[:, :, :], one_hot[:, :, 0, :], one_hot[:, :, 1, :], ALU.add
                                ).then_inc(chosen_made.sem, 1)
                dve.wait_ge(chosen_made.sem, chosen_made.upto(b.n, 1))
                v.tensor_tensor(taken_mid[:, :], taken[:, b.par, :], chosen[:, 0, :], ALU.add
                                ).then_inc(chosen_made.sem, 1)
                dve.wait_ge(chosen_made.sem, chosen_made.upto(b.n, 2))
                dve.wait_ge(ranks_made.sem, ranks_made.upto(b.n - 1))
                v.tensor_tensor(taken[:, 1 - b.par, :], taken_mid[:, :], chosen[:, 1, :], ALU.add
                                ).then_inc(chosen_made.sem, 1)
                dve.wait_ge(gap_exp_made.sem, gap_exp_made.upto(b.n))
                v.tensor_scalar(gap_den[:, :], gap_exp[:, :], 1.0, None, ALU.add).then_inc(w_step.sem, 1)
                dve.wait_ge(w_step.sem, w_step.upto(b.n, 1))
                v.reciprocal(top_w[:, :, 0], gap_den[:, :]).then_inc(w_step.sem, 1)
                dve.wait_ge(w_step.sem, w_step.upto(b.n, 2))
                v.tensor_tensor(top_w[:, :, 1], top_w[:, :, 0], gap_exp[:, :], ALU.mult
                                ).then_inc(w_step.sem, 1)
                dve.wait_ge(w_step.sem, w_step.upto(b.n, 3))
                v.tensor_scalar(all_w[:, bass.ds(b.n, 1), :].rearrange("p a n -> p (a n)"),
                                top_w[:, :, :].rearrange("p j k -> p (j k)"), tanh_g[:, 1:2], None,
                                ALU.mult).then_inc(route_kept.sem, 1)
                v.tensor_copy(all_hot[:, bass.ds(b.n, 1)].rearrange("p a n e -> p (a n e)"),
                              one_hot[:, :, :, :].rearrange("p j k e -> p (j k e)")
                              ).then_inc(route_kept.sem, 1)

            def rank(b):
                dve.wait_ge(ranks_made.sem, ranks_made.upto(b.n))
                v.tensor_tensor(place[:, :, :], SM[:, 0:ST * E].rearrange("p (j n) -> p j n", j=ST),
                                expert_row[:, :].unsqueeze(1).to_broadcast([P, ST, E]), ALU.add
                                ).then_inc(place_step.sem, 1)
                dve.wait_ge(place_step.sem, place_step.upto(b.n, 1))
                v.tensor_tensor(place_pick[:, :, :].rearrange("p (j k) e -> p j k e", j=ST), one_hot[:, :, :, :],
                                place[:, :, :].unsqueeze(2).to_broadcast([P, ST, TOPK, E]), ALU.mult
                                ).then_inc(place_step.sem, 1)
                dve.wait_ge(place_step.sem, place_step.upto(b.n, 2))
                v.tensor_reduce(slot_f[:, :], place_pick[:, :, :], AX_X, ALU.add).then_inc(place_step.sem, 1)
                dve.wait_ge(place_step.sem, place_step.upto(b.n, 3))
                dve.wait_ge(scattered[b.par].sem, scattered[b.par].upto(b.half - 1))
                v.tensor_copy(slot_u[:, b.par, :], slot_f[:, :]).then_inc(slots_made.sem, 1)
                v.tensor_copy(all_slot[:, bass.ds(b.n, 1), :].rearrange("p a n -> p (a n)"), slot_f[:, :]
                              ).then_inc(route_kept.sem, 1)

            def shared(b, m):
                dve.wait_ge(sh_tanh_made.sem, sh_tanh_made.upto(b.n, m + 1))
                dve.wait_ge(sh_lo_made.sem, sh_lo_made.upto(b.n, m - 1))
                v.scalar_tensor_tensor(sh_act[:, m % 2, :], silu_t[:, :], 1.0, GU[m][:, 0:S], ALU.add, ALU.mult
                                       ).then_inc(sh_silu_made.sem, 1)
                dve.wait_ge(sh_silu_made.sem, sh_silu_made.upto(b.n, m + 1))
                v.scalar_tensor_tensor(sh_act[:, m % 2, :], sh_act[:, m % 2, :], 0.5, GU[m][:, S:2 * S],
                                       ALU.mult, ALU.mult).then_inc(sh_act_made.sem, 1)

            def turn(b, j):
                dve.wait_ge(x2nT_made.sem, x2nT_made.upto(b.n, j + 1))
                own = x2nT[:, :, :, j * P:(j + 1) * P]
                v.tensor_tensor(own[:, 1], TP[:, :].rearrange("p (c t) -> p c t", c=DC), own[:, 0], ALU.subtract
                                ).then_inc(x2lo_made.sem, 1)

            def shared_down(b, j):
                dve.wait_ge(sh_down_made.sem, sh_down_made.upto(b.n, j + 1))
                v.scalar_tensor_tensor(base_tile(b, j), FF[:, :], tanh_g[:, 1:2], base_tile(b, j),
                                       ALU.mult, ALU.add
                                       ).then_inc(base_made.sem, 1)

            steps = [0]

            def then(ins):
                steps[0] += 1
                ins.then_inc(table_step.sem, 1)
                dve.wait_ge(table_step.sem, steps[0])

            def count_rows(b):
                then(v.memset(zeros, 0.0))
                dve.wait_ge(counts_made.sem, counts_made.upto(0))
                then(v.tensor_copy(count[:, :], SM[:, 0:E]))
                then(v.tensor_tensor(pad_f[:, :], count[:, :], expert_row[:, :], ALU.add))
                v.tensor_copy(pad_tab[:, :], pad_f[0:1, :]).then_inc(pads_made.sem, 1)

            def step(t, ahead=True, front=True, attend=True, route=True, rest=True):
                N, F, A, G, H = t + 2, t + 1, t, t + -1, t + -2
                if attend:
                    head(A, 0)
                if route:
                    h_stats(G)
                if rest:
                    shared(H, 2)
                if attend:
                    head(A, 1)
                if route:
                    center(G)
                if ahead:
                    stats(N)
                if rest:
                    shared(H, 3)
                if attend:
                    head(A, 2)
                if front:
                    norm_front(F, 0)
                if route:
                    x2_add(G)
                if attend:
                    out_pair(A, 0)
                if rest:
                    shared_down(H, 0)
                if attend:
                    head(A, 3)
                if front:
                    norm_front(F, 1)
                if route:
                    x2_stats(G)
                if attend:
                    head(A, 4)
                    out_pair(A, 1)
                if route:
                    post_norm(G)
                if rest and route:
                    top(H)
                if rest:
                    shared_down(H, 1)
                if attend:
                    head(A, 5)
                if route:
                    turn(G, 0)
                if front:
                    read_gates(F)
                if attend:
                    head(A, 6)
                if route:
                    turn(G, 1)
                if rest and route:
                    rank(H)
                if attend:
                    head(A, 7)
                    out_pair(A, 2)
                if route:
                    router(G)
                if front:
                    rows(F)
                if route:
                    shared(G, 0)
                    keep_logits(G)
                    shared(G, 1)
                if front:
                    columns(F)
                if attend:
                    out_pair(A, 3)

            def drain(G, H):
                h_stats(G)
                shared(H, 2)
                center(G)
                x2_add(G)
                x2_stats(G)
                top(H)
                shared(H, 3)
                post_norm(G)
                turn(G, 0)
                shared_down(H, 0)
                turn(G, 1)
                rank(H)
                router(G)
                shared_down(H, 1)
                keep_logits(G)
                top(G)
                rank(G)
                count_rows(G)
                shared(G, 0)
                shared(G, 1)

            stats(Item(0, 0))
            step(Item(0, -1), attend=False, route=False, rest=False)
            step(Item(0, 0), route=False, rest=False)
            step(Item(0, 1), rest=False)
            step(Item(0, 2))
            with dve.Fori(0, (B - 6) // 2) as i:
                step(Item(i, 3))
                step(Item(i, 4))
            step(Item(0, B - 3))
            step(Item(0, B - 2), ahead=False)
            step(Item(0, B - 1), ahead=False, front=False)
            drain(Item(0, B - 1), Item(0, B - 2))
            then(v.tensor_scalar(count_i[:, :], count[:, :], float(P - 1), None, ALU.add))
            then(v.tensor_scalar(tiles_i[:, :], count_i[:, :], P.bit_length() - 1, None,
                                 ALU.arith_shift_right))
            then(v.tensor_copy(tiles_f[:, :], tiles_i[:, :]))
            then(v.tensor_tensor_scan(tile_end[:, :], tiles_f[:, :], zeros[:, 0:E], 0.0, ALU.add, ALU.add))
            then(v.tensor_tensor(tile_first[:, :], tile_end[:, :], tiles_f[:, :], ALU.subtract))
            then(v.tensor_scalar(ended[:, :], tile_end[:, :], part_no[:, 0:1], None, ALU.is_le))
            then(v.tensor_reduce(tile_info[:, 0:1], ended[:, :], AX_X, ALU.add))
            then(v.tensor_tensor(ended_at[:, :], ended[:, :], tile_end[:, :], ALU.mult))
            then(v.tensor_reduce(tile_info[:, 1:2], ended_at[:, :], AX_X, ALU.max))
            then(v.tensor_tensor(tile_info[:, 1:2], part_no[:, 0:1], tile_info[:, 1:2], ALU.subtract))
            then(v.tensor_scalar(tile_info[:, 1:2], tile_info[:, 1:2], float(P), None, ALU.mult))
            then(v.tensor_scalar(tile_info[:, 2:3], tile_info[:, 0:1], float(CAP), tile_info[:, 1:2],
                                 ALU.mult, ALU.add))
            then(v.tensor_scalar(tile_info[:, 2:3], tile_info[:, 2:3], float(DUMP), None, ALU.min))
            then(v.tensor_scalar(tile_info[:, 3:4], tile_info[:, 0:1], float(E - 1), None, ALU.min))
            assert steps[0] == TABLE_STEPS
            v.tensor_copy(first_tab[:, :], tile_first[0:1, :])
            dve.wait_ge(tables_turned.sem, tables_turned.upto(0))
            v.tensor_copy(row_tab[:, :], SM[0:1, 0:P])
            v.tensor_copy(expert_tab[:, :], SM[0:1, P:2 * P]).then_inc(tables_made.sem, 1)

            step(Item(0, B + 1), ahead=False, front=False, attend=False, route=False)

            dve.wait_ge(expert0_hi_in.sem, expert0_hi_in.upto(0))
            v.tensor_tensor(w_ring[:, 0, 1, :], stage[0], w_ring[:, 0, 0, :], ALU.subtract
                            ).then_inc(expert_in.sem, 1)

            def silu(t):
                dve.wait_ge(act_tanh_made.sem, act_tanh_made.upto(t.n))
                v.scalar_tensor_tensor(act_g[:, t.par, :], act_t[:, t.par, :], 1.0,
                                       bank[2 + t.par][:, 0:I], ALU.add, ALU.mult
                                       ).then_inc(act_silu_made.sem, 1)
                dve.wait_ge(act_silu_made.sem, act_silu_made.upto(t.n))
                v.scalar_tensor_tensor(act_a[:, t.par, :], act_g[:, t.par, :], 0.5,
                                       bank[2 + t.par][:, I:2 * I], ALU.mult, ALU.mult
                                       ).then_inc(act_made.sem, 1)

            def copy_actT(t):
                dve.wait_ge(act_turned.sem, act_turned.upto(t.n))
                dve.wait_ge(y_made.sem, y_made.upto(t.n - 2))
                v.tensor_copy(act_aT[:, 0, t.par, :], bank[4][:, 0:I]).then_inc(aT_hi_made.sem, 1)
                dve.wait_ge(aT_hi_made.sem, aT_hi_made.upto(t.n))
                v.tensor_tensor(act_aT[:, 1, t.par, :], bank[4][:, 0:I], act_aT[:, 0, t.par, :], ALU.subtract
                                ).then_inc(actT_made.sem, 1)

            def rest_x(t):
                dve.wait_ge(xtT_made.sem, xtT_made.upto(t.n))
                v.tensor_tensor(xtT[:, 1, t.par, :], bank[t.par][:, :], xtT[:, 0, t.par, :], ALU.subtract
                                ).then_inc(xt_lo_made.sem, 1)

            def expert_step(t, ahead2=True, ahead1=True):
                copy_actT(t)
                if ahead2:
                    rest_x(t + 2)
                if ahead1:
                    silu(t + 1)

            rest_x(Item(0, 0))
            rest_x(Item(0, 1))
            silu(Item(0, 0))
            expert_step(Item(0, 0))
            expert_step(Item(0, 1))
            then(v.tensor_scalar(shift[:, :], tile_first[:, :], float(P), None, ALU.mult))
            then(v.tensor_tensor(shift[:, :], shift[:, :], expert_row[:, :], ALU.subtract))
            hot = all_hot[:, :, :, :].rearrange("p b n e -> p (b n) e")
            then(v.tensor_tensor(hot_shift, hot, shift[:, :].unsqueeze(1).to_broadcast([P, B * ST * TOPK, E]),
                                 ALU.mult))
            then(v.tensor_reduce(y_slot_f[:, :], hot_shift, AX_X, ALU.add))
            then(v.tensor_tensor(y_slot_f[:, :], y_slot_f[:, :],
                                 all_slot[:, :, :].rearrange("p b n -> p (b n)"), ALU.add))
            then(v.tensor_copy(y_slot[:, :], y_slot_f[:, :]))
            with dve.Fori(0, (TILES - 4) // 2) as i:
                expert_step(Item(i, 2))
                expert_step(Item(i, 3))
            expert_step(Item(0, TILES - 2), ahead2=False)
            expert_step(Item(0, TILES - 1), ahead2=False, ahead1=False)

            def place_rows(n, k):
                v.tensor_copy(y_at[:, k, :], y_slot[:, bass.ds(n * TOPK, TOPK)]).then_inc(y_at_made.sem, 1)

            weights = all_w[:, :, :].rearrange("p b n -> p (b n)")

            def combine(lap, k, more=True):
                n = lap * 4 + k
                dve.wait_ge(y_got[k].sem, y_got[k].upto(lap))
                v.scalar_tensor_tensor(y_in[k][:, 0, :], y_in[k][:, 0, :], weights[:, bass.ds(n * TOPK, 1)],
                                       base_out[:, bass.ds(n, 1), :].rearrange("p a d -> p (a d)"),
                                       ALU.mult, ALU.add).then_inc(fin_step.sem, 1)
                dve.wait_ge(fin_step.sem, fin_step.upto(n))
                dve.wait_ge(out_stored[k].sem, out_stored[k].upto(lap - 1))
                v.scalar_tensor_tensor(fin[k], y_in[k][:, 1, :], weights[:, bass.ds(n * TOPK + 1, 1)],
                                       y_in[k][:, 0, :], ALU.mult, ALU.add).then_inc(fin_made.sem, 1)
                if more:
                    place_rows(n + 4, k)

            dve.wait_ge(table_step.sem, table_step.upto(steps[0] - 1))
            for k in range(4):
                place_rows(k, k)
            for k in range(4):
                combine(0, k)
            with dve.Fori(1, NT // 4 - 1) as i:
                for k in range(4):
                    combine(i, k)
            for k in range(4):
                combine(NT // 4 - 1, k, more=False)


FIRST_CONSTS = 5
POOL_CONSTS = 23
TABLE_STEPS = 17


_INS = ['x', 'ctx_1024', 'g_xattn', 'g_ffn', 'L0_xattn_igate_w', 'L0_xattn_igate_b', 'L0_xattn_fgate_w',
        'L0_xattn_fgate_b', 'L0_xattn_ln_scale', 'L0_ffn_router_w', 'L0_ffn_expert_gate', 'L0_ffn_expert_up',
        'L0_ffn_expert_down', 'L0_ffn_shared_gate', 'L0_ffn_shared_up', 'L0_ffn_shared_down']
_OUTS = [((B, S, D), 'float32')]


def kernel(**inputs):
    import numpy as _np
    import concourse.bacc as _bacc
    from concourse import mybir as _mybir
    from concourse.bass_utils import run_bass_kernel_spmd as _run

    nc = _bacc.Bacc("TRN2", target_bir_lowering=False, num_devices=1)
    arrays, args = {}, []
    for name in _INS:
        a = _np.ascontiguousarray(inputs[name])
        arrays[f"in_{name}_dram"] = a
        args.append(nc.dram_tensor(f"in_{name}_dram", a.shape, _mybir.dt.from_np(a.dtype), kind="ExternalInput").ap())
    for i, (shape, dtype) in enumerate(_OUTS):
        dt = _mybir.dt.from_np(_np.dtype(dtype))
        args.append(nc.dram_tensor(f"out_{i}_dram", shape, dt, kind="ExternalOutput").ap())
    flamingo_kernel(nc, *args)
    r = _run(nc, [arrays], core_ids=[0])
    got = tuple(r.results[0][f"out_{i}_dram"] for i in range(len(_OUTS)))
    return got[0]
```
